# Optimizing a Trainium2 kernel written in Bass

```python
import numpy as np
import jax
import jax.numpy as jnp

def _softmax(x, axis=-1):
    return jax.nn.softmax(x, axis=axis)

def _gelu(x):
    return jax.nn.gelu(x, approximate=True)

def _silu(x):
    return jax.nn.silu(x)

def _sigmoid(x):
    return jax.nn.sigmoid(x)

def _layernorm(x, axis=-1, eps=1e-05):
    m = jnp.mean(x, axis=axis, keepdims=True)
    v = jnp.var(x, axis=axis, keepdims=True)
    return (x - m) / jnp.sqrt(v + eps)

def _scatter_add(tgt, idx, src, axis=0):
    return tgt.at[idx].add(src)

def _segment_sum(src, seg, n):
    return jax.ops.segment_sum(src, seg, n)
kernel_name = 'mk_seq_postln_d2_jaxref_r8_89965d'

def setup_inputs(seed: int=0):
    np.random.seed(seed)
    _w = jnp.asarray

    def _L0_attn_setup():
        import jax, jax.numpy as jnp
        import numpy as np
        NUM_HEADS = 16
        EPS = 1e-05
        CHUNK = 128

        def _linear_attention(x, Wq, Wk, Wv, Wo, bo):
            B, T, E = x.shape
            H = NUM_HEADS
            d = E // H

            def proj(W):
                return (x @ W.T).reshape(B, T, H, d).transpose(0, 2, 1, 3)
            phi_q = jax.nn.elu(proj(Wq)) + 1.0
            phi_k = jax.nn.elu(proj(Wk)) + 1.0
            V = proj(Wv)
            nC = T // CHUNK

            def to_chunks(a):
                return a.reshape(B, H, nC, CHUNK, d).transpose(2, 0, 1, 3, 4)
            qc, kc, vc = (to_chunks(phi_q), to_chunks(phi_k), to_chunks(V))
            mask = jnp.tril(jnp.ones((CHUNK, CHUNK), x.dtype))
            S0 = jnp.zeros((B, H, d, d), x.dtype)
            z0 = jnp.zeros((B, H, d), x.dtype)

            def step(carry, inp):
                S, z = carry
                q, k, v = inp
                A = jnp.einsum('bhid,bhjd->bhij', q, k) * mask
                num = jnp.einsum('bhij,bhjd->bhid', A, v) + jnp.einsum('bhid,bhde->bhie', q, S)
                den = jnp.sum(A, axis=-1) + jnp.einsum('bhid,bhd->bhi', q, z) + EPS
                out = num / den[..., None]
                S = S + jnp.einsum('bhjd,bhje->bhde', k, v)
                z = z + jnp.sum(k, axis=2)
                return ((S, z), out)
            _, outs = jax.lax.scan(step, (S0, z0), (qc, kc, vc))
            out = outs.transpose(1, 2, 0, 3, 4).reshape(B, H, T, d)
            out = out.transpose(0, 2, 1, 3).reshape(B, T, E)
            return out @ Wo.T + bo
        key = jax.random.key(seed)
        ks = jax.random.split(key, 6)
        B, T, E = (2, 256, 128)
        s = 1.0 / np.sqrt(E)
        return {'x': jax.random.normal(ks[0], (B, T, E), jnp.float32), 'Wq': jax.random.normal(ks[1], (E, E), jnp.float32) * s, 'Wk': jax.random.normal(ks[2], (E, E), jnp.float32) * s, 'Wv': jax.random.normal(ks[3], (E, E), jnp.float32) * s, 'Wo': jax.random.normal(ks[4], (E, E), jnp.float32) * s, 'bo': jnp.zeros((E,), jnp.float32)}
    _L0_attn_in = _L0_attn_setup()

    def _L0_ffn_setup():
        import jax, jax.numpy as jnp
        import numpy as np
        EPS = 1e-05
        key = jax.random.key(seed)
        kx, kw, kb = jax.random.split(key, 3)
        B, S, K, N = (8, 1024, 128, 128)
        x = jax.random.normal(kx, (B, S, K), dtype=jnp.float32)
        W = jax.random.normal(kw, (N, K), dtype=jnp.float32) * 0.02
        weight_scale = jnp.maximum(jnp.max(jnp.abs(W), axis=1, keepdims=True) / 127.0, EPS)
        weight_int8 = jnp.clip(jnp.round(W / weight_scale), -128, 127).astype(jnp.int8)
        bias = jax.random.normal(kb, (N,), dtype=jnp.float32) * 0.01
        return {'x': x, 'weight_int8': weight_int8, 'weight_scale': weight_scale, 'bias': bias}
    _L0_ffn_in = _L0_ffn_setup()

    def _L1_attn_setup():
        import jax, jax.numpy as jnp
        import numpy as np
        LN_EPS = 1e-05

        def _layer_norm(c, ln_w, ln_b):
            mu = jnp.mean(c, axis=-1, keepdims=True)
            var = jnp.mean(jnp.square(c - mu), axis=-1, keepdims=True)
            return (c - mu) * jax.lax.rsqrt(var + LN_EPS) * ln_w + ln_b
        key = jax.random.key(seed)
        k_x, k_w, k_b, k_g, k_beta = jax.random.split(key, 5)
        B, S, D, H = (8, 256, 128, 128)
        x = jax.random.normal(k_x, (B, S, D), dtype=jnp.float32)
        W = jax.random.normal(k_w, (4 * H, D), dtype=jnp.float32) * (1.0 / np.sqrt(D))
        b = jax.random.normal(k_b, (4 * H,), dtype=jnp.float32) * 0.01
        ln_w = jnp.ones((H,), dtype=jnp.float32) + 0.01 * jax.random.normal(k_g, (H,), dtype=jnp.float32)
        ln_b = 0.01 * jax.random.normal(k_beta, (H,), dtype=jnp.float32)
        return {'x': x, 'W': W, 'b': b, 'ln_w': ln_w, 'ln_b': ln_b}
    _L1_attn_in = _L1_attn_setup()

    def _L1_ffn_setup():
        import jax, jax.numpy as jnp
        import numpy as np
        B, T, C = (4, 256, 128)
        E = 8
        K = 2
        H = 176
        HS = 176 * 2
        key = jax.random.key(seed)
        k = jax.random.split(key, 8)
        s = 0.02
        return {'x': jax.random.normal(k[0], (B, T, C), jnp.float32), 'Wg': jax.random.normal(k[1], (C, E), jnp.float32) * s, 'W1': jax.random.normal(k[2], (E, C, H), jnp.float32) * s, 'W2': jax.random.normal(k[3], (E, C, H), jnp.float32) * s, 'W3': jax.random.normal(k[4], (E, H, C), jnp.float32) * s, 'Ws1': jax.random.normal(k[5], (C, HS), jnp.float32) * s, 'Ws2': jax.random.normal(k[6], (C, HS), jnp.float32) * s, 'Ws3': jax.random.normal(k[7], (HS, C), jnp.float32) * s}
    _L1_ffn_in = _L1_ffn_setup()
    _d = {'L0_attn_x': _L0_attn_in['x'], 'L0_attn_Wq': _L0_attn_in['Wq'], 'L0_attn_Wk': _L0_attn_in['Wk'], 'L0_attn_Wv': _L0_attn_in['Wv'], 'L0_attn_Wo': _L0_attn_in['Wo'], 'L0_attn_bo': _L0_attn_in['bo'], 'L0_ffn_weight_int8': _L0_ffn_in['weight_int8'], 'L0_ffn_weight_scale': _L0_ffn_in['weight_scale'], 'L0_ffn_bias': _L0_ffn_in['bias'], 'L1_attn_W': _L1_attn_in['W'], 'L1_attn_b': _L1_attn_in['b'], 'L1_attn_ln_w': _L1_attn_in['ln_w'], 'L1_attn_ln_b': _L1_attn_in['ln_b'], 'L1_ffn_Wg': _L1_ffn_in['Wg'], 'L1_ffn_W1': _L1_ffn_in['W1'], 'L1_ffn_W2': _L1_ffn_in['W2'], 'L1_ffn_W3': _L1_ffn_in['W3'], 'L1_ffn_Ws1': _L1_ffn_in['Ws1'], 'L1_ffn_Ws2': _L1_ffn_in['Ws2'], 'L1_ffn_Ws3': _L1_ffn_in['Ws3']}
    _x0 = _d['L0_attn_x']
    _d['L0_attn_x'] = jax.random.normal(jax.random.fold_in(jax.random.key(seed), 1), (2, 2048, 128), dtype=_x0.dtype)
    del _x0
    return _d

def reference(L0_attn_x, L0_attn_Wq, L0_attn_Wk, L0_attn_Wv, L0_attn_Wo, L0_attn_bo, L0_ffn_weight_int8, L0_ffn_weight_scale, L0_ffn_bias, L1_attn_W, L1_attn_b, L1_attn_ln_w, L1_attn_ln_b, L1_ffn_Wg, L1_ffn_W1, L1_ffn_W2, L1_ffn_W3, L1_ffn_Ws1, L1_ffn_Ws2, L1_ffn_Ws3):

    def _L0_attn_ref(x, Wq, Wk, Wv, Wo, bo):
        import jax, jax.numpy as jnp
        import numpy as np
        NUM_HEADS = 16
        EPS = 1e-05
        CHUNK = 128

        def _linear_attention(x, Wq, Wk, Wv, Wo, bo):
            B, T, E = x.shape
            H = NUM_HEADS
            d = E // H

            def proj(W):
                return (x @ W.T).reshape(B, T, H, d).transpose(0, 2, 1, 3)
            phi_q = jax.nn.elu(proj(Wq)) + 1.0
            phi_k = jax.nn.elu(proj(Wk)) + 1.0
            V = proj(Wv)
            nC = T // CHUNK

            def to_chunks(a):
                return a.reshape(B, H, nC, CHUNK, d).transpose(2, 0, 1, 3, 4)
            qc, kc, vc = (to_chunks(phi_q), to_chunks(phi_k), to_chunks(V))
            mask = jnp.tril(jnp.ones((CHUNK, CHUNK), x.dtype))
            S0 = jnp.zeros((B, H, d, d), x.dtype)
            z0 = jnp.zeros((B, H, d), x.dtype)

            def step(carry, inp):
                S, z = carry
                q, k, v = inp
                A = jnp.einsum('bhid,bhjd->bhij', q, k) * mask
                num = jnp.einsum('bhij,bhjd->bhid', A, v) + jnp.einsum('bhid,bhde->bhie', q, S)
                den = jnp.sum(A, axis=-1) + jnp.einsum('bhid,bhd->bhi', q, z) + EPS
                out = num / den[..., None]
                S = S + jnp.einsum('bhjd,bhje->bhde', k, v)
                z = z + jnp.sum(k, axis=2)
                return ((S, z), out)
            _, outs = jax.lax.scan(step, (S0, z0), (qc, kc, vc))
            out = outs.transpose(1, 2, 0, 3, 4).reshape(B, H, T, d)
            out = out.transpose(0, 2, 1, 3).reshape(B, T, E)
            return out @ Wo.T + bo
        return _linear_attention(x, Wq, Wk, Wv, Wo, bo)

    def _L0_ffn_ref(x, weight_int8, weight_scale, bias):
        import jax, jax.numpy as jnp
        import numpy as np
        EPS = 1e-05
        B, S, K = x.shape
        x2 = x.reshape(-1, K)
        x_scale = jnp.maximum(jnp.abs(x2).max() / 127.0, EPS)
        x_int8 = jnp.clip(jnp.round(x2 / x_scale), -128, 127).astype(jnp.int8)
        acc_i32 = jax.lax.dot_general(x_int8, weight_int8.T, dimension_numbers=(((1,), (0,)), ((), ())), preferred_element_type=jnp.int32)
        out = acc_i32.astype(jnp.float32) * x_scale * weight_scale.T
        out = out + bias
        return out.reshape(B, S, -1)

    def _L1_attn_ref(x, W, b, ln_w, ln_b):
        import jax, jax.numpy as jnp
        import numpy as np
        LN_EPS = 1e-05

        def _layer_norm(c, ln_w, ln_b):
            mu = jnp.mean(c, axis=-1, keepdims=True)
            var = jnp.mean(jnp.square(c - mu), axis=-1, keepdims=True)
            return (c - mu) * jax.lax.rsqrt(var + LN_EPS) * ln_w + ln_b
        B, S, D = x.shape
        H = W.shape[0] // 4
        gates = jnp.einsum('bsd,gd->bsg', x, W) + b
        f, i, o, z_raw = jnp.split(gates, 4, axis=-1)
        f = jax.nn.sigmoid(f)
        i = jax.nn.sigmoid(i)
        o = jax.nn.sigmoid(o)
        z = jnp.tanh(z_raw)

        def step(c, fioz_t):
            f_t, i_t, o_t, z_t = fioz_t
            c = f_t * c + i_t * z_t
            h = o_t * jnp.tanh(_layer_norm(c, ln_w, ln_b))
            return (c, h)
        c0 = jnp.zeros((B, H), dtype=x.dtype)
        fs = jnp.swapaxes(f, 0, 1)
        is_ = jnp.swapaxes(i, 0, 1)
        os_ = jnp.swapaxes(o, 0, 1)
        zs = jnp.swapaxes(z, 0, 1)
        _, h_seq = jax.lax.scan(step, c0, (fs, is_, os_, zs))
        return jnp.swapaxes(h_seq, 0, 1)

    def _L1_ffn_ref(x, Wg, W1, W2, W3, Ws1, Ws2, Ws3):
        import jax, jax.numpy as jnp
        import numpy as np
        B, T, C = (4, 256, 128)
        E = 8
        K = 2
        H = 176
        HS = 176 * 2
        b, t, c = x.shape
        xf = x.reshape(-1, c)
        n = xf.shape[0]
        router = xf @ Wg
        top_logits, idx = jax.lax.top_k(router, K)
        probs = jax.nn.softmax(top_logits.astype(jnp.float32), axis=-1).astype(x.dtype)
        w = jnp.zeros((n, E), x.dtype).at[jnp.arange(n)[:, None], idx].add(probs)
        h = jax.nn.silu(jnp.einsum('tc,ech->eth', xf, W1)) * jnp.einsum('tc,ech->eth', xf, W2)
        y = jnp.einsum('eth,ehc,te->tc', h, W3, w)
        y = y.reshape(b, t, c)
        hs = jax.nn.silu(xf @ Ws1) * (xf @ Ws2)
        y = y + (hs @ Ws3).reshape(b, t, c)
        return y
    x = L0_attn_x
    x = _layernorm(x + _L0_attn_ref(x, L0_attn_Wq, L0_attn_Wk, L0_attn_Wv, L0_attn_Wo, L0_attn_bo), axis=-1)
    x = _layernorm(x + _L0_ffn_ref(x, L0_ffn_weight_int8, L0_ffn_weight_scale, L0_ffn_bias), axis=-1)
    x = _layernorm(x + _L1_attn_ref(x, L1_attn_W, L1_attn_b, L1_attn_ln_w, L1_attn_ln_b), axis=-1)
    x = _layernorm(x + _L1_ffn_ref(x, L1_ffn_Wg, L1_ffn_W1, L1_ffn_W2, L1_ffn_W3, L1_ffn_Ws1, L1_ffn_Ws2, L1_ffn_Ws3), axis=-1)
    return x

_drawn_inputs = setup_inputs


def setup_inputs(seed=0):
    import zlib

    import numpy as np

    out = dict(_drawn_inputs(seed))
    spreads = {'L0_attn_bo': (0.0, 0.1)}
    factors = {'L0_attn_Wq': 3.361,
     'L0_ffn_bias': 5.49,
     'L1_attn_b': 8.0,
     'L1_attn_ln_w': 8.0,
     'L1_attn_ln_b': 8.0,
     'L1_ffn_Wg': 8.0,
     'L1_ffn_W1': 8.0,
     'L1_ffn_W2': 8.0,
     'L1_ffn_W3': 8.0,
     'L1_ffn_Ws1': 5.897,
     'L1_ffn_Ws2': 5.875,
     'L1_ffn_Ws3': 5.911}
    for name, (base, spread) in spreads.items():
        noise = np.random.default_rng([zlib.crc32(name.encode()), seed]).standard_normal(out[name].shape)
        drawn = base * np.exp(spread * noise) if base else spread * noise
        out[name] = jnp.asarray(drawn.astype(out[name].dtype))
    for name, factor in factors.items():
        out[name] = (out[name] * factor).astype(out[name].dtype)
    return out
```

```python
import concourse.bass as bass
from concourse import mybir
from contextlib import ExitStack

F32 = mybir.dt.float32
F32R = mybir.dt.float32r
BF16 = mybir.dt.bfloat16
I32 = mybir.dt.int32
ALU = mybir.AluOpType
ACT = mybir.ActivationFunctionType
AX = mybir.AxisListType

P = 128
CHUNK = 128
SUB = 4
TILE = SUB * CHUNK
LN_EPS = 1e-5
DEN_EPS = 1e-5
SCALE_EPS = 1e-5
MAGIC = 1.5 * 2.0 ** 23


def build_program(nc, x_in, Wq, Wk, Wv, Wo, bo, W8, w8_scale, ffn_bias, Wgates, gate_bias,
                  ln_w, ln_b, Wrouter, W1, W2, W3, Ws1, Ws2, Ws3, out):
    B, T_LEN, E = x_in.shape
    HEADS = 16
    D = E // HEADS
    QUADS = 4
    DV = D + 1
    NT = B * T_LEN // TILE
    NC = NT * SUB
    PAIRS = NT // 2
    TPB = T_LEN // TILE
    EXPERTS = Wrouter.shape[1]
    HID = W1.shape[2]
    HSH = Ws1.shape[1]
    ROUTED = EXPERTS * HID
    HALL = ROUTED + HSH
    NJ = -(-HALL // P)
    NJR = ROUTED // P
    LASTK = HALL - (NJ - 1) * P
    ROUTE = 21
    AHEAD = 3
    W_COLS = 2 * HALL + NJ * P
    WSLICE = W_COLS // NT
    assert ROUTED % P == 0 and W_COLS % NT == 0 and E == P and TPB % 2 == 0

    x_tiles = x_in.rearrange("b (n s p) e -> (b n) p s e", p=P, s=SUB)
    out_tiles = out.rearrange("b (n s p) e -> (b n) p s e", p=P, s=SUB)

    with ExitStack() as ctx:
        def sb(name, shape, dt=F32):
            return ctx.enter_context(nc.sbuf_tensor(name, shape, dt))

        def bank(name, shape, dt=F32):
            return ctx.enter_context(nc.psum_tensor(name, shape, dt))

        def sem(name):
            return ctx.enter_context(nc.semaphore(name))

        ident = sb("ident", [P, P])
        causal = sb("causal", [P, CHUNK])
        head_of = sb("head_of", [P, QUADS, 4])
        head_of_2 = sb("head_of_2", [P, QUADS, 4])
        in_quad = sb("in_quad", [P, 4])
        keep = sb("keep", [P, PAIRS])
        carry = sb("carry", [P, 1])
        ones_row = sb("ones_row", [1, P])
        minus_half = sb("minus_half", [P, SUB])
        rev_index = sb("rev_index", [P, SUB, EXPERTS])
        sel16 = sb("sel16", [16, ROUTED])
        sel16_b = sb("sel16_b", [16, ROUTED])
        sel16_r = sb("sel16_r", [16, ROUTED], F32R)
        w_nat = sb("w_nat", [P, 9, P])
        w8_raw = sb("w8_raw", [P, P, 2], I32)
        wT = sb("wT", [P, 8, P])
        w8T = sb("w8T", [P, P], BF16)
        rows = sb("rows", [1, 6, P])
        rows_bc = sb("rows_bc", [P, 5, P])
        o_bias4 = sb("o_bias4", [1, SUB, P])
        gate_b = sb("gate_b", [P, 3])
        gate_bh = sb("gate_bh", [P, 2])
        w_router = sb("w_router", [P, EXPERTS])
        w_router_hi = sb("w_router_hi", [P, EXPERTS], F32R)
        w_router_lo = sb("w_router_lo", [P, EXPERTS], F32R)
        w_ff = sb("w_ff", [P, W_COLS])
        w_hi = sb("w_hi", [P, W_COLS], F32R)
        w_lo = sb("w_lo", [P, W_COLS], F32R)
        amax = sb("amax", [P, NT])
        amax1 = sb("amax1", [P, 1])
        amax_all = sb("amax_all", [P, 1])
        x_scale = sb("x_scale", [P, 1])
        inv_scale = sb("inv_scale", [P, 1])
        deq_scale = sb("deq_scale", [P, P])
        x1_all = sb("x1_all", [P, NC, E])

        first = ctx.enter_context(ExitStack())

        def sb1(name, shape, dt=F32):
            return first.enter_context(nc.sbuf_tensor(name, shape, dt))

        x_cur = [sb1(f"x_cur{p}", [P, SUB, E]) for p in range(2)]
        x_bo = [sb1(f"x_bo{p}", [P, SUB, E]) for p in range(2)]
        xT = sb1("xT", [P, TILE])
        exp_q = sb1("exp_q", [P, TILE])
        exp_k = sb1("exp_k", [P, TILE])
        qT = [sb1(f"qT{p}", [P, TILE]) for p in range(2)]
        kT = [sb1(f"kT{p}", [P, TILE]) for p in range(2)]
        q_heads = [sb1(f"q_heads{p}", [P, 4, TILE]) for p in range(2)]
        k_tok = [sb1(f"k_tok{p}", [P, SUB, P]) for p in range(2)]
        v_tok = [sb1(f"v_tok{p}", [P, SUB, HEADS, DV]) for p in range(2)]
        scores = sb1("scores", [P, QUADS, 4 * CHUNK])
        state = sb1("state", [P, 2, HEADS * DV])
        kv_own = sb1("kv_own", [P, HEADS * DV])
        den = sb1("den", [P, HEADS])
        rden = sb1("rden", [P, HEADS])
        attn = sb1("attn", [P, HEADS, D])
        attnT = sb1("attnT", [P, P])
        y_attn = sb1("y_attn", [P, SUB, E])
        a_stats = sb1("a_stats", [P, SUB, 6])
        a_mv = sb1("a_mv", [P, SUB, 2])
        a_var = sb1("a_var", [P, SUB])
        a_rstd = sb1("a_rstd", [P, SUB])

        first.close()

        xq = sb("xq", [P, SUB, E])
        x1_b = sb("x1_b", [P, SUB, E])
        xqT = sb("xqT", [P, TILE], BF16)
        y_ffn = sb("y_ffn", [P, SUB, E])
        stats = [sb(f"stats{n}", [P, SUB, 6]) for n in range(4)]
        mv = [sb(f"mv{n}", [P, SUB, 2]) for n in range(4)]
        var_eps = [sb(f"var_eps{n}", [P, SUB]) for n in range(4)]
        rstd = [sb(f"rstd{n}", [P, SUB]) for n in range(4)]
        x2 = sb("x2", [P, SUB, E])
        x2T = sb("x2T", [P, TILE])
        tanh_f = sb("tanh_f", [P, TILE])
        tanh_i = sb("tanh_i", [P, TILE])
        tanh_z = sb("tanh_z", [P, TILE])
        tanh_o = sb("tanh_o", [P, SUB, E])
        f_gate = sb("f_gate", [P, TILE])
        iz2 = sb("iz2", [P, TILE])
        cell2 = sb("cell2", [P, TILE])
        c_norm = sb("c_norm", [P, SUB, E])
        c_aff = sb("c_aff", [P, SUB, E])
        tanh_c = sb("tanh_c", [P, SUB, E])
        h2 = sb("h2", [P, SUB, E])
        y_lstm = sb("y_lstm", [P, SUB, E])

        x3 = [sb(f"x3_{p}", [P, SUB, E]) for p in range(2)]
        x3T_hi = [sb(f"x3T_hi{p}", [P, TILE], F32R) for p in range(2)]
        x3T_lo = [sb(f"x3T_lo{p}", [P, TILE], F32R) for p in range(2)]
        logits = sb("logits", [P, SUB, EXPERTS])
        logits2 = sb("logits2", [P, SUB, EXPERTS])
        top = [sb(f"top{n}", [P, SUB]) for n in range(2)]
        is_top = [sb(f"is_top{n}", [P, SUB, EXPERTS]) for n in range(2)]
        rank = [sb(f"rank{n}", [P, SUB, EXPERTS]) for n in range(2)]
        best = [sb(f"best{n}", [P, SUB]) for n in range(2)]
        pick = [sb(f"pick{n}", [P, SUB, EXPERTS]) for n in range(2)]
        gap = sb("gap", [P, SUB])
        tanh_gap = sb("tanh_gap", [P, SUB])
        pick_sum = sb("pick_sum", [P, SUB, EXPERTS])
        pick_dif = sb("pick_dif", [P, SUB, EXPERTS])
        dif_t = sb("dif_t", [P, SUB, EXPERTS])
        w2x = sb("w2x", [P, SUB, EXPERTS])
        w_tok = sb("w_tok", [P, SUB, EXPERTS])
        w_tok_r = sb("w_tok_r", [P, SUB, EXPERTS], F32R)
        w_parts = sb("w_parts", [P, SUB, 2, EXPERTS])
        w_partsT = [sb(f"w_partsT{p}", [16, TILE], F32R) for p in range(2)]
        silu_g = [sb(f"silu_g{n}", [P, TILE]) for n in range(2)]
        gu = [sb(f"gu{n}", [P, TILE]) for n in range(2)]
        hid = [sb(f"hid{n}", [P, TILE]) for n in range(2)]
        hid_hi = [sb(f"hid_hi{n}", [P, TILE], F32R) for n in range(4)]
        hid_lo = [sb(f"hid_lo{n}", [P, TILE], F32R) for n in range(4)]
        yT = sb("yT", [P, TILE])
        y_moe = sb("y_moe", [P, SUB, E])
        x4 = sb("x4", [P, SUB, E])

        pb = [bank(f"bank{n}", [P, 512]) for n in range(8)]
        ps_scores = pb[0:4]
        ps_tr = pb[4]
        ps_proj = pb[5]
        ps_num = pb[6][:, 0:HEADS * DV]
        ps_kv = pb[6][:, 256:256 + HEADS * DV]
        ps_attnT = pb[7][:, 0:P]
        ps_wo = pb[7][:, 256:256 + P]
        ps_g = pb[0:2]
        ps_u = pb[2:4]
        ps_w = pb[4]
        ps_y = pb[5]
        ps_a = pb[6]
        ps_b = pb[7]

        s = {n: sem(n) for n in (
            "wl_square wl_int8 wl_rows wl_cols wl_router wl_ff x_loaded out_stored "
            "z_set consts_ready one_set v_ones state_zero ff_pad_zero "
            "w_tr w_tr_copied w8_cast w8T_ready rows_bc_ps rows_bc_ready o_bias_ready gate_bh_ready "
            "quad_ready router_hi router_ready sel_r_ready ff_hi ff_split "
            "xT_ps xT_ready q_ps expq_ready expq_min q_ready k_ps expk_ready expk_min k_ready v_ps v_ready "
            "ktok_ps ktok_ready qheads_v qheads_p xbo_ready "
            "score_ps masked kv_ps kv_own_ready state_ready state_kept attn_num_ps den_ready rden_ready attn_ready "
            "attnT_ps attnT_ready wo_ps yattn_ready astats_ready amv_ready avar_ready arstd_ready x1_ready amax_ready "
            "amax1_ready amax_all_ready scale_a scale_b scale_ready deq_ready "
            "xq_round xq_ready x1b_ready xqT_ps xqT_ready q8_ps deq_done yffn_ready stats_ready mv_ready vareps_ready "
            "rstd_ready x2_ready x2T_ps x2T_ready f_ps tf_ready i_ps ti_ready z_ps tz_ready o_ps to_ready "
            "f_ready iz_ready cell_ready carry_ready cellT_ps cnorm_ready cscaled caff_ready tc_ready h2_ready "
            "ylstm_ready x3_ready x3T_ps x3hi_ready x3lo_ready logit_ps logit_copied route_a route_b gap_ready tgap_ready "
            "route_c w_ready wr_ready wparts_ready wT_ps wT_ready "
            "g_ps u_ps w_ps silu_ready gu_ready hid_ready hi_ready lo_ready down_ps "
            "yT_ready y_ps ymoe_ready x4_ready route_step").split()}
        norms = ("ffn", "cell", "lstm", "moe")
        st_r = [sem(f"{n}_stats_ready") for n in norms]
        mv_r = [sem(f"{n}_meanvar_ready") for n in norms]
        ve_r = [sem(f"{n}_vareps_ready") for n in norms]
        rs_r = [sem(f"{n}_rstd_ready") for n in norms]
        nm_r = [sem(f"{n}_normed") for n in norms[:3]] + [s["x4_ready"]]

        block = ctx.enter_context(nc.Block())

        def settled(eng):
            eng.nop(nofuse=True)


        @block.sync
        def _(sp):
            def load_x(t, p, first=False):
                if not first:
                    sp.wait_ge(s["x_loaded"], 16 * t)
                    settled(sp)
                    sp.wait_ge(s["xT_ps"], t - 1)
                    settled(sp)
                    sp.wait_ge(s["xbo_ready"], t - 1)
                    settled(sp)
                sp.dma_start(x_cur[p][:], x_tiles[bass.ds(t, 1)].rearrange("o p s e -> (o p) s e")
                             if not isinstance(t, int) else x_tiles[t]).then_inc(s["x_loaded"], 16)

            load_x(0, 0, first=True)
            for n, w in enumerate((Wq, Wk, Wv, Wo)):
                sp.dma_start(w_nat[:, n, :], w).then_inc(s["wl_square"], 16)
            sp.wait_ge(s["x_loaded"], 16)
            load_x(1, 1, first=True)
            sp.dma_start(w_nat[:, 4:8, :], Wgates.rearrange("(g p) d -> p g d", p=P)).then_inc(s["wl_square"], 16)
            sp.dma_start(w8_raw[:].rearrange("p k w -> p (k w)"), W8.bitcast(I32)).then_inc(s["wl_int8"], 16)
            sp.dma_start(w_router[:], Wrouter).then_inc(s["wl_router"], 16)
            with sp.Fori(1, PAIRS) as i:
                load_x(2 * i, 0)
                load_x(2 * i + 1, 1)

            def store(t):
                sp.wait_ge(s["x4_ready"], SUB * (t + 1))
                settled(sp)
                sp.dma_start(out_tiles[bass.ds(t, 1)].rearrange("o p s e -> (o p) s e"), x4[:])\
                  .then_inc(s["out_stored"], 16)

            with sp.Fori(0, NT) as t:
                store(t)
            sp.wait_ge(s["out_stored"], 16 * NT)

        @block.scalar
        def _(act):
            for n, r in enumerate((bo, ffn_bias, None, ln_w, ln_b, gate_bias[2 * P:3 * P])):
                src = w8_scale.rearrange("n o -> o n") if r is None else r.rearrange("(o n) -> o n", o=1)
                act.dma_start(rows[:, n, :], src).then_inc(s["wl_rows"], 16)
            gb = gate_bias.rearrange("(g p o) -> g p o", p=P, o=1)
            for n, g in enumerate((0, 1, 3)):
                act.dma_start(gate_b[:, n:n + 1], gb[g]).then_inc(s["wl_cols"], 16)
            col = 0
            for routed, shared in ((W1, Ws1), (W2, Ws2)):
                act.dma_start(w_ff[:, col:col + ROUTED].rearrange("c (e h) -> c e h", e=EXPERTS),
                              routed.rearrange("e c h -> c e h")).then_inc(s["wl_ff"], 16)
                act.dma_start(w_ff[:, col + ROUTED:col + HALL], shared).then_inc(s["wl_ff"], 16)
                col += HALL
            act.dma_start(w_ff[:, col:col + NJR * P].rearrange("p (j c) -> p j c", j=NJR),
                          W3.rearrange("e h c -> (e h) c").rearrange("(j p) c -> p j c", p=P)).then_inc(s["wl_ff"], 16)
            act.dma_start(w_ff[:, col + NJR * P:col + (NJ - 1) * P].rearrange("p (j c) -> p j c", j=NJ - 1 - NJR),
                          Ws3[0:(NJ - 1 - NJR) * P, :].rearrange("(j p) c -> p j c", p=P)).then_inc(s["wl_ff"], 16)
            act.wait_ge(s["ff_pad_zero"], 1)
            act.dma_start(w_ff[0:LASTK, col + (NJ - 1) * P:col + NJ * P],
                          Ws3[(NJ - 1 - NJR) * P:HSH, :]).then_inc(s["wl_ff"], 16)

            for b in range(2):
                act.wait_ge(s["w_tr"], b + 1)
                nc.scalar.activation(wT[:, 4 * b:4 * b + 4, :], ps_scores[b][:].rearrange("p (n c) -> p n c", n=4),
                                     ACT.Copy).then_inc(s["w_tr_copied"], 1)
            act.wait_ge(s["w_tr"], 3)
            nc.scalar.activation(w8T[:], ps_scores[2][:, 0:P], ACT.Copy).then_inc(s["w8T_ready"], 1)
            for b, (lo, hi) in enumerate(((0, 4), (4, 5))):
                act.wait_ge(s["rows_bc_ps"], b + 1)
                nc.scalar.activation(rows_bc[:, lo:hi, :],
                                     (ps_scores[3], ps_tr)[b][:, 0:(hi - lo) * P].rearrange("p (n c) -> p n c", c=P),
                                     ACT.Copy).then_inc(s["rows_bc_ready"], 1)

            def front(t, p, part):
                if part == 0:
                    act.wait_ge(s["xT_ps"], t + 1)
                    act.wait_ge(s["v_ps"], t)
                    nc.scalar.activation(xT[:], ps_tr[:], ACT.Copy).then_inc(s["xT_ready"], 1)
                    act.wait_ge(s["q_ps"], t + 1)
                    act.wait_ge(s["q_ready"], t)
                    nc.scalar.activation(exp_q[:], ps_proj[:], ACT.Exp).then_inc(s["expq_ready"], 1)
                elif part == 1:
                    act.wait_ge(s["k_ps"], t + 1)
                    act.wait_ge(s["k_ready"], t)
                    nc.scalar.activation(exp_k[:], ps_proj[:], ACT.Exp).then_inc(s["expk_ready"], 1)
                elif part == 2:
                    act.wait_ge(s["v_ps"], t + 1)
                    if not (isinstance(t, int) and t == 0):
                        act.wait_ge(s["attn_num_ps"], 4 * SUB * (t - 1))
                    act.wait_ge(s["v_ones"], 2)
                    nc.scalar.activation(v_tok[p][:].rearrange("p s h d -> p (s h) d")[:, :, 0:D],
                                         ps_proj[:].rearrange("p (n d) -> p n d", d=D), ACT.Copy)\
                      .then_inc(s["v_ready"], 1)
                else:
                    act.wait_ge(s["ktok_ps"], t + 1)
                    if not (isinstance(t, int) and t == 0):
                        act.wait_ge(s["kv_ps"], SUB * (t - 1))
                    nc.scalar.activation(k_tok[p][:].rearrange("p s d -> p (s d)"), ps_tr[:], ACT.Copy)\
                      .then_inc(s["ktok_ready"], 1)

            def chunk_out(c):
                act.wait_ge(s["attnT_ps"], c + 1)
                act.wait_ge(s["wo_ps"], c)
                nc.scalar.activation(attnT[:], ps_attnT, ACT.Copy).then_inc(s["attnT_ready"], 1)

            def tile(t, p, last):
                for c in range(SUB):
                    if not last and c < 3:
                        front(t + 1, 1 - p, c)
                    chunk_out(SUB * t + c)
                    if not last and c == 2:
                        front(t + 1, 1 - p, 3)

            for part in range(4):
                front(0, 0, part)
            with act.Fori(0, PAIRS - 1) as i:
                tile(2 * i, 0, False)
                tile(2 * i + 1, 1, False)
            tile(NT - 2, 0, False)
            tile(NT - 1, 1, True)

            def chain(t, p, slot):
                if slot == 1:
                    act.wait_ge(s["xqT_ps"], t + 1)
                    act.wait_ge(s["q8_ps"], t)
                    nc.scalar.activation(xqT[:], ps_a[:], ACT.Copy, bias=-MAGIC).then_inc(s["xqT_ready"], 1)
                elif slot == 4:
                    act.wait_ge(s["x2T_ps"], t + 1)
                    act.wait_ge(s["o_ps"], t)
                    nc.scalar.activation(x2T[:], ps_a[:], ACT.Copy).then_inc(s["x2T_ready"], 1)
                elif slot == 5:
                    act.wait_ge(s["f_ps"], t + 1)
                    act.wait_ge(s["f_ready"], t)
                    nc.scalar.activation(tanh_f[:], ps_b[:], ACT.Tanh, bias=gate_bh[:, 0:1], scale=0.5)\
                      .then_inc(s["tf_ready"], 1)
                    act.wait_ge(s["i_ps"], t + 1)
                    act.wait_ge(s["iz_ready"], t)
                    nc.scalar.activation(tanh_i[:], ps_a[:], ACT.Tanh, bias=gate_bh[:, 1:2], scale=0.5)\
                      .then_inc(s["ti_ready"], 1)
                elif slot == 6:
                    act.wait_ge(s["z_ps"], t + 1)
                    nc.scalar.activation(tanh_z[:], ps_b[:], ACT.Tanh, bias=gate_b[:, 2:3])\
                      .then_inc(s["tz_ready"], 1)
                    act.wait_ge(s["o_ps"], t + 1)
                    act.wait_ge(s["h2_ready"], t)
                    nc.scalar.activation(tanh_o[:].rearrange("p s e -> p (s e)"), ps_a[:], ACT.Tanh, scale=0.5)\
                      .then_inc(s["to_ready"], 1)
                elif slot == 8:
                    act.wait_ge(s["caff_ready"], t + 1)
                    nc.scalar.activation(tanh_c[:], c_aff[:], ACT.Tanh).then_inc(s["tc_ready"], 1)
                elif slot == 9:
                    act.wait_ge(s["x3T_ps"], t + 1)
                    if not (isinstance(t, int) and t == 0):
                        act.wait_ge(s["g_ps"], NJ * (t - 1))
                        act.wait_ge(s["u_ps"], NJ * (t - 1))
                    nc.scalar.activation(x3T_hi[p][:], ps_a[:], ACT.Copy).then_inc(s["x3hi_ready"], 1)
                elif slot == 10:
                    act.wait_ge(s["gap_ready"], t + 1)
                    act.wait_ge(s["route_step"], ROUTE * t)
                    nc.scalar.activation(tanh_gap[:], gap[:], ACT.Tanh, scale=0.5).then_inc(s["tgap_ready"], 1)
                    act.wait_ge(s["wT_ps"], t + 1)
                    if not (isinstance(t, int) and t == 0):
                        act.wait_ge(s["w_ps"], NJR * (t - 1))
                    nc.scalar.activation(w_partsT[p][:], ps_b[0:16, :], ACT.Copy).then_inc(s["wT_ready"], 1)

            def block_act(t, p, j):
                n = NJ * t + j
                b = (NJ * p + j) % 4
                m = P if j < NJ - 1 else LASTK
                act.wait_ge(s["g_ps"], n + 1)
                if not (isinstance(n, int) and n < 2):
                    act.wait_ge(s["gu_ready"], n - 1)
                nc.scalar.activation(silu_g[j % 2][0:m], ps_g[j % 2][0:m], ACT.Silu).then_inc(s["silu_ready"], 1)
                act.wait_ge(s["hid_ready"], n + 1)
                if not (isinstance(n, int) and n < 4):
                    act.wait_ge(s["down_ps"], n - 3)
                    act.wait_ge(s["lo_ready"], n - 3)
                nc.scalar.activation(hid_hi[b][0:m], hid[j % 2][0:m], ACT.Copy).then_inc(s["hi_ready"], 1)

            def finish(t):
                act.wait_ge(s["down_ps"], NJ * (t + 1))
                act.wait_ge(s["y_ps"], t)
                nc.scalar.activation(yT[:], ps_y[:], ACT.Copy).then_inc(s["yT_ready"], 1)

            def moe_tile(t, p, last):
                for j in range(NJ):
                    if j + AHEAD < NJ:
                        block_act(t, p, j + AHEAD)
                    elif not last:
                        block_act(t + 1, 1 - p, j + AHEAD - NJ)
                    if not last:
                        chain(t + 1, 1 - p, j)
                finish(t)

            act.wait_ge(s["gate_bh_ready"], 1)
            for slot in range(NJ):
                chain(0, 0, slot)
            for j in range(AHEAD):
                block_act(0, 0, j)
            with act.Fori(0, PAIRS - 1) as i:
                moe_tile(2 * i, 0, False)
                moe_tile(2 * i + 1, 1, False)
            moe_tile(NT - 2, 0, False)
            moe_tile(NT - 1, 1, True)

        @block.gpsimd
        def _(pool):
            nc.gpsimd.memset(ident[:], 0.0).then_inc(s["z_set"], 1)
            nc.gpsimd.memset(causal[:], 1.0).then_inc(s["z_set"], 1)
            nc.gpsimd.memset(head_of[:], 1.0).then_inc(s["z_set"], 1)
            pool.wait_ge(s["z_set"], 3)
            nc.gpsimd.affine_select(out=ident[:], in_=ident[:], compare_op=ALU.not_equal, fill=1.0, base=0,
                                    pattern=[[-1, P]], channel_multiplier=1).then_inc(s["one_set"], 1)
            nc.gpsimd.affine_select(out=causal[:], in_=causal[:], compare_op=ALU.is_ge, fill=0.0, base=0,
                                    pattern=[[1, CHUNK]], channel_multiplier=-1).then_inc(s["one_set"], 1)
            nc.gpsimd.affine_select(out=head_of_2[:], in_=head_of[:], compare_op=ALU.is_ge, fill=0.0, base=0,
                                    pattern=[[-4 * D, QUADS], [-D, 4]], channel_multiplier=1).then_inc(s["one_set"], 1)
            pool.wait_ge(s["one_set"], 3)
            nc.gpsimd.affine_select(out=head_of[:], in_=head_of_2[:], compare_op=ALU.is_ge, fill=0.0, base=D - 1,
                                    pattern=[[4 * D, QUADS], [D, 4]], channel_multiplier=-1).then_inc(s["one_set"], 1)
            nc.gpsimd.memset(ones_row[:], 1.0).then_inc(s["one_set"], 1)
            pool.wait_ge(s["one_set"], 5)
            nc.gpsimd.memset(minus_half[:], -0.5).then_inc(s["consts_ready"], 1)
            pool.wait_ge(s["consts_ready"], 1)
            nc.gpsimd.memset(w_ff[96:P, W_COLS - P:W_COLS], 0.0).then_inc(s["ff_pad_zero"], 1)
            pool.wait_ge(s["ff_pad_zero"], 1)
            for p in range(2):
                nc.gpsimd.memset(v_tok[p][:], 1.0).then_inc(s["v_ones"], 1)
            nc.gpsimd.memset(state[:], 0.0).then_inc(s["state_zero"], 1)
            nc.gpsimd.memset(carry[:], 0.0).then_inc(s["state_zero"], 1)
            nc.gpsimd.memset(keep[:], 1.0).then_inc(s["state_zero"], 1)
            pool.wait_ge(s["state_zero"], 3)
            nc.gpsimd.memset(keep[:, TPB // 2 - 1:TPB // 2], 0.0).then_inc(s["state_zero"], 1)
            pool.wait_ge(s["rows_bc_ready"], 1)

            def keep_residual(t, p):
                pool.wait_ge(s["x_loaded"], 16 * (t + 1))
                if not (isinstance(t, int) and t == 0):
                    pool.wait_ge(s["yattn_ready"], SUB * (t - 1))
                settled(pool)
                nc.gpsimd.tensor_tensor(x_bo[p][:], x_cur[p][:],
                                        rows_bc[:, 0:1, :].to_broadcast([P, SUB, E]), ALU.add)\
                  .then_inc(s["xbo_ready"], 1)

            def split_heads(t, p):
                pool.wait_ge(s["q_ready"], t + 1)
                if not (isinstance(t, int) and t == 0):
                    pool.wait_ge(s["score_ps"], 4 * SUB * (t - 1))
                settled(pool)
                for r in (2, 3):
                    nc.gpsimd.tensor_scalar(q_heads[p][:, r, :], qT[p][:], in_quad[:, r:r + 1], 1.0, ALU.mult, ALU.mult)\
                      .then_inc(s["qheads_p"], 1)

            def attn_rstd(t):
                pool.wait_ge(s["amv_ready"], SUB * (t + 1))
                pool.wait_ge(s["x1_ready"], SUB * t)
                settled(pool)
                nc.gpsimd.tensor_scalar(a_var[:], a_mv[:, :, 1], LN_EPS, 1.0, ALU.add, ALU.mult)\
                  .then_inc(s["avar_ready"], 1)
                pool.wait_ge(s["avar_ready"], t + 1)
                settled(pool)
                nc.gpsimd.tensor_tensor(a_rstd[:], a_var[:], minus_half[:], ALU.pow).then_inc(s["arstd_ready"], 1)

            def split_weights(t):
                cols = bass.ds(t * WSLICE, WSLICE)
                nc.gpsimd.tensor_copy(w_hi[:, cols], w_ff[:, cols]).then_inc(s["ff_hi"], 1)
                pool.wait_ge(s["ff_hi"], t + 1)
                settled(pool)
                nc.gpsimd.tensor_tensor(w_lo[:, cols], w_ff[:, cols], w_hi[:, cols].bitcast(F32), ALU.subtract)\
                  .then_inc(s["ff_split"], 1)

            keep_residual(0, 0)
            pool.wait_ge(s["quad_ready"], 1)
            split_heads(0, 0)
            for n, (dst, e0) in enumerate(((sel16, 0), (sel16_b, EXPERTS))):
                nc.gpsimd.memset(dst[:], 1.0).then_inc(s["sel_r_ready"], 1)
                pool.wait_ge(s["sel_r_ready"], 3 * n + 1)
                nc.gpsimd.affine_select(out=dst[:], in_=dst[:], compare_op=ALU.is_ge, fill=0.0, base=HID * e0,
                                        pattern=[[1, ROUTED]], channel_multiplier=-HID).then_inc(s["sel_r_ready"], 1)
                pool.wait_ge(s["sel_r_ready"], 3 * n + 2)
                nc.gpsimd.affine_select(out=dst[:], in_=dst[:], compare_op=ALU.is_ge, fill=0.0, base=HID - 1 - HID * e0,
                                        pattern=[[-1, ROUTED]], channel_multiplier=HID).then_inc(s["sel_r_ready"], 1)
                pool.wait_ge(s["sel_r_ready"], 3 * n + 3)
            nc.gpsimd.tensor_tensor(sel16_r[:], sel16[:], sel16_b[:], ALU.add).then_inc(s["sel_r_ready"], 1)
            nc.gpsimd.iota(rev_index[:], pattern=[[0, SUB], [-1, EXPERTS]], base=EXPERTS, channel_multiplier=0,
                           allow_small_or_imprecise_dtypes=True).then_inc(s["sel_r_ready"], 1)
            pool.wait_ge(s["wl_router"], 16)
            nc.gpsimd.tensor_copy(w_router_hi[:], w_router[:]).then_inc(s["router_hi"], 1)
            pool.wait_ge(s["router_hi"], 1)
            nc.gpsimd.tensor_tensor(w_router_lo[:], w_router[:], w_router_hi[:].bitcast(F32), ALU.subtract)\
              .then_inc(s["router_ready"], 1)
            pool.wait_ge(s["wl_ff"], 16 * 7)

            def tile(t, p, last):
                if not last:
                    keep_residual(t + 1, 1 - p)
                    split_heads(t + 1, 1 - p)
                split_weights(t)
                attn_rstd(t)

            with pool.Fori(0, PAIRS - 1) as i:
                tile(2 * i, 0, False)
                tile(2 * i + 1, 1, False)
            tile(NT - 2, 0, False)
            tile(NT - 1, 1, True)

            pool.wait_ge(s["amax1_ready"], 1)
            nc.gpsimd.partition_all_reduce(amax_all[:], amax1[:], P, bass.bass_isa.ReduceOp.max)\
              .then_inc(s["amax_all_ready"], 1)

            def norm_std(k, t, eps, ready, vareps, rs, used=None):
                pool.wait_ge(ready, SUB * (t + 1))
                if used is not None:
                    pool.wait_ge(used, SUB * t)
                settled(pool)
                nc.gpsimd.tensor_scalar(var_eps[k][:], mv[k][:, :, 1], eps, 1.0, ALU.add, ALU.mult)\
                  .then_inc(vareps, 1)
                pool.wait_ge(vareps, t + 1)
                settled(pool)
                nc.gpsimd.tensor_tensor(rstd[k][:], var_eps[k][:], minus_half[:], ALU.pow).then_inc(rs, 1)

            def chain(t, p, slot):
                if slot == 0:
                    pool.wait_ge(s["yffn_ready"], t)
                    settled(pool)
                    nc.gpsimd.tensor_tensor(x1_b[:], x1_all[:, bass.ds(SUB * t, SUB), :],
                                            rows_bc[:, 1:2, :].to_broadcast([P, SUB, E]), ALU.add)\
                      .then_inc(s["x1b_ready"], 1)
                elif slot == 2:
                    norm_std(0, t, LN_EPS, mv_r[0], ve_r[0], rs_r[0], nm_r[0])
                elif slot == 5:
                    pool.wait_ge(s["tf_ready"], t + 1)
                    pool.wait_ge(s["cell_ready"], t)
                    settled(pool)
                    nc.gpsimd.tensor_scalar(f_gate[:], tanh_f[:], 1.0, 0.5, ALU.add, ALU.mult)\
                      .then_inc(s["f_ready"], 1)
                elif slot == 7:
                    norm_std(1, t, 4 * LN_EPS, mv_r[1], ve_r[1], rs_r[1], nm_r[1])
                    pool.wait_ge(nm_r[1], SUB * (t + 1))
                    settled(pool)
                    nc.gpsimd.tensor_tensor(c_norm[:], c_norm[:], rows_bc[:, 3:4, :].to_broadcast([P, SUB, E]), ALU.mult)\
                      .then_inc(s["cscaled"], 1)
                    pool.wait_ge(s["cscaled"], t + 1)
                    pool.wait_ge(s["tc_ready"], t)
                    settled(pool)
                    nc.gpsimd.tensor_tensor(c_aff[:], c_norm[:], rows_bc[:, 4:5, :].to_broadcast([P, SUB, E]), ALU.add)\
                      .then_inc(s["caff_ready"], 1)
                elif slot == 8:
                    norm_std(2, t, LN_EPS, mv_r[2], ve_r[2], rs_r[2], nm_r[2])

            def block_pool(t, p, j):
                n = NJ * t + j
                b = (NJ * p + j) % 4
                m = P if j < NJ - 1 else LASTK
                pool.wait_ge(s["hi_ready"], n + 1)
                if not (isinstance(n, int) and n < 4):
                    pool.wait_ge(s["down_ps"], n - 3)
                settled(pool)
                nc.gpsimd.tensor_tensor(hid_lo[b][0:m], hid[j % 2][0:m], hid_hi[b][0:m].bitcast(F32), ALU.subtract)\
                  .then_inc(s["lo_ready"], 1)

            def moe_tile(t, p, last):
                for j in range(NJ):
                    if j + AHEAD < NJ:
                        block_pool(t, p, j + AHEAD)
                    elif not last:
                        block_pool(t + 1, 1 - p, j + AHEAD - NJ)
                    if not last:
                        chain(t + 1, 1 - p, j)
                norm_std(3, t, LN_EPS, mv_r[3], ve_r[3], rs_r[3], nm_r[3])

            for slot in range(NJ):
                chain(0, 0, slot)
            for j in range(AHEAD):
                block_pool(0, 0, j)
            with pool.Fori(0, PAIRS - 1) as i:
                moe_tile(2 * i, 0, False)
                moe_tile(2 * i + 1, 1, False)
            moe_tile(NT - 2, 0, False)
            moe_tile(NT - 1, 1, True)

        @block.vector
        def _(dve):
            dve.wait_ge(s["consts_ready"], 1)
            nc.vector.tensor_reduce(in_quad[:], head_of[:].rearrange("p g r -> p r g"), AX.X, ALU.add)\
              .then_inc(s["quad_ready"], 1)
            dve.wait_ge(s["wl_int8"], 16)
            nc.vector.tensor_copy(w_nat[:, 8, :], w8_raw[:, :, 0]).then_inc(s["w8_cast"], 1)
            dve.wait_ge(s["wl_rows"], 16 * 6)
            nc.vector.tensor_copy(o_bias4[:], rows[:, 5:6, :].to_broadcast([1, SUB, P])).then_inc(s["o_bias_ready"], 1)
            dve.wait_ge(s["wl_cols"], 16 * 3)
            nc.vector.tensor_scalar(gate_bh[:], gate_b[:, 0:2], 0.5, None, ALU.mult).then_inc(s["gate_bh_ready"], 1)
            dve.wait_ge(s["state_zero"], 4)
            dve.wait_ge(s["quad_ready"], 1)

            own_head = head_of[:].rearrange("p g r -> p (g r)").unsqueeze(2).to_broadcast([P, HEADS, DV])

            def front_q(t, p):
                dve.wait_ge(s["expq_ready"], t + 1)
                nc.vector.tensor_scalar(exp_q[:], exp_q[:], 1.0, None, ALU.min).then_inc(s["expq_min"], 1)
                dve.wait_ge(s["expq_min"], t + 1)
                if not (isinstance(t, int) and t == 0):
                    dve.wait_ge(s["attn_num_ps"], 4 * SUB * (t - 1))
                    dve.wait_ge(s["qheads_p"], 2 * (t - 1))
                nc.vector.scalar_tensor_tensor(qT[p][:], ps_proj[:], 0.0, exp_q[:], ALU.max, ALU.add)\
                  .then_inc(s["q_ready"], 1)

            def front_heads(t, p):
                dve.wait_ge(s["q_ready"], t + 1)
                if not (isinstance(t, int) and t == 0):
                    dve.wait_ge(s["score_ps"], 4 * SUB * (t - 1))
                for r in (0, 1):
                    nc.vector.tensor_scalar(q_heads[p][:, r, :], qT[p][:], in_quad[:, r:r + 1], None, ALU.mult)\
                      .then_inc(s["qheads_v"], 1)

            def front_k(t, p):
                dve.wait_ge(s["expk_ready"], t + 1)
                nc.vector.tensor_scalar(exp_k[:], exp_k[:], 1.0, None, ALU.min).then_inc(s["expk_min"], 1)
                dve.wait_ge(s["expk_min"], t + 1)
                if not (isinstance(t, int) and t == 0):
                    dve.wait_ge(s["score_ps"], 4 * SUB * (t - 1))
                    dve.wait_ge(s["ktok_ps"], t - 1)
                nc.vector.scalar_tensor_tensor(kT[p][:], ps_proj[:], 0.0, exp_k[:], ALU.max, ALU.add)\
                  .then_inc(s["k_ready"], 1)

            def mask(c, g):
                dve.wait_ge(s["score_ps"], 4 * c + g + 1)
                if not (isinstance(c, int) and c == 0):
                    dve.wait_ge(s["attn_num_ps"], 4 * (c - 1) + g + 1)
                nc.vector.tensor_tensor(scores[:, g, :].rearrange("p (r i) -> p r i", r=4),
                                        ps_scores[g][:].rearrange("p (r i) -> p r i", r=4),
                                        causal[:].unsqueeze(1).to_broadcast([P, 4, CHUNK]), ALU.mult)\
                  .then_inc(s["masked"], 1)

            def update_state(c, par, ends_row=None):
                dve.wait_ge(s["kv_ps"], c + 1)
                dve.wait_ge(s["attn_num_ps"], 4 * c + 4)
                dve.wait_ge(s["state_ready"], c)
                nc.vector.tensor_tensor(kv_own[:].rearrange("p (h d) -> p h d", h=HEADS),
                                        ps_kv.rearrange("p (h d) -> p h d", h=HEADS), own_head, ALU.mult)\
                  .then_inc(s["kv_own_ready"], 1)
                dve.wait_ge(s["kv_own_ready"], c + 1)
                if ends_row is None:
                    nc.vector.tensor_tensor(state[:, 1 - par, :], state[:, par, :], kv_own[:], ALU.add)\
                      .then_inc(s["state_ready"], 1)
                else:
                    nc.vector.tensor_tensor(kv_own[:], state[:, par, :], kv_own[:], ALU.add)\
                      .then_inc(s["state_kept"], 1)
                    dve.wait_ge(s["state_kept"], ends_row + 1)
                    settled(dve)
                    nc.vector.tensor_scalar(state[:, 1 - par, :], kv_own[:], keep[:, bass.ds(ends_row, 1)], None,
                                            ALU.mult).then_inc(s["state_ready"], 1)

            def normalise(c):
                num = ps_num.rearrange("p (h d) -> p h d", h=HEADS)
                dve.wait_ge(s["rden_ready"], c)
                nc.vector.tensor_scalar(den[:], num[:, :, D], DEN_EPS, None, ALU.add).then_inc(s["den_ready"], 1)
                dve.wait_ge(s["den_ready"], c + 1)
                dve.wait_ge(s["attn_ready"], c)
                nc.vector.reciprocal(rden[:], den[:]).then_inc(s["rden_ready"], 1)
                dve.wait_ge(s["rden_ready"], c + 1)
                dve.wait_ge(s["attnT_ps"], c)
                nc.vector.tensor_tensor(attn[:], num[:, :, 0:D], rden[:].unsqueeze(2).to_broadcast([P, HEADS, D]),
                                        ALU.mult).then_inc(s["attn_ready"], 1)

            def residual(t, p, n):
                c = SUB * t + n
                dve.wait_ge(s["wo_ps"], c + 1)
                dve.wait_ge(s["xbo_ready"], t + 1)
                dve.wait_ge(s["x1_ready"], SUB * t)
                nc.vector.tensor_tensor(y_attn[:, n, :], ps_wo, x_bo[p][:, n, :], ALU.add)\
                  .then_inc(s["yattn_ready"], 1)
                dve.wait_ge(s["yattn_ready"], c + 1)
                dve.wait_ge(s["amv_ready"], SUB * t)
                nc.vector.bn_stats(a_stats[:, n, :], y_attn[:, n, :]).then_inc(s["astats_ready"], 1)

            def attn_norm(t):
                for n in range(SUB):
                    dve.wait_ge(s["astats_ready"], SUB * t + n + 1)
                    dve.wait_ge(s["avar_ready"], t)
                    settled(dve)
                    nc.vector.bn_aggr(a_mv[:, n, :], a_stats[:, n, :]).then_inc(s["amv_ready"], 1)
                dve.wait_ge(s["arstd_ready"], t + 1)
                settled(dve)
                for n in range(SUB):
                    nc.vector.tensor_scalar(x1_all[:, bass.ds(SUB * t + n, 1), :],
                                            y_attn[:, n:n + 1, :], a_mv[:, n, 0:1],
                                            a_rstd[:, n:n + 1], ALU.subtract, ALU.mult).then_inc(s["x1_ready"], 1)
                dve.wait_ge(s["x1_ready"], SUB * (t + 1))
                settled(dve)
                nc.vector.tensor_reduce(amax[:, bass.ds(t, 1)], x1_all[:, bass.ds(SUB * t, SUB), :]
                                        .rearrange("p s e -> p (s e)"), AX.X, ALU.max,
                                        apply_absolute_value=True).then_inc(s["amax_ready"], 1)

            def attn_tile(t, p, i, last):
                for n in range(SUB):
                    c = SUB * t + n
                    update_state(c, n % 2, ends_row=i if (p == 1 and n == SUB - 1) else None)
                    normalise(c)
                    more = not (last and n == SUB - 1)
                    if more:
                        mask(c + 1, 0)
                    if not last and n == 0:
                        front_q(t + 1, 1 - p)
                    if not last and n == 1:
                        front_k(t + 1, 1 - p)
                    if more:
                        mask(c + 1, 1)
                    if not last and n == 0:
                        front_heads(t + 1, 1 - p)
                    if more:
                        mask(c + 1, 2)
                        mask(c + 1, 3)
                    residual(t, p, n)
                attn_norm(t)

            front_q(0, 0)
            front_heads(0, 0)
            front_k(0, 0)
            for g in range(QUADS):
                mask(0, g)
            with dve.Fori(0, PAIRS - 1) as i:
                attn_tile(2 * i, 0, i, False)
                attn_tile(2 * i + 1, 1, i, False)
            attn_tile(NT - 2, 0, PAIRS - 1, False)
            attn_tile(NT - 1, 1, PAIRS - 1, True)

            dve.wait_ge(s["amax_ready"], NT)
            nc.vector.tensor_reduce(amax1[:], amax[:], AX.X, ALU.max).then_inc(s["amax1_ready"], 1)
            dve.wait_ge(s["amax_all_ready"], 1)
            nc.vector.tensor_scalar(x_scale[:], amax_all[:], 1.0 / 127.0, SCALE_EPS, ALU.mult, ALU.max)\
              .then_inc(s["scale_ready"], 1)
            dve.wait_ge(s["scale_ready"], 1)
            nc.vector.reciprocal(inv_scale[:], x_scale[:]).then_inc(s["scale_ready"], 1)
            nc.vector.tensor_scalar(deq_scale[:], rows_bc[:, 2, :], x_scale[:], None, ALU.mult)\
              .then_inc(s["deq_ready"], 1)
            dve.wait_ge(s["scale_ready"], 2)
            dve.wait_ge(s["deq_ready"], 1)

            def layer_stats(k, t, src):
                for n in range(SUB):
                    dve.wait_ge(mv_r[k], SUB * t)
                    nc.vector.bn_stats(stats[k][:, n, :], src(n)).then_inc(st_r[k], 1)
                for n in range(SUB):
                    dve.wait_ge(st_r[k], SUB * t + n + 1)
                    dve.wait_ge(ve_r[k], t)
                    settled(dve)
                    nc.vector.bn_aggr(mv[k][:, n, :], stats[k][:, n, :]).then_inc(mv_r[k], 1)

            def layer_norm(k, t, dst, src):
                dve.wait_ge(rs_r[k], t + 1)
                for n in range(SUB):
                    nc.vector.tensor_scalar(dst(n), src(n), mv[k][:, n, 0:1], rstd[k][:, n:n + 1],
                                            ALU.subtract, ALU.mult).then_inc(nm_r[k], 1)

            def chain(t, p, i, slot):
                if slot == 0:
                    dve.wait_ge(s["xqT_ps"], t)
                    settled(dve)
                    nc.vector.tensor_scalar(xq[:], x1_all[:, bass.ds(SUB * t, SUB), :], inv_scale[:], MAGIC,
                                            ALU.mult, ALU.add).then_inc(s["xq_round"], 1)
                    dve.wait_ge(s["xq_round"], t + 1)
                    nc.vector.tensor_scalar(xq[:], xq[:], MAGIC - 128.0, MAGIC + 127.0, ALU.max, ALU.min)\
                      .then_inc(s["xq_ready"], 1)
                elif slot == 2:
                    dve.wait_ge(s["q8_ps"], t + 1)
                    dve.wait_ge(nm_r[0], SUB * t)
                    nc.vector.tensor_tensor(y_ffn[:], ps_b[:].rearrange("p (s e) -> p s e", s=SUB),
                                            deq_scale[:].unsqueeze(1).to_broadcast([P, SUB, E]), ALU.mult)\
                      .then_inc(s["deq_done"], 1)
                    dve.wait_ge(s["deq_done"], t + 1)
                    dve.wait_ge(s["x1b_ready"], t + 1)
                    nc.vector.tensor_tensor(y_ffn[:], y_ffn[:], x1_b[:], ALU.add).then_inc(s["yffn_ready"], 1)
                    dve.wait_ge(s["yffn_ready"], t + 1)
                    layer_stats(0, t, lambda n: y_ffn[:, n, :])
                elif slot == 3:
                    dve.wait_ge(s["ylstm_ready"], t)
                    dve.wait_ge(s["x2T_ps"], t)
                    layer_norm(0, t, lambda n: x2[:, n, :], lambda n: y_ffn[:, n, :])
                elif slot == 6:
                    dve.wait_ge(s["ti_ready"], t + 1)
                    dve.wait_ge(s["tz_ready"], t + 1)
                    dve.wait_ge(s["cell_ready"], t)
                    nc.vector.scalar_tensor_tensor(iz2[:], tanh_i[:], 1.0, tanh_z[:], ALU.add, ALU.mult)\
                      .then_inc(s["iz_ready"], 1)
                    dve.wait_ge(s["iz_ready"], t + 1)
                    dve.wait_ge(s["f_ready"], t + 1)
                    dve.wait_ge(s["carry_ready"], t)
                    dve.wait_ge(s["cellT_ps"], t)
                    nc.vector.tensor_tensor_scan(cell2[:], f_gate[:], iz2[:], carry[:], ALU.mult, ALU.add)\
                      .then_inc(s["cell_ready"], 1)
                    dve.wait_ge(s["cell_ready"], t + 1)
                    if p == 1:
                        settled(dve)
                        nc.vector.tensor_scalar(carry[:], cell2[:, TILE - 1:TILE], keep[:, bass.ds(i, 1)], None, ALU.mult)\
                          .then_inc(s["carry_ready"], 1)
                    else:
                        nc.vector.tensor_copy(carry[:], cell2[:, TILE - 1:TILE]).then_inc(s["carry_ready"], 1)
                elif slot == 7:
                    dve.wait_ge(s["cellT_ps"], t + 1)
                    layer_stats(1, t, lambda n: ps_b[:, P * n:P * n + P])
                    dve.wait_ge(s["caff_ready"], t)
                    layer_norm(1, t, lambda n: c_norm[:, n, :], lambda n: ps_b[:, P * n:P * n + P])
                elif slot == 8:
                    dve.wait_ge(s["tc_ready"], t + 1)
                    dve.wait_ge(s["to_ready"], t + 1)
                    dve.wait_ge(s["ylstm_ready"], t)
                    nc.vector.scalar_tensor_tensor(h2[:], tanh_o[:], 1.0, tanh_c[:], ALU.add, ALU.mult)\
                      .then_inc(s["h2_ready"], 1)
                    dve.wait_ge(s["h2_ready"], t + 1)
                    dve.wait_ge(nm_r[2], SUB * t)
                    nc.vector.scalar_tensor_tensor(y_lstm[:], h2[:], 0.5, x2[:], ALU.mult, ALU.add)\
                      .then_inc(s["ylstm_ready"], 1)
                    dve.wait_ge(s["ylstm_ready"], t + 1)
                    layer_stats(2, t, lambda n: y_lstm[:, n, :])
                elif slot == 9:
                    if not (isinstance(t, int) and t == 0):
                        dve.wait_ge(s["ymoe_ready"], t - 1)
                    layer_norm(2, t, lambda n: x3[p][:, n, :], lambda n: y_lstm[:, n, :])
                    dve.wait_ge(s["x3T_ps"], t + 1)
                    dve.wait_ge(s["x3hi_ready"], t + 1)
                    if not (isinstance(t, int) and t == 0):
                        dve.wait_ge(s["u_ps"], NJ * (t - 1))
                    nc.vector.tensor_tensor(x3T_lo[p][:], ps_a[:], x3T_hi[p][:].bitcast(F32), ALU.subtract)\
                      .then_inc(s["x3lo_ready"], 1)
                elif slot == 10:
                    route(t)

            def route(t):
                def after(n):
                    dve.wait_ge(s["route_step"], ROUTE * t + n)

                def step(ins):
                    ins.then_inc(s["route_step"], 1)

                each = lambda a: a[:].unsqueeze(2).to_broadcast([P, SUB, EXPERTS])
                dve.wait_ge(s["logit_ps"], t + 1)
                after(0)
                step(nc.vector.tensor_copy(logits[:], ps_b[:, 0:SUB * EXPERTS].rearrange("p (s e) -> p s e", s=SUB)))
                left = logits
                for k in range(2):
                    after(7 * k + 1)
                    step(nc.vector.tensor_reduce(top[k][:], left[:], AX.X, ALU.max))
                    after(7 * k + 2)
                    step(nc.vector.tensor_tensor(is_top[k][:], left[:], each(top[k]), ALU.is_equal))
                    after(7 * k + 3)
                    step(nc.vector.tensor_tensor(rank[k][:], is_top[k][:], rev_index[:], ALU.mult))
                    after(7 * k + 4)
                    step(nc.vector.tensor_reduce(best[k][:], rank[k][:], AX.X, ALU.max))
                    after(7 * k + 5)
                    step(nc.vector.tensor_tensor(pick[k][:], rank[k][:], each(best[k]), ALU.is_equal))
                    if k == 0:
                        after(6)
                        step(nc.vector.scalar_tensor_tensor(logits2[:], pick[0][:], -3.0e38, logits[:],
                                                            ALU.mult, ALU.add))
                        step(nc.vector.tensor_copy(pick_sum[:], pick[0][:]))
                        left = logits2
                after(13)
                dve.wait_ge(s["tgap_ready"], t)
                nc.vector.tensor_tensor(gap[:], top[0][:], top[1][:], ALU.subtract).then_inc(s["gap_ready"], 1)
                step(nc.vector.tensor_tensor(pick_dif[:], pick_sum[:], pick[1][:], ALU.subtract))
                after(14)
                step(nc.vector.tensor_tensor(pick_sum[:], pick_sum[:], pick[1][:], ALU.add))
                dve.wait_ge(s["tgap_ready"], t + 1)
                after(15)
                step(nc.vector.tensor_tensor(dif_t[:], pick_dif[:], each(tanh_gap), ALU.mult))
                after(16)
                step(nc.vector.tensor_tensor(w2x[:], pick_sum[:], dif_t[:], ALU.add))
                after(17)
                step(nc.vector.tensor_scalar(w_tok[:], w2x[:], 0.5, None, ALU.mult))
                after(18)
                step(nc.vector.tensor_copy(w_tok_r[:], w_tok[:]))
                after(19)
                dve.wait_ge(s["wT_ps"], t)
                step(nc.vector.tensor_copy(w_parts[:, :, 0, :], w_tok_r[:].bitcast(F32)))
                step(nc.vector.tensor_tensor(w_parts[:, :, 1, :], w_tok[:], w_tok_r[:].bitcast(F32), ALU.subtract))

            def block_dve(t, p, j):
                n = NJ * t + j
                m = P if j < NJ - 1 else LASTK
                early = isinstance(n, int) and n < 2
                dve.wait_ge(s["silu_ready"], n + 1)
                dve.wait_ge(s["u_ps"], n + 1)
                if not early:
                    dve.wait_ge(s["hid_ready"], n - 1)
                nc.vector.tensor_tensor(gu[j % 2][0:m], silu_g[j % 2][0:m], ps_u[j % 2][0:m], ALU.mult)\
                  .then_inc(s["gu_ready"], 1)
                dve.wait_ge(s["gu_ready"], n + 1)
                if not early:
                    dve.wait_ge(s["hi_ready"], n - 1)
                    dve.wait_ge(s["lo_ready"], n - 1)
                if j < NJR:
                    dve.wait_ge(s["w_ps"], NJR * t + j + 1)
                    nc.vector.tensor_tensor(hid[j % 2][0:m], gu[j % 2][0:m], ps_w[0:m], ALU.mult)\
                      .then_inc(s["hid_ready"], 1)
                else:
                    nc.vector.tensor_copy(hid[j % 2][0:m], gu[j % 2][0:m]).then_inc(s["hid_ready"], 1)

            def finish(t, p):
                dve.wait_ge(s["y_ps"], t + 1)
                dve.wait_ge(nm_r[3], SUB * t)
                nc.vector.tensor_tensor(y_moe[:], ps_a[:].rearrange("p (s e) -> p s e", s=SUB), x3[p][:], ALU.add)\
                  .then_inc(s["ymoe_ready"], 1)
                dve.wait_ge(s["ymoe_ready"], t + 1)
                layer_stats(3, t, lambda n: y_moe[:, n, :])
                dve.wait_ge(s["out_stored"], 16 * t)
                layer_norm(3, t, lambda n: x4[:, n, :], lambda n: y_moe[:, n, :])

            def moe_tile(t, p, i, last):
                for j in range(NJ):
                    if j + AHEAD < NJ:
                        block_dve(t, p, j + AHEAD)
                    elif not last:
                        block_dve(t + 1, 1 - p, j + AHEAD - NJ)
                    if not last:
                        chain(t + 1, 1 - p, i, j)
                finish(t, p)

            for slot in range(NJ):
                chain(0, 0, None, slot)
            for j in range(AHEAD):
                block_dve(0, 0, j)
            with dve.Fori(0, PAIRS - 1) as i:
                moe_tile(2 * i, 0, i, False)
                moe_tile(2 * i + 1, 1, i, False)
            moe_tile(NT - 2, 0, PAIRS - 1, False)
            moe_tile(NT - 1, 1, PAIRS - 1, True)

        @block.tensor
        def _(pe):
            def turn(dst, src):
                return nc.tensor.transpose(dst, src, ident[0:src.shape[0], 0:src.shape[0]])

            pe.wait_ge(s["consts_ready"], 1)
            pe.wait_ge(s["wl_square"], 16 * 5)
            for b in range(2):
                for n in range(4):
                    ins = turn(ps_scores[b][:, P * n:P * n + P], w_nat[:, 4 * b + n, :])
                ins.then_inc(s["w_tr"], 1)
            pe.wait_ge(s["w8_cast"], 1)
            turn(ps_scores[2][:, 0:P], w_nat[:, 8, :]).then_inc(s["w_tr"], 1)
            pe.wait_ge(s["wl_rows"], 16 * 6)
            nc.tensor.matmul(ps_scores[3][:], ones_row[:], rows[:, 0:4, :], start=True, stop=True)\
              .then_inc(s["rows_bc_ps"], 1)
            nc.tensor.matmul(ps_tr[:, 0:P], ones_row[:], rows[:, 4, :], start=True, stop=True)\
              .then_inc(s["rows_bc_ps"], 1)
            pe.wait_ge(s["w_tr_copied"], 2)
            pe.wait_ge(s["w8T_ready"], 1)
            pe.wait_ge(s["rows_bc_ready"], 2)
            pe.wait_ge(s["state_zero"], 4)

            def x_transposed(t, p):
                pe.wait_ge(s["x_loaded"], 16 * (t + 1))
                pe.wait_ge(s["ktok_ready"], t)
                for n in range(SUB):
                    ins = turn(ps_tr[:, P * n:P * n + P], x_cur[p][:, n, :])
                ins.then_inc(s["xT_ps"], 1)

            def project_q(t):
                pe.wait_ge(s["xT_ready"], t + 1)
                pe.wait_ge(s["v_ready"], t)
                nc.tensor.matmul(ps_proj[:], wT[:, 0, :], xT[:], start=True, stop=True).then_inc(s["q_ps"], 1)

            def project_k(t):
                pe.wait_ge(s["q_ready"], t + 1)
                nc.tensor.matmul(ps_proj[:], wT[:, 1, :], xT[:], start=True, stop=True).then_inc(s["k_ps"], 1)

            def project_v(t):
                pe.wait_ge(s["k_ready"], t + 1)
                for n in range(SUB):
                    ins = nc.tensor.matmul(ps_proj[:, P * n:P * n + P], xT[:, P * n:P * n + P], wT[:, 2, :],
                                           start=True, stop=True)
                ins.then_inc(s["v_ps"], 1)

            def k_transposed(t, p):
                pe.wait_ge(s["k_ready"], t + 1)
                pe.wait_ge(s["xT_ready"], t + 1)
                for n in range(SUB):
                    ins = turn(ps_tr[:, P * n:P * n + P], kT[p][:, P * n:P * n + P])
                ins.then_inc(s["ktok_ps"], 1)

            def score(c, n, p, t, g):
                rows32 = slice(32 * g, 32 * g + 32)
                if n == 0 and g == 0:
                    pe.wait_ge(s["k_ready"], t + 1)
                    pe.wait_ge(s["qheads_v"], 2 * (t + 1))
                    pe.wait_ge(s["qheads_p"], 2 * (t + 1))
                if not (isinstance(c, int) and c == 0):
                    pe.wait_ge(s["masked"], 4 * (c - 1) + g + 1)
                nc.tensor.matmul(ps_scores[g][:].rearrange("p (r i) -> p r i", r=4),
                                 kT[p][rows32, CHUNK * n:CHUNK * (n + 1)],
                                 q_heads[p][rows32, :, CHUNK * n:CHUNK * (n + 1)],
                                 start=True, stop=True).then_inc(s["score_ps"], 1)

            def attend(c, n, p):
                o = ps_num
                pe.wait_ge(s["state_ready"], c)
                nc.tensor.matmul(o, qT[p][:, CHUNK * n:CHUNK * (n + 1)], state[:, n % 2, :], start=True, stop=False)
                for g in range(QUADS):
                    pe.wait_ge(s["masked"], 4 * c + g + 1)
                    for r in range(4):
                        h = 4 * g + r
                        ins = nc.tensor.matmul(o[:, DV * h:DV * h + DV], scores[:, g, CHUNK * r:CHUNK * (r + 1)],
                                               v_tok[p][:, n, h, :], start=False, stop=(h == HEADS - 1))
                    ins.then_inc(s["attn_num_ps"], 1)

            def key_values(c, n, p, t):
                if n == 0:
                    pe.wait_ge(s["ktok_ready"], t + 1)
                    pe.wait_ge(s["v_ready"], t + 1)
                pe.wait_ge(s["kv_own_ready"], c)
                pe.wait_ge(s["attn_ready"], c)
                nc.tensor.matmul(ps_kv, k_tok[p][:, n, :], v_tok[p][:, n, :, :].rearrange("p h d -> p (h d)"),
                                 start=True, stop=True).then_inc(s["kv_ps"], 1)

            def attn_transposed(c):
                pe.wait_ge(s["attn_ready"], c + 1)
                pe.wait_ge(s["yattn_ready"], c)
                turn(ps_attnT, attn[:].rearrange("p h d -> p (h d)")).then_inc(s["attnT_ps"], 1)

            def out_project(c):
                pe.wait_ge(s["attnT_ready"], c + 1)
                nc.tensor.matmul(ps_wo, attnT[:], wT[:, 3, :], start=True, stop=True).then_inc(s["wo_ps"], 1)

            def attn_tile(t, p, last):
                for n in range(SUB):
                    c = SUB * t + n
                    nt, np_, nn = (t, p, n + 1) if n < SUB - 1 else (t + 1, 1 - p, 0)
                    more = not (last and n == SUB - 1)
                    if not last and n == 0:
                        x_transposed(t + 1, 1 - p)
                    key_values(c, n, p, t)
                    attend(c, n, p)
                    if more:
                        score(c + 1, nn, np_, nt, 0)
                    if not last and n < 3:
                        (project_q, project_k, project_v)[n](t + 1)
                    if more:
                        score(c + 1, nn, np_, nt, 1)
                    attn_transposed(c)
                    if not last and n == 2:
                        k_transposed(t + 1, 1 - p)
                    if more:
                        score(c + 1, nn, np_, nt, 2)
                        score(c + 1, nn, np_, nt, 3)
                    out_project(c)

            x_transposed(0, 0)
            project_q(0)
            project_k(0)
            project_v(0)
            k_transposed(0, 0)
            for g in range(QUADS):
                score(0, 0, 0, 0, g)
            with pe.Fori(0, PAIRS - 1) as i:
                attn_tile(2 * i, 0, False)
                attn_tile(2 * i + 1, 1, False)
            attn_tile(NT - 2, 0, False)
            attn_tile(NT - 1, 1, True)

            pe.wait_ge(s["yattn_ready"], NC)
            pe.wait_ge(s["o_bias_ready"], 1)

            def chain(t, p, slot):
                if slot == 0:
                    pe.wait_ge(s["xq_ready"], t + 1)
                    if not (isinstance(t, int) and t == 0):
                        pe.wait_ge(s["ymoe_ready"], t - 1)
                    for n in range(SUB):
                        ins = turn(ps_a[:, P * n:P * n + P], xq[:, n, :])
                    ins.then_inc(s["xqT_ps"], 1)
                elif slot == 1:
                    pe.wait_ge(s["xqT_ready"], t + 1)
                    pe.wait_ge(s["wT_ready"], t)
                    for n in range(SUB):
                        ins = nc.tensor.matmul(ps_b[:, P * n:P * n + P], xqT[:, P * n:P * n + P], w8T[:],
                                               start=True, stop=True)
                    ins.then_inc(s["q8_ps"], 1)
                elif slot == 3:
                    pe.wait_ge(nm_r[0], SUB * (t + 1))
                    for n in range(SUB):
                        ins = turn(ps_a[:, P * n:P * n + P], x2[:, n, :])
                    ins.then_inc(s["x2T_ps"], 1)
                elif slot == 4:
                    pe.wait_ge(s["x2T_ready"], t + 1)
                    pe.wait_ge(s["deq_done"], t + 1)
                    nc.tensor.matmul(ps_b[:], wT[:, 4, :], x2T[:], start=True, stop=True).then_inc(s["f_ps"], 1)
                    nc.tensor.matmul(ps_a[:], wT[:, 5, :], x2T[:], start=True, stop=True).then_inc(s["i_ps"], 1)
                elif slot == 5:
                    pe.wait_ge(s["tf_ready"], t + 1)
                    nc.tensor.matmul(ps_b[:], wT[:, 7, :], x2T[:], start=True, stop=True).then_inc(s["z_ps"], 1)
                    pe.wait_ge(s["ti_ready"], t + 1)
                    nc.tensor.matmul(ps_a[:], ones_row[:], o_bias4[:].rearrange("o s e -> o (s e)"),
                                     start=True, stop=False)
                    for n in range(SUB):
                        ins = nc.tensor.matmul(ps_a[:, P * n:P * n + P], x2T[:, P * n:P * n + P], wT[:, 6, :],
                                               start=False, stop=(n == SUB - 1))
                    ins.then_inc(s["o_ps"], 1)
                elif slot == 6:
                    pe.wait_ge(s["cell_ready"], t + 1)
                    pe.wait_ge(s["tz_ready"], t + 1)
                    for n in range(SUB):
                        ins = turn(ps_b[:, P * n:P * n + P], cell2[:, P * n:P * n + P])
                    ins.then_inc(s["cellT_ps"], 1)
                elif slot == 9:
                    pe.wait_ge(nm_r[2], SUB * (t + 1))
                    pe.wait_ge(s["to_ready"], t + 1)
                    for n in range(SUB):
                        ins = turn(ps_a[:, P * n:P * n + P], x3[p][:, n, :])
                    ins.then_inc(s["x3T_ps"], 1)
                elif slot == 10:
                    pe.wait_ge(s["x3hi_ready"], t + 1)
                    pe.wait_ge(s["x3lo_ready"], t + 1)
                    pe.wait_ge(nm_r[1], SUB * (t + 1))
                    pe.wait_ge(s["router_ready"], 1)
                    for n in range(SUB):
                        o = ps_b[:, EXPERTS * n:EXPERTS * (n + 1)]
                        tok = slice(P * n, P * n + P)
                        nc.tensor.matmul(o, x3T_hi[p][:, tok], w_router_hi[:], start=True, stop=False)
                        nc.tensor.matmul(o, x3T_lo[p][:, tok], w_router_hi[:], start=False, stop=False)
                        ins = nc.tensor.matmul(o, x3T_hi[p][:, tok], w_router_lo[:], start=False, stop=True)
                    ins.then_inc(s["logit_ps"], 1)
                    pe.wait_ge(s["route_step"], ROUTE * (t + 1))
                    for n in range(SUB):
                        ins = turn(ps_b[0:16, P * n:P * n + P], w_parts[:, n, :, :].rearrange("p a e -> p (a e)"))
                    ins.then_inc(s["wT_ps"], 1)

            def product3(o, w_cols, m, hi, lo, first, last):
                k = hi.shape[0]
                nc.tensor.matmul(o, w_hi[0:k, w_cols:w_cols + m], hi, start=first, stop=False)
                nc.tensor.matmul(o, w_hi[0:k, w_cols:w_cols + m], lo, start=False, stop=False)
                return nc.tensor.matmul(o, w_lo[0:k, w_cols:w_cols + m], hi, start=False, stop=last)

            def up(t, p, j):
                n = NJ * t + j
                m = P if j < NJ - 1 else LASTK
                early = isinstance(n, int) and n < 2
                if not early:
                    pe.wait_ge(s["silu_ready"], n - 1)
                product3(ps_g[j % 2][0:m], P * j, m, x3T_hi[p][:], x3T_lo[p][:], True, True).then_inc(s["g_ps"], 1)
                if not early:
                    pe.wait_ge(s["gu_ready"], n - 1)
                product3(ps_u[j % 2][0:m], HALL + P * j, m, x3T_hi[p][:], x3T_lo[p][:], True, True)\
                    .then_inc(s["u_ps"], 1)
                if j < NJR:
                    if j == 0:
                        pe.wait_ge(s["wT_ready"], t + 1)
                    pe.wait_ge(s["hid_ready"], n)
                    nc.tensor.matmul(ps_w[:], sel16_r[:, P * j:P * j + P], w_partsT[p][:], start=True, stop=True)\
                      .then_inc(s["w_ps"], 1)

            def down(t, p, j):
                n = NJ * t + j
                b = (NJ * p + j) % 4
                m = P if j < NJ - 1 else LASTK
                if j == 0:
                    pe.wait_ge(s["yT_ready"], t)
                pe.wait_ge(s["hi_ready"], n + 1)
                pe.wait_ge(s["lo_ready"], n + 1)
                product3(ps_y[:], 2 * HALL + P * j, P, hid_hi[b][0:m], hid_lo[b][0:m], j == 0, j == NJ - 1)\
                    .then_inc(s["down_ps"], 1)

            def finish(t):
                pe.wait_ge(s["yT_ready"], t + 1)
                for n in range(SUB):
                    ins = turn(ps_a[:, P * n:P * n + P], yT[:, P * n:P * n + P])
                ins.then_inc(s["y_ps"], 1)

            def moe_tile(t, p, last):
                for j in range(NJ):
                    down(t, p, j)
                    if j + AHEAD < NJ:
                        up(t, p, j + AHEAD)
                    elif not last:
                        up(t + 1, 1 - p, j + AHEAD - NJ)
                    if not last:
                        chain(t + 1, 1 - p, j)
                finish(t)

            for slot in range(NJ):
                chain(0, 0, slot)
            pe.wait_ge(s["ff_split"], NT)
            pe.wait_ge(s["sel_r_ready"], 8)
            for j in range(AHEAD):
                up(0, 0, j)
            with pe.Fori(0, PAIRS - 1) as i:
                moe_tile(2 * i, 0, False)
                moe_tile(2 * i + 1, 1, False)
            moe_tile(NT - 2, 0, False)
            moe_tile(NT - 1, 1, True)


_INS = ['L0_attn_x', 'L0_attn_Wq', 'L0_attn_Wk', 'L0_attn_Wv', 'L0_attn_Wo', 'L0_attn_bo', 'L0_ffn_weight_int8',
        'L0_ffn_weight_scale', 'L0_ffn_bias', 'L1_attn_W', 'L1_attn_b', 'L1_attn_ln_w', 'L1_attn_ln_b', 'L1_ffn_Wg',
        'L1_ffn_W1', 'L1_ffn_W2', 'L1_ffn_W3', 'L1_ffn_Ws1', 'L1_ffn_Ws2', 'L1_ffn_Ws3']
_OUTS = [((2, 2048, 128), 'float32')]


def kernel(**inputs):
    import numpy as _np
    import concourse.bacc as _bacc
    from concourse import mybir as _mybir
    from concourse.bass_utils import run_bass_kernel_spmd as _run

    nc = _bacc.Bacc("TRN2", target_bir_lowering=False, num_devices=1)
    arrays, args = {}, []
    for name in _INS:
        a = _np.ascontiguousarray(inputs[name])
        if a.dtype.kind in "iu":
            a = a.astype(_np.int64)
        arrays[f"in_{name}_dram"] = a
        args.append(nc.dram_tensor(f"in_{name}_dram", a.shape, _mybir.dt.from_np(a.dtype), kind="ExternalInput").ap())
    for i, (shape, dtype) in enumerate(_OUTS):
        dt = _mybir.dt.from_np(_np.dtype(dtype))
        args.append(nc.dram_tensor(f"out_{i}_dram", shape, dt, kind="ExternalOutput").ap())
    build_program(nc, *args)
    r = _run(nc, [arrays], core_ids=[0])
    got = tuple(r.results[0][f"out_{i}_dram"] for i in range(len(_OUTS)))
    return got[0]
```

```python
import concourse.bass as bass
from concourse import mybir
from contextlib import ExitStack

F32 = mybir.dt.float32
F32R = mybir.dt.float32r
BF16 = mybir.dt.bfloat16
I32 = mybir.dt.int32
ALU = mybir.AluOpType
ACT = mybir.ActivationFunctionType
AX = mybir.AxisListType

P = 128
CHUNK = 128
SUB = 4
TILE = SUB * CHUNK
LN_EPS = 1e-5
DEN_EPS = 1e-5
SCALE_EPS = 1e-5
MAGIC = 1.5 * 2.0 ** 23


def build_program(nc, x_in, Wq, Wk, Wv, Wo, bo, W8, w8_scale, ffn_bias, Wgates, gate_bias,
                  ln_w, ln_b, Wrouter, W1, W2, W3, Ws1, Ws2, Ws3, out):
    B, T_LEN, E = x_in.shape
    HEADS = 16
    D = E // HEADS
    QUADS = 4
    DV = D + 1
    NT = B * T_LEN // TILE
    NC = NT * SUB
    PAIRS = NT // 2
    TPB = T_LEN // TILE
    EXPERTS = Wrouter.shape[1]
    HID = W1.shape[2]
    HSH = Ws1.shape[1]
    ROUTED = EXPERTS * HID
    HALL = ROUTED + HSH
    NJ = -(-HALL // P)
    NJR = ROUTED // P
    LASTK = HALL - (NJ - 1) * P
    ROUTE = 21
    AHEAD = 3
    W_COLS = 2 * HALL + NJ * P
    WSLICE = W_COLS // NT
    SPAN = [CHUNK - 32 * b for b in range(4)]
    SPAN_AT = [0, 128, 224, 288]
    SPANS = sum(SPAN)
    QV = 4 * DV
    assert ROUTED % P == 0 and W_COLS % NT == 0 and E == P and TPB % 2 == 0

    x_tiles = x_in.rearrange("b (n s p) e -> (b n) p s e", p=P, s=SUB)
    out_tiles = out.rearrange("b (n s p) e -> (b n) p s e", p=P, s=SUB)

    with ExitStack() as ctx:
        def sb(name, shape, dt=F32):
            return ctx.enter_context(nc.sbuf_tensor(name, shape, dt))

        def bank(name, shape, dt=F32):
            return ctx.enter_context(nc.psum_tensor(name, shape, dt))

        def sem(name):
            return ctx.enter_context(nc.semaphore(name))

        ident = sb("ident", [P, P])
        causal = sb("causal", [P, SPANS])
        head_of = sb("head_of", [P, QUADS, 4])
        head_of_2 = sb("head_of_2", [P, QUADS, 4])
        in_quad = sb("in_quad", [P, 4])
        keep = sb("keep", [P, PAIRS])
        carry = sb("carry", [P, 1])
        ones_row = sb("ones_row", [1, P])
        minus_half = sb("minus_half", [P, SUB])
        rev_index = sb("rev_index", [P, SUB, EXPERTS])
        sel16_r = sb("sel16_r", [16, ROUTED], F32R)
        wT = sb("wT", [P, 8, P])
        w8T = sb("w8T", [P, P], BF16)
        rows = sb("rows", [1, 6, P])
        rows_bc = sb("rows_bc", [P, 5, P])
        o_bias4 = sb("o_bias4", [1, SUB, P])
        gate_b = sb("gate_b", [P, 3])
        gate_bh = sb("gate_bh", [P, 2])
        w_router = sb("w_router", [P, EXPERTS])
        w_router_hi = sb("w_router_hi", [P, EXPERTS], F32R)
        w_router_lo = sb("w_router_lo", [P, EXPERTS], F32R)
        w_hi = sb("w_hi", [P, W_COLS], F32R)
        w_lo = sb("w_lo", [P, W_COLS], F32R)
        amax = sb("amax", [P, NT])
        amax1 = sb("amax1", [P, 1])
        amax_all = sb("amax_all", [P, 1])
        x_scale = sb("x_scale", [P, 1])
        inv_scale = sb("inv_scale", [P, 1])
        deq_scale = sb("deq_scale", [P, P])
        x1_all = sb("x1_all", [P, NC + SUB, E])

        first = ctx.enter_context(ExitStack())

        def sb1(name, shape, dt=F32):
            return first.enter_context(nc.sbuf_tensor(name, shape, dt))

        sel16 = sb1("sel16", [16, ROUTED])
        sel16_b = sb1("sel16_b", [16, ROUTED])
        w_nat = sb1("w_nat", [P, 9, P])
        w8_raw = sb1("w8_raw", [P, P, 2], I32)
        w_ff = sb1("w_ff", [P, W_COLS])
        x_cur = [sb1(f"x_cur{p}", [P, SUB, E]) for p in range(2)]
        x_bo = [sb1(f"x_bo{p}", [P, SUB, E]) for p in range(2)]
        repeat4 = sb1("repeat4", [P, 4, 4, 32])
        xT = sb1("xT", [P, TILE])
        exp_q = sb1("exp_q", [P, TILE])
        exp_k = sb1("exp_k", [P, TILE])
        qT = [sb1(f"qT{p}", [P, TILE]) for p in range(2)]
        kT = [sb1(f"kT{p}", [P, TILE]) for p in range(2)]
        k_heads = [sb1(f"k_heads{p}", [P, 4 * SUB, 4, 32]) for p in range(2)]
        k_tok = [sb1(f"k_tok{p}", [P, SUB, P]) for p in range(2)]
        v_tok = [sb1(f"v_tok{p}", [P, SUB, HEADS, DV]) for p in range(2)]
        v_own = [sb1(f"v_own{p}", [P, SUB, 4 * QUADS, 4, DV]) for p in range(2)]
        scores = sb1("scores", [P, QUADS, SPANS])
        state = sb1("state", [P, 2, QUADS, 64])
        numT = sb1("numT", [64 + QV, 2 * CHUNK])
        kv_sum = sb1("kv_sum", [P, HEADS * DV])
        kv_own = sb1("kv_own", [P, HEADS * DV])
        den = sb1("den", [P, HEADS])
        rden = sb1("rden", [P, HEADS])
        attn = sb1("attn", [P, HEADS, D])
        attnT = sb1("attnT", [P, P])
        y_attn = sb1("y_attn", [P, SUB, E])
        a_stats = sb1("a_stats", [P, SUB, 6])
        a_mv = sb1("a_mv", [P, SUB, 2])
        a_var = sb1("a_var", [P, SUB])
        a_rstd = sb1("a_rstd", [P, SUB])

        first.close()

        xq = sb("xq", [P, SUB, E])
        x1_b = sb("x1_b", [P, SUB, E])
        xqT = sb("xqT", [P, TILE], BF16)
        y_ffn = sb("y_ffn", [P, SUB, E])
        stats = [sb(f"stats{n}", [P, SUB, 6]) for n in range(4)]
        mv = [sb(f"mv{n}", [P, SUB, 2]) for n in range(4)]
        var_eps = [sb(f"var_eps{n}", [P, SUB]) for n in range(4)]
        rstd = [sb(f"rstd{n}", [P, SUB]) for n in range(4)]
        x2 = [sb(f"x2_{p}", [P, SUB, E]) for p in range(2)]
        x2T = sb("x2T", [P, TILE])
        tanh_f = sb("tanh_f", [P, TILE])
        tanh_i = sb("tanh_i", [P, TILE])
        tanh_z = sb("tanh_z", [P, TILE])
        tanh_o = [sb(f"tanh_o{p}", [P, SUB, E]) for p in range(2)]
        f_gate = sb("f_gate", [P, TILE])
        iz2 = sb("iz2", [P, TILE])
        cell2 = [sb(f"cell2_{p}", [P, TILE]) for p in range(2)]
        c_norm = sb("c_norm", [P, SUB, E])
        c_aff = sb("c_aff", [P, SUB, E])
        tanh_c = sb("tanh_c", [P, SUB, E])
        h2 = sb("h2", [P, SUB, E])
        y_lstm = sb("y_lstm", [P, SUB, E])

        x3 = [sb(f"x3_{p}", [P, SUB, E]) for p in range(2)]
        x3T_hi = [sb(f"x3T_hi{p}", [P, TILE], F32R) for p in range(2)]
        x3T_lo = [sb(f"x3T_lo{p}", [P, TILE], F32R) for p in range(2)]
        logits = sb("logits", [P, SUB, EXPERTS])
        logits2 = sb("logits2", [P, SUB, EXPERTS])
        top = [sb(f"top{n}", [P, SUB]) for n in range(2)]
        is_top = [sb(f"is_top{n}", [P, SUB, EXPERTS]) for n in range(2)]
        rank = [sb(f"rank{n}", [P, SUB, EXPERTS]) for n in range(2)]
        best = [sb(f"best{n}", [P, SUB]) for n in range(2)]
        pick = [sb(f"pick{n}", [P, SUB, EXPERTS]) for n in range(2)]
        gap = sb("gap", [P, SUB])
        tanh_gap = sb("tanh_gap", [P, SUB])
        pick_sum = sb("pick_sum", [P, SUB, EXPERTS])
        pick_dif = sb("pick_dif", [P, SUB, EXPERTS])
        dif_t = sb("dif_t", [P, SUB, EXPERTS])
        w2x = sb("w2x", [P, SUB, EXPERTS])
        w_tok = sb("w_tok", [P, SUB, EXPERTS])
        w_tok_r = sb("w_tok_r", [P, SUB, EXPERTS], F32R)
        w_parts = sb("w_parts", [P, SUB, 2, EXPERTS])
        w_partsT = [sb(f"w_partsT{p}", [16, TILE], F32R) for p in range(2)]
        silu_g = [sb(f"silu_g{n}", [P, TILE]) for n in range(2)]
        gu = [sb(f"gu{n}", [P, TILE]) for n in range(2)]
        hid = [sb(f"hid{n}", [P, TILE]) for n in range(2)]
        hid_hi = [sb(f"hid_hi{n}", [P, TILE], F32R) for n in range(4)]
        hid_lo = [sb(f"hid_lo{n}", [P, TILE], F32R) for n in range(4)]
        yT = sb("yT", [P, TILE])
        y_moe = sb("y_moe", [P, SUB, E])
        x4 = sb("x4", [P, SUB, E])

        pb = [bank(f"bank{n}", [P, 512]) for n in range(8)]
        ps_scores = pb[0:4]
        ps_tr = pb[4]
        ps_proj = pb[5]
        ps_numT = pb[6][:, 0:2 * CHUNK]
        ps_kv = pb[3][:, SPANS:SPANS + HEADS * DV]
        ps_num = pb[7][:, 0:4 * 64]
        ps_attnT = pb[7][:, 256:256 + P]
        ps_wo = pb[7][:, 384:384 + P]
        ps_g = pb[0:2]
        ps_u = pb[2:4]
        ps_w = pb[4]
        ps_y = pb[5]
        ps_a = pb[6]
        ps_b = pb[7]

        s = {n: sem(n) for n in (
            "wl_square wl_int8 wl_rows wl_cols wl_router wl_ff x_loaded out_stored "
            "z_set consts_ready one_set v_ones state_zero ff_pad_zero "
            "w_tr w_tr_copied w8_cast w8T_ready rows_bc_ps rows_bc_ready o_bias_ready gate_bh_ready "
            "quad_ready router_hi router_ready sel_r_ready ff_hi ff_split "
            "xT_ps xT_ready q_ps expq_ready expq_min q_ready k_ps expk_ready expk_min k_ready v_ps v_ready "
            "ktok_ps ktok_ready kheads_v kheads_p vown_ready vown_ps vown_set num_turned numT_ready span_set xbo_ready "
            "score_ps masked kv_ps kv_own_ready state_ready state_kept attn_num_ps den_ready rden_ready attn_ready "
            "attnT_ps attnT_ready wo_ps yattn_ready astats_ready amv_ready avar_ready arstd_ready x1_ready amax_ready "
            "amax1_ready amax_all_ready scale_ready deq_ready "
            "xq_round xq_ready x1b_ready xqT_ps xqT_ready q8_ps deq_done yffn_ready "
            "x2T_ps x2T_ready f_ps tf_ready i_ps ti_ready z_ps tz_ready o_ps to_ready "
            "f_ready iz_ready cell_ready carry_ready cellT_ps cscaled caff_ready tc_ready h2_ready "
            "ylstm_ready x3T_ps x3hi_ready x3lo_ready logit_ps gap_ready tgap_ready "
            "wT_ps wT_ready "
            "g_ps u_ps w_ps silu_ready gu_ready hid_ready hi_ready lo_ready down_ps "
            "yT_ready y_ps ymoe_ready x4_ready route_step").split()}
        norms = ("ffn", "cell", "lstm", "moe")
        st_r = [sem(f"{n}_stats_ready") for n in norms]
        mv_r = [sem(f"{n}_meanvar_ready") for n in norms]
        ve_r = [sem(f"{n}_vareps_ready") for n in norms]
        rs_r = [sem(f"{n}_rstd_ready") for n in norms]
        nm_r = [sem(f"{n}_normed") for n in norms[:3]] + [s["x4_ready"]]

        block = ctx.enter_context(nc.Block())

        def settled(eng):
            eng.nop(nofuse=True)


        @block.sync
        def _(sp):
            def load_x(t, p, first=False):
                if not first:
                    sp.wait_ge(s["x_loaded"], 16 * t)
                    settled(sp)
                    sp.wait_ge(s["xT_ps"], t - 1)
                    settled(sp)
                    sp.wait_ge(s["xbo_ready"], t - 1)
                    settled(sp)
                sp.dma_start(x_cur[p][:], x_tiles[bass.ds(t, 1)].rearrange("o p s e -> (o p) s e")
                             if not isinstance(t, int) else x_tiles[t]).then_inc(s["x_loaded"], 16)

            load_x(0, 0, first=True)
            for n, w in enumerate((Wq, Wk, Wv, Wo)):
                sp.dma_start(w_nat[:, n, :], w).then_inc(s["wl_square"], 16)
            sp.wait_ge(s["x_loaded"], 16)
            load_x(1, 1, first=True)
            sp.dma_start(w_nat[:, 4:8, :], Wgates.rearrange("(g p) d -> p g d", p=P)).then_inc(s["wl_square"], 16)
            sp.dma_start(w8_raw[:].rearrange("p k w -> p (k w)"), W8.bitcast(I32)).then_inc(s["wl_int8"], 16)
            sp.dma_start(w_router[:], Wrouter).then_inc(s["wl_router"], 16)
            with sp.Fori(1, PAIRS) as i:
                load_x(2 * i, 0)
                load_x(2 * i + 1, 1)

            def store(t):
                sp.wait_ge(s["x4_ready"], SUB * (t + 1))
                settled(sp)
                sp.dma_start(out_tiles[bass.ds(t, 1)].rearrange("o p s e -> (o p) s e"), x4[:])\
                  .then_inc(s["out_stored"], 16)

            with sp.Fori(0, NT) as t:
                store(t)
            sp.wait_ge(s["out_stored"], 16 * NT)

        @block.scalar
        def _(act):
            for n, r in enumerate((bo, ffn_bias, None, ln_w, ln_b, gate_bias[2 * P:3 * P])):
                src = w8_scale.rearrange("n o -> o n") if r is None else r.rearrange("(o n) -> o n", o=1)
                act.dma_start(rows[:, n, :], src).then_inc(s["wl_rows"], 16)
            gb = gate_bias.rearrange("(g p o) -> g p o", p=P, o=1)
            for n, g in enumerate((0, 1, 3)):
                act.dma_start(gate_b[:, n:n + 1], gb[g]).then_inc(s["wl_cols"], 16)
            col = 0
            for routed, shared in ((W1, Ws1), (W2, Ws2)):
                act.dma_start(w_ff[:, col:col + ROUTED].rearrange("c (e h) -> c e h", e=EXPERTS),
                              routed.rearrange("e c h -> c e h")).then_inc(s["wl_ff"], 16)
                act.dma_start(w_ff[:, col + ROUTED:col + HALL], shared).then_inc(s["wl_ff"], 16)
                col += HALL
            act.dma_start(w_ff[:, col:col + NJR * P].rearrange("p (j c) -> p j c", j=NJR),
                          W3.rearrange("e h c -> (e h) c").rearrange("(j p) c -> p j c", p=P)).then_inc(s["wl_ff"], 16)
            act.dma_start(w_ff[:, col + NJR * P:col + (NJ - 1) * P].rearrange("p (j c) -> p j c", j=NJ - 1 - NJR),
                          Ws3[0:(NJ - 1 - NJR) * P, :].rearrange("(j p) c -> p j c", p=P)).then_inc(s["wl_ff"], 16)
            act.wait_ge(s["ff_pad_zero"], 1)
            act.dma_start(w_ff[0:LASTK, col + (NJ - 1) * P:col + NJ * P],
                          Ws3[(NJ - 1 - NJR) * P:HSH, :]).then_inc(s["wl_ff"], 16)

            for b in range(2):
                act.wait_ge(s["w_tr"], b + 1)
                nc.scalar.activation(wT[:, 4 * b:4 * b + 4, :], ps_scores[b][:].rearrange("p (n c) -> p n c", n=4),
                                     ACT.Copy).then_inc(s["w_tr_copied"], 1)
            act.wait_ge(s["w_tr"], 3)
            nc.scalar.activation(w8T[:], ps_scores[2][:, 0:P], ACT.Copy).then_inc(s["w8T_ready"], 1)
            for b, (lo, hi) in enumerate(((0, 4), (4, 5))):
                act.wait_ge(s["rows_bc_ps"], b + 1)
                nc.scalar.activation(rows_bc[:, lo:hi, :],
                                     (ps_scores[3], ps_tr)[b][:, 0:(hi - lo) * P].rearrange("p (n c) -> p n c", c=P),
                                     ACT.Copy).then_inc(s["rows_bc_ready"], 1)

            def front(t, p, part):
                late = not (isinstance(t, int) and t == 0)
                if part == 0:
                    act.wait_ge(s["xT_ps"], t + 1)
                    act.wait_ge(s["k_ps"], t)
                    nc.scalar.activation(xT[:], ps_tr[:], ACT.Copy).then_inc(s["xT_ready"], 1)
                    act.wait_ge(s["v_ps"], t + 1)
                    if late:
                        act.wait_ge(s["kv_ps"], SUB * (t - 1))
                        act.wait_ge(s["vown_ps"], SUB * (t - 1))
                    act.wait_ge(s["v_ones"], 2)
                    nc.scalar.activation(v_tok[p][:].rearrange("p s h d -> p (s h) d")[:, :, 0:D],
                                         ps_proj[:].rearrange("p (n d) -> p n d", d=D), ACT.Copy)\
                      .then_inc(s["v_ready"], 1)
                    act.wait_ge(s["q_ps"], t + 1)
                    act.wait_ge(s["q_ready"], t)
                    nc.scalar.activation(exp_q[:], ps_proj[:], ACT.Exp).then_inc(s["expq_ready"], 1)
                elif part == 1:
                    act.wait_ge(s["k_ps"], t + 1)
                    act.wait_ge(s["k_ready"], t)
                    nc.scalar.activation(exp_k[:], ps_proj[:], ACT.Exp).then_inc(s["expk_ready"], 1)
                elif part == 2:
                    act.wait_ge(s["ktok_ps"], t + 1)
                    if late:
                        act.wait_ge(s["kv_ps"], SUB * (t - 1))
                    nc.scalar.activation(k_tok[p][:].rearrange("p s d -> p (s d)"), ps_proj[:], ACT.Copy)\
                      .then_inc(s["ktok_ready"], 1)

            def own_values(t, p, n):
                act.wait_ge(s["vown_ps"], SUB * t + n + 1)
                if not (isinstance(t, int) and t == 0):
                    act.wait_ge(s["attn_num_ps"], 4 * SUB * (t - 1))
                act.wait_ge(s["vown_set"], 10)
                for r in range(4):
                    rows32 = slice(32 * r, 32 * r + 32)
                    nc.scalar.activation(v_own[p][rows32, n, :, r, 0:D],
                                         ps_tr[rows32].rearrange("p (n r d) -> p n r d", r=4, d=D)[:, :, r, :],
                                         ACT.Copy).then_inc(s["vown_ready"], 1)

            def chunk_turned(c):
                act.wait_ge(s["attnT_ps"], c + 1)
                act.wait_ge(s["wo_ps"], c)
                nc.scalar.activation(attnT[:], ps_attnT, ACT.Copy).then_inc(s["attnT_ready"], 1)

            def chunk_sums(c):
                act.wait_ge(s["attn_num_ps"], 4 * c + 4)
                act.wait_ge(s["num_turned"], c)
                nc.scalar.activation(numT[:], ps_numT[0:64 + QV], ACT.Copy).then_inc(s["numT_ready"], 1)

            def attn_tile(t, p, last=False):
                for n in range(SUB):
                    c = SUB * t + n
                    if not (isinstance(c, int) and c == 0):
                        chunk_turned(c - 1)
                    chunk_sums(c)
                    if not last:
                        front(t + 1, 1 - p, n)
                        own_values(t + 1, 1 - p, n)

            for part in range(3):
                front(0, 0, part)
                own_values(0, 0, part)
            front(0, 0, 3)
            own_values(0, 0, 3)
            attn_tile(0, 0)
            attn_tile(1, 1)
            with act.Fori(1, PAIRS - 1) as i:
                attn_tile(2 * i, 0)
                attn_tile(2 * i + 1, 1)
            attn_tile(NT - 2, 0)
            attn_tile(NT - 1, 1, last=True)
            chunk_turned(NC - 1)

            def recur(t, p, slot):
                if slot == 0:
                    act.wait_ge(s["xqT_ps"], t + 1)
                    act.wait_ge(s["q8_ps"], t)
                    nc.scalar.activation(xqT[:], ps_a[:], ACT.Copy, bias=-MAGIC).then_inc(s["xqT_ready"], 1)
                elif slot == 5:
                    act.wait_ge(s["x2T_ps"], t + 1)
                    act.wait_ge(s["o_ps"], t)
                    nc.scalar.activation(x2T[:], ps_a[:], ACT.Copy).then_inc(s["x2T_ready"], 1)
                elif slot == 7:
                    act.wait_ge(s["f_ps"], t + 1)
                    act.wait_ge(s["f_ready"], t)
                    nc.scalar.activation(tanh_f[:], ps_a[:], ACT.Tanh, bias=gate_bh[:, 0:1], scale=0.5)\
                      .then_inc(s["tf_ready"], 1)
                elif slot == 8:
                    act.wait_ge(s["i_ps"], t + 1)
                    act.wait_ge(s["iz_ready"], t)
                    nc.scalar.activation(tanh_i[:], ps_a[:], ACT.Tanh, bias=gate_bh[:, 1:2], scale=0.5)\
                      .then_inc(s["ti_ready"], 1)
                elif slot == 9:
                    act.wait_ge(s["z_ps"], t + 1)
                    nc.scalar.activation(tanh_z[:], ps_a[:], ACT.Tanh, bias=gate_b[:, 2:3])\
                      .then_inc(s["tz_ready"], 1)
                elif slot == 10:
                    act.wait_ge(s["o_ps"], t + 1)
                    if not (isinstance(t, int) and t < 2):
                        act.wait_ge(s["h2_ready"], t - 1)
                    nc.scalar.activation(tanh_o[p][:].rearrange("p s e -> p (s e)"), ps_a[:], ACT.Tanh, scale=0.5)\
                      .then_inc(s["to_ready"], 1)

            def emit(t, p, slot):
                if slot == 3:
                    act.wait_ge(s["caff_ready"], t + 1)
                    act.wait_ge(s["h2_ready"], t)
                    nc.scalar.activation(tanh_c[:], c_aff[:], ACT.Tanh).then_inc(s["tc_ready"], 1)
                elif slot == 6:
                    act.wait_ge(s["x3T_ps"], t + 1)
                    if not (isinstance(t, int) and t < 2):
                        act.wait_ge(s["u_ps"], NJ * (t - 1))
                    nc.scalar.activation(x3T_hi[p][:], ps_b[:], ACT.Copy).then_inc(s["x3hi_ready"], 1)
                elif slot == 9:
                    act.wait_ge(s["gap_ready"], t + 1)
                    act.wait_ge(s["route_step"], ROUTE * t)
                    nc.scalar.activation(tanh_gap[:], gap[:], ACT.Tanh, scale=0.5).then_inc(s["tgap_ready"], 1)
                elif slot == 10:
                    act.wait_ge(s["wT_ps"], t + 1)
                    if not (isinstance(t, int) and t < 2):
                        act.wait_ge(s["w_ps"], NJR * (t - 1))
                    nc.scalar.activation(w_partsT[p][:], ps_b[0:16, :], ACT.Copy).then_inc(s["wT_ready"], 1)

            def block_silu(t, p, j):
                n = NJ * t + j
                m = P if j < NJ - 1 else LASTK
                act.wait_ge(s["g_ps"], n + 1)
                if not (isinstance(n, int) and n < 2):
                    act.wait_ge(s["hid_ready"], n - 1)
                nc.scalar.activation(silu_g[j % 2][0:m], ps_g[j % 2][0:m], ACT.Silu).then_inc(s["silu_ready"], 1)

            def block_high(t, p, j):
                n = NJ * t + j
                b = (NJ * p + j) % 4
                m = P if j < NJ - 1 else LASTK
                act.wait_ge(s["hid_ready"], n + 1)
                if not (isinstance(n, int) and n < 4):
                    act.wait_ge(s["down_ps"], n - 3)
                    act.wait_ge(s["lo_ready"], n - 3)
                nc.scalar.activation(hid_hi[b][0:m], hid[j % 2][0:m], ACT.Copy).then_inc(s["hi_ready"], 1)

            def finish(t):
                act.wait_ge(s["down_ps"], NJ * (t + 1))
                act.wait_ge(s["y_ps"], t)
                nc.scalar.activation(yT[:], ps_y[:], ACT.Copy).then_inc(s["yT_ready"], 1)

            def moe_tile(t, p, last=False):
                for j in range(NJ):
                    if j == 0 and not (isinstance(t, int) and t == 0):
                        finish(t - 1)
                    ahead = j + AHEAD
                    if ahead < NJ:
                        block_silu(t, p, ahead)
                        block_high(t, p, ahead - 1)
                    elif not last:
                        block_silu(t + 1, 1 - p, ahead - NJ)
                        if ahead == NJ:
                            block_high(t, p, NJ - 1)
                        else:
                            block_high(t + 1, 1 - p, ahead - NJ - 1)
                    elif ahead == NJ:
                        block_high(t, p, NJ - 1)
                    if not last:
                        recur(t + 2, p, j)
                        emit(t + 1, 1 - p, j)

            act.wait_ge(s["gate_bh_ready"], 1)
            for slot in range(NJ):
                recur(0, 0, slot)
            for slot in range(NJ):
                recur(1, 1, slot)
                emit(0, 0, slot)
            for j in range(AHEAD):
                block_silu(0, 0, j)
                if j:
                    block_high(0, 0, j - 1)
            moe_tile(0, 0)
            moe_tile(1, 1)
            with act.Fori(1, PAIRS - 1) as i:
                moe_tile(2 * i, 0)
                moe_tile(2 * i + 1, 1)
            moe_tile(NT - 2, 0)
            moe_tile(NT - 1, 1, last=True)
            finish(NT - 1)

        @block.gpsimd
        def _(pool):
            nc.gpsimd.memset(ident[:], 0.0).then_inc(s["z_set"], 1)
            nc.gpsimd.memset(causal[:], 1.0).then_inc(s["z_set"], 1)
            nc.gpsimd.memset(head_of[:], 1.0).then_inc(s["z_set"], 1)
            pool.wait_ge(s["z_set"], 3)
            nc.gpsimd.affine_select(out=ident[:], in_=ident[:], compare_op=ALU.not_equal, fill=1.0, base=0,
                                    pattern=[[-1, P]], channel_multiplier=1).then_inc(s["one_set"], 1)
            nc.gpsimd.memset(x1_all[:, NC:NC + SUB, :], 0.0).then_inc(s["one_set"], 1)
            nc.gpsimd.affine_select(out=head_of_2[:], in_=head_of[:], compare_op=ALU.is_ge, fill=0.0, base=0,
                                    pattern=[[-4 * D, QUADS], [-D, 4]], channel_multiplier=1).then_inc(s["one_set"], 1)
            pool.wait_ge(s["one_set"], 3)
            nc.gpsimd.affine_select(out=head_of[:], in_=head_of_2[:], compare_op=ALU.is_ge, fill=0.0, base=D - 1,
                                    pattern=[[4 * D, QUADS], [D, 4]], channel_multiplier=-1).then_inc(s["one_set"], 1)
            nc.gpsimd.memset(ones_row[:], 1.0).then_inc(s["one_set"], 1)
            pool.wait_ge(s["one_set"], 5)
            nc.gpsimd.memset(minus_half[:], -0.5).then_inc(s["consts_ready"], 1)
            pool.wait_ge(s["consts_ready"], 1)
            nc.gpsimd.memset(w_ff[96:P, W_COLS - P:W_COLS], 0.0).then_inc(s["ff_pad_zero"], 1)
            pool.wait_ge(s["ff_pad_zero"], 1)
            for r in range(4):
                for b in range(4):
                    part = causal[32 * r:32 * r + 32, SPAN_AT[b]:SPAN_AT[b] + SPAN[b]]
                    nc.gpsimd.affine_select(out=part, in_=part, compare_op=ALU.is_ge, fill=0.0, base=0,
                                            pattern=[[1, SPAN[b]]], channel_multiplier=-1).then_inc(s["span_set"], 1)
                    pool.wait_ge(s["span_set"], 4 * r + b + 1)
            for p in range(2):
                nc.gpsimd.memset(v_own[p][:], 0.0).then_inc(s["vown_set"], 1)
            pool.wait_ge(s["vown_set"], 2)
            for p in range(2):
                for r in range(4):
                    nc.gpsimd.memset(v_own[p][32 * r:32 * r + 32, :, :, r, D:DV], 1.0).then_inc(s["vown_set"], 1)
                    pool.wait_ge(s["vown_set"], 3 + 4 * p + r)
            for p in range(2):
                nc.gpsimd.memset(v_tok[p][:], 1.0).then_inc(s["v_ones"], 1)
            nc.gpsimd.memset(state[:], 0.0).then_inc(s["state_zero"], 1)
            nc.gpsimd.memset(carry[:], 0.0).then_inc(s["state_zero"], 1)
            nc.gpsimd.memset(keep[:], 1.0).then_inc(s["state_zero"], 1)
            pool.wait_ge(s["state_zero"], 3)
            nc.gpsimd.memset(keep[:, TPB // 2 - 1:TPB // 2], 0.0).then_inc(s["state_zero"], 1)
            pool.wait_ge(s["rows_bc_ready"], 1)

            def keep_residual(t, p):
                pool.wait_ge(s["x_loaded"], 16 * (t + 1))
                if not (isinstance(t, int) and t == 0):
                    pool.wait_ge(s["yattn_ready"], SUB * (t - 1))
                settled(pool)
                nc.gpsimd.tensor_tensor(x_bo[p][:], x_cur[p][:],
                                        rows_bc[:, 0:1, :].to_broadcast([P, SUB, E]), ALU.add)\
                  .then_inc(s["xbo_ready"], 1)

            def split_heads(t, p):
                pool.wait_ge(s["k_ready"], t + 1)
                if not (isinstance(t, int) and t == 0):
                    pool.wait_ge(s["score_ps"], 4 * SUB * (t - 1))
                settled(pool)
                for r in (2, 3):
                    nc.gpsimd.tensor_scalar(k_heads[p][:, :, r, :], kT[p][:].rearrange("p (q j) -> p q j", j=32), in_quad[:, r:r + 1], 1.0, ALU.mult, ALU.mult)\
                      .then_inc(s["kheads_p"], 1)

            def attn_rstd(t):
                pool.wait_ge(s["amv_ready"], SUB * (t + 1))
                pool.wait_ge(s["x1_ready"], SUB * t)
                settled(pool)
                nc.gpsimd.tensor_scalar(a_var[:], a_mv[:, :, 1], LN_EPS, 1.0, ALU.add, ALU.mult)\
                  .then_inc(s["avar_ready"], 1)
                pool.wait_ge(s["avar_ready"], t + 1)
                settled(pool)
                nc.gpsimd.tensor_tensor(a_rstd[:], a_var[:], minus_half[:], ALU.pow).then_inc(s["arstd_ready"], 1)

            def split_weights(t):
                cols = bass.ds(t * WSLICE, WSLICE)
                nc.gpsimd.tensor_copy(w_hi[:, cols], w_ff[:, cols]).then_inc(s["ff_hi"], 1)
                pool.wait_ge(s["ff_hi"], t + 1)
                settled(pool)
                nc.gpsimd.tensor_tensor(w_lo[:, cols], w_ff[:, cols], w_hi[:, cols].bitcast(F32), ALU.subtract)\
                  .then_inc(s["ff_split"], 1)

            keep_residual(0, 0)
            pool.wait_ge(s["quad_ready"], 1)
            split_heads(0, 0)
            for n, (dst, e0) in enumerate(((sel16, 0), (sel16_b, EXPERTS))):
                nc.gpsimd.memset(dst[:], 1.0).then_inc(s["sel_r_ready"], 1)
                pool.wait_ge(s["sel_r_ready"], 3 * n + 1)
                nc.gpsimd.affine_select(out=dst[:], in_=dst[:], compare_op=ALU.is_ge, fill=0.0, base=HID * e0,
                                        pattern=[[1, ROUTED]], channel_multiplier=-HID).then_inc(s["sel_r_ready"], 1)
                pool.wait_ge(s["sel_r_ready"], 3 * n + 2)
                nc.gpsimd.affine_select(out=dst[:], in_=dst[:], compare_op=ALU.is_ge, fill=0.0, base=HID - 1 - HID * e0,
                                        pattern=[[-1, ROUTED]], channel_multiplier=HID).then_inc(s["sel_r_ready"], 1)
                pool.wait_ge(s["sel_r_ready"], 3 * n + 3)
            nc.gpsimd.tensor_tensor(sel16_r[:], sel16[:], sel16_b[:], ALU.add).then_inc(s["sel_r_ready"], 1)
            nc.gpsimd.iota(rev_index[:], pattern=[[0, SUB], [-1, EXPERTS]], base=EXPERTS, channel_multiplier=0,
                           allow_small_or_imprecise_dtypes=True).then_inc(s["sel_r_ready"], 1)
            pool.wait_ge(s["wl_router"], 16)
            nc.gpsimd.tensor_copy(w_router_hi[:], w_router[:]).then_inc(s["router_hi"], 1)
            pool.wait_ge(s["router_hi"], 1)
            nc.gpsimd.tensor_tensor(w_router_lo[:], w_router[:], w_router_hi[:].bitcast(F32), ALU.subtract)\
              .then_inc(s["router_ready"], 1)
            pool.wait_ge(s["wl_ff"], 16 * 7)

            def attn_tile(t, p, last=False):
                if not (isinstance(t, int) and t == 0):
                    attn_rstd(t - 1)
                if not last:
                    split_heads(t + 1, 1 - p)
                    keep_residual(t + 1, 1 - p)
                split_weights(t)

            attn_tile(0, 0)
            attn_tile(1, 1)
            with pool.Fori(1, PAIRS - 1) as i:
                attn_tile(2 * i, 0)
                attn_tile(2 * i + 1, 1)
            attn_tile(NT - 2, 0)
            attn_tile(NT - 1, 1, last=True)
            attn_rstd(NT - 1)

            pool.wait_ge(s["amax1_ready"], 1)
            nc.gpsimd.partition_all_reduce(amax_all[:], amax1[:], P, bass.bass_isa.ReduceOp.max)\
              .then_inc(s["amax_all_ready"], 1)

            def norm_std(k, t, eps, ready, vareps, rs, used=None):
                pool.wait_ge(ready, SUB * (t + 1))
                if used is not None:
                    pool.wait_ge(used, SUB * t)
                settled(pool)
                nc.gpsimd.tensor_scalar(var_eps[k][:], mv[k][:, :, 1], eps, 1.0, ALU.add, ALU.mult)\
                  .then_inc(vareps, 1)
                pool.wait_ge(vareps, t + 1)
                settled(pool)
                nc.gpsimd.tensor_tensor(rstd[k][:], var_eps[k][:], minus_half[:], ALU.pow).then_inc(rs, 1)

            def recur(t, p, slot):
                if slot == 0:
                    pool.wait_ge(s["yffn_ready"], t)
                    settled(pool)
                    nc.gpsimd.tensor_tensor(x1_b[:], x1_all[:, bass.ds(SUB * t, SUB), :],
                                            rows_bc[:, 1:2, :].to_broadcast([P, SUB, E]), ALU.add)\
                      .then_inc(s["x1b_ready"], 1)
                elif slot == 2:
                    norm_std(0, t, LN_EPS, mv_r[0], ve_r[0], rs_r[0], nm_r[0])
                elif slot == 7:
                    pool.wait_ge(s["tf_ready"], t + 1)
                    pool.wait_ge(s["cell_ready"], t)
                    settled(pool)
                    nc.gpsimd.tensor_scalar(f_gate[:], tanh_f[:], 1.0, 0.5, ALU.add, ALU.mult)\
                      .then_inc(s["f_ready"], 1)

            def emit(t, p, slot):
                if slot == 1:
                    norm_std(1, t, 4 * LN_EPS, mv_r[1], ve_r[1], rs_r[1], nm_r[1])
                elif slot == 2:
                    pool.wait_ge(nm_r[1], SUB * (t + 1))
                    settled(pool)
                    nc.gpsimd.tensor_tensor(c_norm[:], c_norm[:], rows_bc[:, 3:4, :].to_broadcast([P, SUB, E]), ALU.mult)\
                      .then_inc(s["cscaled"], 1)
                    pool.wait_ge(s["cscaled"], t + 1)
                    pool.wait_ge(s["tc_ready"], t)
                    settled(pool)
                    nc.gpsimd.tensor_tensor(c_aff[:], c_norm[:], rows_bc[:, 4:5, :].to_broadcast([P, SUB, E]), ALU.add)\
                      .then_inc(s["caff_ready"], 1)
                elif slot == 4:
                    norm_std(2, t, LN_EPS, mv_r[2], ve_r[2], rs_r[2], nm_r[2])

            def block_low(t, p, j):
                n = NJ * t + j
                b = (NJ * p + j) % 4
                m = P if j < NJ - 1 else LASTK
                pool.wait_ge(s["hi_ready"], n + 1)
                if not (isinstance(n, int) and n < 4):
                    pool.wait_ge(s["down_ps"], n - 3)
                settled(pool)
                nc.gpsimd.tensor_tensor(hid_lo[b][0:m], hid[j % 2][0:m], hid_hi[b][0:m].bitcast(F32), ALU.subtract)\
                  .then_inc(s["lo_ready"], 1)

            def moe_tile(t, p, last=False):
                for j in range(NJ):
                    if j == 0 and not (isinstance(t, int) and t == 0):
                        norm_std(3, t - 1, LN_EPS, mv_r[3], ve_r[3], rs_r[3], nm_r[3])
                    ahead = j + AHEAD
                    if ahead <= NJ:
                        block_low(t, p, ahead - 1)
                    elif not last:
                        block_low(t + 1, 1 - p, ahead - NJ - 1)
                    if not last:
                        recur(t + 2, p, j)
                        emit(t + 1, 1 - p, j)

            for slot in range(NJ):
                recur(0, 0, slot)
            for slot in range(NJ):
                recur(1, 1, slot)
                emit(0, 0, slot)
            for j in range(AHEAD - 1):
                block_low(0, 0, j)
            moe_tile(0, 0)
            moe_tile(1, 1)
            with pool.Fori(1, PAIRS - 1) as i:
                moe_tile(2 * i, 0)
                moe_tile(2 * i + 1, 1)
            moe_tile(NT - 2, 0)
            moe_tile(NT - 1, 1, last=True)
            norm_std(3, NT - 1, LN_EPS, mv_r[3], ve_r[3], rs_r[3], nm_r[3])

        @block.vector
        def _(dve):
            dve.wait_ge(s["consts_ready"], 1)
            nc.vector.tensor_reduce(in_quad[:], head_of[:].rearrange("p g r -> p r g"), AX.X, ALU.add)\
              .then_inc(s["quad_ready"], 1)
            nc.vector.tensor_copy(repeat4[:], ident[:].rearrange("p (b j) -> p b j", j=32).unsqueeze(2)
                                  .to_broadcast([P, 4, 4, 32])).then_inc(s["quad_ready"], 1)
            dve.wait_ge(s["wl_int8"], 16)
            nc.vector.tensor_copy(w_nat[:, 8, :], w8_raw[:, :, 0]).then_inc(s["w8_cast"], 1)
            dve.wait_ge(s["wl_rows"], 16 * 6)
            nc.vector.tensor_copy(o_bias4[:], rows[:, 5:6, :].to_broadcast([1, SUB, P])).then_inc(s["o_bias_ready"], 1)
            dve.wait_ge(s["wl_cols"], 16 * 3)
            nc.vector.tensor_scalar(gate_bh[:], gate_b[:, 0:2], 0.5, None, ALU.mult).then_inc(s["gate_bh_ready"], 1)
            dve.wait_ge(s["state_zero"], 4)
            dve.wait_ge(s["quad_ready"], 1)

            own_head = head_of[:].rearrange("p g r -> p (g r)").unsqueeze(2).to_broadcast([P, HEADS, DV])

            def front_q(t, p):
                dve.wait_ge(s["expq_ready"], t + 1)
                nc.vector.tensor_scalar(exp_q[:], exp_q[:], 1.0, None, ALU.min).then_inc(s["expq_min"], 1)
                dve.wait_ge(s["expq_min"], t + 1)
                if not (isinstance(t, int) and t == 0):
                    dve.wait_ge(s["attn_num_ps"], 4 * SUB * (t - 1))
                nc.vector.scalar_tensor_tensor(qT[p][:], ps_proj[:], 0.0, exp_q[:], ALU.max, ALU.add)\
                  .then_inc(s["q_ready"], 1)

            def front_heads(t, p):
                dve.wait_ge(s["k_ready"], t + 1)
                for r in (0, 1):
                    nc.vector.tensor_scalar(k_heads[p][:, :, r, :], kT[p][:].rearrange("p (q j) -> p q j", j=32), in_quad[:, r:r + 1], None, ALU.mult)\
                      .then_inc(s["kheads_v"], 1)

            def front_k(t, p):
                dve.wait_ge(s["expk_ready"], t + 1)
                nc.vector.tensor_scalar(exp_k[:], exp_k[:], 1.0, None, ALU.min).then_inc(s["expk_min"], 1)
                dve.wait_ge(s["expk_min"], t + 1)
                if not (isinstance(t, int) and t == 0):
                    dve.wait_ge(s["score_ps"], 4 * SUB * (t - 1))
                    dve.wait_ge(s["kheads_p"], 2 * (t - 1))
                    dve.wait_ge(s["ktok_ps"], t - 1)
                nc.vector.scalar_tensor_tensor(kT[p][:], ps_proj[:], 0.0, exp_k[:], ALU.max, ALU.add)\
                  .then_inc(s["k_ready"], 1)

            def mask(c, g):
                dve.wait_ge(s["score_ps"], 4 * c + g + 1)
                if not (isinstance(c, int) and c == 0):
                    dve.wait_ge(s["attn_num_ps"], 4 * (c - 1) + g + 1)
                nc.vector.tensor_tensor(scores[:, g, :], ps_scores[g][:, 0:SPANS], causal[:], ALU.mult)\
                  .then_inc(s["masked"], 1)

            def state_of(par):
                return state[:, par, :, 0:QV]

            def quads(a):
                return a[:].rearrange("p (g d) -> p g d", g=QUADS)

            def update_state(c, par, ends_row=None):
                dve.wait_ge(s["kv_ps"], c + 1)
                dve.wait_ge(s["score_ps"], 4 * c + 4)
                dve.wait_ge(s["state_ready"], c)
                nc.vector.tensor_tensor(kv_own[:].rearrange("p (h d) -> p h d", h=HEADS),
                                        ps_kv.rearrange("p (h d) -> p h d", h=HEADS), own_head, ALU.mult)\
                  .then_inc(s["kv_own_ready"], 1)
                dve.wait_ge(s["kv_own_ready"], c + 1)
                if ends_row is None:
                    nc.vector.tensor_tensor(state_of(1 - par), state_of(par), quads(kv_own), ALU.add)\
                      .then_inc(s["state_ready"], 1)
                else:
                    nc.vector.tensor_tensor(quads(kv_sum), state_of(par), quads(kv_own), ALU.add)\
                      .then_inc(s["state_kept"], 1)
                    dve.wait_ge(s["state_kept"], ends_row + 1)
                    settled(dve)
                    nc.vector.tensor_scalar(state_of(1 - par), quads(kv_sum), keep[:, bass.ds(ends_row, 1)], None,
                                            ALU.mult).then_inc(s["state_ready"], 1)

            def normalise(c):
                num = ps_num.rearrange("p (g d) -> p g d", g=QUADS)[:, :, 0:QV].rearrange("p g (r d) -> p g r d", r=4)
                by_quad = lambda a: a[:].rearrange("p (g r) -> p g r", g=QUADS)
                dve.wait_ge(s["num_turned"], c + 1)
                dve.wait_ge(s["rden_ready"], c)
                nc.vector.tensor_scalar(by_quad(den), num[:, :, :, D], DEN_EPS, None, ALU.add)\
                  .then_inc(s["den_ready"], 1)
                dve.wait_ge(s["den_ready"], c + 1)
                dve.wait_ge(s["attn_ready"], c)
                nc.vector.reciprocal(rden[:], den[:]).then_inc(s["rden_ready"], 1)
                dve.wait_ge(s["rden_ready"], c + 1)
                dve.wait_ge(s["attnT_ps"], c)
                nc.vector.tensor_tensor(attn[:].rearrange("p (g r) d -> p g r d", g=QUADS), num[:, :, :, 0:D],
                                        by_quad(rden).unsqueeze(3).to_broadcast([P, QUADS, 4, D]), ALU.mult).then_inc(s["attn_ready"], 1)

            def residual(t, p, n):
                c = SUB * t + n
                dve.wait_ge(s["wo_ps"], c + 1)
                dve.wait_ge(s["xbo_ready"], t + 1)
                dve.wait_ge(s["x1_ready"], SUB * t)
                nc.vector.tensor_tensor(y_attn[:, n, :], ps_wo, x_bo[p][:, n, :], ALU.add)\
                  .then_inc(s["yattn_ready"], 1)
                dve.wait_ge(s["yattn_ready"], c + 1)
                dve.wait_ge(s["amv_ready"], SUB * t)
                nc.vector.bn_stats(a_stats[:, n, :], y_attn[:, n, :]).then_inc(s["astats_ready"], 1)

            def attn_norm(t):
                for n in range(SUB):
                    dve.wait_ge(s["astats_ready"], SUB * t + n + 1)
                    dve.wait_ge(s["avar_ready"], t)
                    settled(dve)
                    nc.vector.bn_aggr(a_mv[:, n, :], a_stats[:, n, :]).then_inc(s["amv_ready"], 1)
                dve.wait_ge(s["arstd_ready"], t + 1)
                settled(dve)
                for n in range(SUB):
                    nc.vector.tensor_scalar(x1_all[:, bass.ds(SUB * t + n, 1), :],
                                            y_attn[:, n:n + 1, :], a_mv[:, n, 0:1],
                                            a_rstd[:, n:n + 1], ALU.subtract, ALU.mult).then_inc(s["x1_ready"], 1)
                dve.wait_ge(s["x1_ready"], SUB * (t + 1))
                settled(dve)
                nc.vector.tensor_reduce(amax[:, bass.ds(t, 1)], x1_all[:, bass.ds(SUB * t, SUB), :]
                                        .rearrange("p s e -> p (s e)"), AX.X, ALU.max,
                                        apply_absolute_value=True).then_inc(s["amax_ready"], 1)

            def attn_tile(t, p, i, last=False):
                for n in range(SUB):
                    c = SUB * t + n
                    begun = not (isinstance(c, int) and c == 0)
                    more = not (last and n == SUB - 1)
                    if begun:
                        normalise(c - 1)
                    update_state(c, n % 2, ends_row=i if (p == 1 and n == SUB - 1) else None)
                    if more:
                        mask(c + 1, 0)
                    if begun:
                        if n == 0:
                            residual(t - 1, 1 - p, SUB - 1)
                        else:
                            residual(t, p, n - 1)
                    if not last and n == 0:
                        front_q(t + 1, 1 - p)
                    if not last and n == 1:
                        front_k(t + 1, 1 - p)
                    if more:
                        mask(c + 1, 1)
                    if not last and n == 1:
                        front_heads(t + 1, 1 - p)
                    if more:
                        mask(c + 1, 2)
                        mask(c + 1, 3)
                    if begun and n == 0:
                        attn_norm(t - 1)

            front_q(0, 0)
            front_k(0, 0)
            front_heads(0, 0)
            dve.wait_ge(s["span_set"], 16)
            for g in range(QUADS):
                mask(0, g)
            attn_tile(0, 0, None)
            attn_tile(1, 1, 0)
            with dve.Fori(1, PAIRS - 1) as i:
                attn_tile(2 * i, 0, None)
                attn_tile(2 * i + 1, 1, i)
            attn_tile(NT - 2, 0, None)
            attn_tile(NT - 1, 1, PAIRS - 1, last=True)
            normalise(NC - 1)
            residual(NT - 1, 1, SUB - 1)
            attn_norm(NT - 1)

            dve.wait_ge(s["amax_ready"], NT)
            nc.vector.tensor_reduce(amax1[:], amax[:], AX.X, ALU.max).then_inc(s["amax1_ready"], 1)
            dve.wait_ge(s["amax_all_ready"], 1)
            nc.vector.tensor_scalar(x_scale[:], amax_all[:], 1.0 / 127.0, SCALE_EPS, ALU.mult, ALU.max)\
              .then_inc(s["scale_ready"], 1)
            dve.wait_ge(s["scale_ready"], 1)
            nc.vector.reciprocal(inv_scale[:], x_scale[:]).then_inc(s["scale_ready"], 1)
            nc.vector.tensor_scalar(deq_scale[:], rows_bc[:, 2, :], x_scale[:], None, ALU.mult)\
              .then_inc(s["deq_ready"], 1)
            dve.wait_ge(s["scale_ready"], 2)
            dve.wait_ge(s["deq_ready"], 1)

            def layer_stats(k, t, src):
                for n in range(SUB):
                    dve.wait_ge(mv_r[k], SUB * t)
                    nc.vector.bn_stats(stats[k][:, n, :], src(n)).then_inc(st_r[k], 1)
                for n in range(SUB):
                    dve.wait_ge(st_r[k], SUB * t + n + 1)
                    dve.wait_ge(ve_r[k], t)
                    settled(dve)
                    nc.vector.bn_aggr(mv[k][:, n, :], stats[k][:, n, :]).then_inc(mv_r[k], 1)

            def layer_norm(k, t, dst, src):
                dve.wait_ge(rs_r[k], t + 1)
                for n in range(SUB):
                    nc.vector.tensor_scalar(dst(n), src(n), mv[k][:, n, 0:1], rstd[k][:, n:n + 1],
                                            ALU.subtract, ALU.mult).then_inc(nm_r[k], 1)

            def recur(t, p, k, slot):
                if slot == 0:
                    dve.wait_ge(s["xqT_ps"], t)
                    settled(dve)
                    nc.vector.tensor_scalar(xq[:], x1_all[:, bass.ds(SUB * t, SUB), :], inv_scale[:], MAGIC,
                                            ALU.mult, ALU.add).then_inc(s["xq_round"], 1)
                    dve.wait_ge(s["xq_round"], t + 1)
                    nc.vector.tensor_scalar(xq[:], xq[:], MAGIC - 128.0, MAGIC + 127.0, ALU.max, ALU.min)\
                      .then_inc(s["xq_ready"], 1)
                elif slot == 2:
                    dve.wait_ge(s["q8_ps"], t + 1)
                    dve.wait_ge(nm_r[0], SUB * t)
                    nc.vector.tensor_tensor(y_ffn[:], ps_a[:].rearrange("p (s e) -> p s e", s=SUB),
                                            deq_scale[:].unsqueeze(1).to_broadcast([P, SUB, E]), ALU.mult)\
                      .then_inc(s["deq_done"], 1)
                    dve.wait_ge(s["deq_done"], t + 1)
                    dve.wait_ge(s["x1b_ready"], t + 1)
                    nc.vector.tensor_tensor(y_ffn[:], y_ffn[:], x1_b[:], ALU.add).then_inc(s["yffn_ready"], 1)
                    dve.wait_ge(s["yffn_ready"], t + 1)
                    layer_stats(0, t, lambda n: y_ffn[:, n, :])
                elif slot == 3:
                    if not (isinstance(t, int) and t < 2):
                        dve.wait_ge(s["ylstm_ready"], t - 1)
                        dve.wait_ge(s["x2T_ps"], t - 1)
                    layer_norm(0, t, lambda n: x2[p][:, n, :], lambda n: y_ffn[:, n, :])
                elif slot == 10:
                    dve.wait_ge(s["ti_ready"], t + 1)
                    dve.wait_ge(s["tz_ready"], t + 1)
                    dve.wait_ge(s["cell_ready"], t)
                    nc.vector.scalar_tensor_tensor(iz2[:], tanh_i[:], 1.0, tanh_z[:], ALU.add, ALU.mult)\
                      .then_inc(s["iz_ready"], 1)
                    dve.wait_ge(s["iz_ready"], t + 1)
                    dve.wait_ge(s["f_ready"], t + 1)
                    dve.wait_ge(s["carry_ready"], t)
                    if not (isinstance(t, int) and t < 2):
                        dve.wait_ge(s["cellT_ps"], t - 1)
                    nc.vector.tensor_tensor_scan(cell2[p][:], f_gate[:], iz2[:], carry[:], ALU.mult, ALU.add)\
                      .then_inc(s["cell_ready"], 1)
                    dve.wait_ge(s["cell_ready"], t + 1)
                    if p == 1:
                        settled(dve)
                        nc.vector.tensor_scalar(carry[:], cell2[p][:, TILE - 1:TILE], keep[:, bass.ds(k, 1)], None,
                                                ALU.mult).then_inc(s["carry_ready"], 1)
                    else:
                        nc.vector.tensor_copy(carry[:], cell2[p][:, TILE - 1:TILE]).then_inc(s["carry_ready"], 1)

            def emit(t, p, slot):
                if slot == 1:
                    dve.wait_ge(s["cellT_ps"], t + 1)
                    layer_stats(1, t, lambda n: ps_b[:, P * n:P * n + P])
                elif slot == 2:
                    dve.wait_ge(s["caff_ready"], t)
                    layer_norm(1, t, lambda n: c_norm[:, n, :], lambda n: ps_b[:, P * n:P * n + P])
                elif slot == 4:
                    dve.wait_ge(s["tc_ready"], t + 1)
                    dve.wait_ge(s["to_ready"], t + 1)
                    dve.wait_ge(s["ylstm_ready"], t)
                    nc.vector.scalar_tensor_tensor(h2[:], tanh_o[p][:], 1.0, tanh_c[:], ALU.add, ALU.mult)\
                      .then_inc(s["h2_ready"], 1)
                    dve.wait_ge(s["h2_ready"], t + 1)
                    dve.wait_ge(nm_r[2], SUB * t)
                    nc.vector.scalar_tensor_tensor(y_lstm[:], h2[:], 0.5, x2[p][:], ALU.mult, ALU.add)\
                      .then_inc(s["ylstm_ready"], 1)
                    dve.wait_ge(s["ylstm_ready"], t + 1)
                    layer_stats(2, t, lambda n: y_lstm[:, n, :])
                elif slot == 5:
                    if not (isinstance(t, int) and t < 2):
                        dve.wait_ge(s["ymoe_ready"], t - 1)
                    layer_norm(2, t, lambda n: x3[p][:, n, :], lambda n: y_lstm[:, n, :])
                elif slot == 6:
                    dve.wait_ge(s["x3T_ps"], t + 1)
                    dve.wait_ge(s["x3hi_ready"], t + 1)
                    if not (isinstance(t, int) and t < 2):
                        dve.wait_ge(s["u_ps"], NJ * (t - 1))
                    nc.vector.tensor_tensor(x3T_lo[p][:], ps_b[:], x3T_hi[p][:].bitcast(F32), ALU.subtract)\
                      .then_inc(s["x3lo_ready"], 1)
                elif slot == 8:
                    route(t, 0)
                elif slot == 9:
                    route(t, 1)

            def route(t, half):
                def after(n):
                    dve.wait_ge(s["route_step"], ROUTE * t + n)

                def step(ins):
                    ins.then_inc(s["route_step"], 1)

                each = lambda a: a[:].unsqueeze(2).to_broadcast([P, SUB, EXPERTS])
                if half == 0:
                    dve.wait_ge(s["logit_ps"], t + 1)
                    after(0)
                    step(nc.vector.tensor_copy(logits[:], ps_b[:, 0:SUB * EXPERTS]
                                               .rearrange("p (s e) -> p s e", s=SUB)))
                if half == 0:
                    for k, left in enumerate((logits, logits2)):
                        after(7 * k + 1)
                        step(nc.vector.tensor_reduce(top[k][:], left[:], AX.X, ALU.max))
                        after(7 * k + 2)
                        step(nc.vector.tensor_tensor(is_top[k][:], left[:], each(top[k]), ALU.is_equal))
                        after(7 * k + 3)
                        step(nc.vector.tensor_tensor(rank[k][:], is_top[k][:], rev_index[:], ALU.mult))
                        after(7 * k + 4)
                        step(nc.vector.tensor_reduce(best[k][:], rank[k][:], AX.X, ALU.max))
                        after(7 * k + 5)
                        step(nc.vector.tensor_tensor(pick[k][:], rank[k][:], each(best[k]), ALU.is_equal))
                        if k == 0:
                            after(6)
                            step(nc.vector.scalar_tensor_tensor(logits2[:], pick[0][:], -3.0e38, logits[:],
                                                                ALU.mult, ALU.add))
                            step(nc.vector.tensor_copy(pick_sum[:], pick[0][:]))
                    after(13)
                    dve.wait_ge(s["tgap_ready"], t)
                    nc.vector.tensor_tensor(gap[:], top[0][:], top[1][:], ALU.subtract).then_inc(s["gap_ready"], 1)
                    step(nc.vector.tensor_tensor(pick_dif[:], pick_sum[:], pick[1][:], ALU.subtract))
                    after(14)
                    step(nc.vector.tensor_tensor(pick_sum[:], pick_sum[:], pick[1][:], ALU.add))
                    return
                dve.wait_ge(s["tgap_ready"], t + 1)
                after(15)
                step(nc.vector.tensor_tensor(dif_t[:], pick_dif[:], each(tanh_gap), ALU.mult))
                after(16)
                step(nc.vector.tensor_tensor(w2x[:], pick_sum[:], dif_t[:], ALU.add))
                after(17)
                step(nc.vector.tensor_scalar(w_tok[:], w2x[:], 0.5, None, ALU.mult))
                after(18)
                step(nc.vector.tensor_copy(w_tok_r[:], w_tok[:]))
                after(19)
                dve.wait_ge(s["wT_ps"], t)
                step(nc.vector.tensor_copy(w_parts[:, :, 0, :], w_tok_r[:].bitcast(F32)))
                step(nc.vector.tensor_tensor(w_parts[:, :, 1, :], w_tok[:], w_tok_r[:].bitcast(F32), ALU.subtract))

            def block_product(t, p, j):
                n = NJ * t + j
                m = P if j < NJ - 1 else LASTK
                early = isinstance(n, int) and n < 2
                dve.wait_ge(s["silu_ready"], n + 1)
                dve.wait_ge(s["u_ps"], n + 1)
                if not early:
                    dve.wait_ge(s["hi_ready"], n - 1)
                    dve.wait_ge(s["lo_ready"], n - 1)
                if j < NJR:
                    nc.vector.tensor_tensor(gu[j % 2][0:m], silu_g[j % 2][0:m], ps_u[j % 2][0:m], ALU.mult)\
                      .then_inc(s["gu_ready"], 1)
                    dve.wait_ge(s["gu_ready"], NJR * t + j + 1)
                    dve.wait_ge(s["w_ps"], NJR * t + j + 1)
                    nc.vector.tensor_tensor(hid[j % 2][0:m], gu[j % 2][0:m], ps_w[0:m], ALU.mult)\
                      .then_inc(s["hid_ready"], 1)
                else:
                    nc.vector.tensor_tensor(hid[j % 2][0:m], silu_g[j % 2][0:m], ps_u[j % 2][0:m], ALU.mult)\
                      .then_inc(s["hid_ready"], 1)

            def finish(t, p):
                dve.wait_ge(s["y_ps"], t + 1)
                dve.wait_ge(nm_r[3], SUB * t)
                nc.vector.tensor_tensor(y_moe[:], ps_b[:].rearrange("p (s e) -> p s e", s=SUB), x3[p][:], ALU.add)\
                  .then_inc(s["ymoe_ready"], 1)
                dve.wait_ge(s["ymoe_ready"], t + 1)
                layer_stats(3, t, lambda n: y_moe[:, n, :])

            def finish_norm(t):
                dve.wait_ge(s["out_stored"], 16 * t)
                layer_norm(3, t, lambda n: x4[:, n, :], lambda n: y_moe[:, n, :])

            def moe_tile(t, p, k, last=False):
                begun = not (isinstance(t, int) and t == 0)
                for j in range(NJ):
                    ahead = j + AHEAD
                    if ahead < NJ:
                        block_product(t, p, ahead)
                    elif not last:
                        block_product(t + 1, 1 - p, ahead - NJ)
                    if begun and j == 0:
                        finish(t - 1, 1 - p)
                    if begun and j == 1:
                        finish_norm(t - 1)
                    if not last:
                        recur(t + 2, p, k, j)
                        emit(t + 1, 1 - p, j)

            for slot in range(NJ):
                recur(0, 0, None, slot)
            for slot in range(NJ):
                recur(1, 1, 0, slot)
                emit(0, 0, slot)
            for j in range(AHEAD):
                block_product(0, 0, j)
            moe_tile(0, 0, None)
            moe_tile(1, 1, 1)
            with dve.Fori(1, PAIRS - 1) as i:
                moe_tile(2 * i, 0, None)
                moe_tile(2 * i + 1, 1, i + 1)
            moe_tile(NT - 2, 0, None)
            moe_tile(NT - 1, 1, None, last=True)
            finish(NT - 1, 1)
            finish_norm(NT - 1)

        @block.tensor
        def _(pe):
            def turn(dst, src):
                return nc.tensor.transpose(dst, src, ident[0:src.shape[0], 0:src.shape[0]])

            pe.wait_ge(s["consts_ready"], 1)
            pe.wait_ge(s["wl_square"], 16 * 5)
            for b in range(2):
                for n in range(4):
                    ins = turn(ps_scores[b][:, P * n:P * n + P], w_nat[:, 4 * b + n, :])
                ins.then_inc(s["w_tr"], 1)
            pe.wait_ge(s["w8_cast"], 1)
            turn(ps_scores[2][:, 0:P], w_nat[:, 8, :]).then_inc(s["w_tr"], 1)
            pe.wait_ge(s["wl_rows"], 16 * 6)
            nc.tensor.matmul(ps_scores[3][:], ones_row[:], rows[:, 0:4, :], start=True, stop=True)\
              .then_inc(s["rows_bc_ps"], 1)
            nc.tensor.matmul(ps_tr[:, 0:P], ones_row[:], rows[:, 4, :], start=True, stop=True)\
              .then_inc(s["rows_bc_ps"], 1)
            pe.wait_ge(s["w_tr_copied"], 2)
            pe.wait_ge(s["w8T_ready"], 1)
            pe.wait_ge(s["rows_bc_ready"], 2)
            pe.wait_ge(s["state_zero"], 4)
            pe.wait_ge(s["quad_ready"], 2)

            def x_transposed(t, p):
                pe.wait_ge(s["x_loaded"], 16 * (t + 1))
                pe.wait_ge(s["vown_ready"], 4 * SUB * t)
                for n in range(SUB):
                    ins = turn(ps_tr[:, P * n:P * n + P], x_cur[p][:, n, :])
                ins.then_inc(s["xT_ps"], 1)

            def project_q(t):
                pe.wait_ge(s["v_ready"], t + 1)
                nc.tensor.matmul(ps_proj[:], wT[:, 0, :], xT[:], start=True, stop=True).then_inc(s["q_ps"], 1)

            def project_k(t):
                pe.wait_ge(s["q_ready"], t + 1)
                nc.tensor.matmul(ps_proj[:], wT[:, 1, :], xT[:], start=True, stop=True).then_inc(s["k_ps"], 1)

            def project_v(t):
                pe.wait_ge(s["xT_ready"], t + 1)
                pe.wait_ge(s["ktok_ready"], t)
                for n in range(SUB):
                    ins = nc.tensor.matmul(ps_proj[:, P * n:P * n + P], xT[:, P * n:P * n + P], wT[:, 2, :],
                                           start=True, stop=True)
                ins.then_inc(s["v_ps"], 1)

            def k_transposed(t, p):
                pe.wait_ge(s["k_ready"], t + 1)
                for n in range(SUB):
                    ins = turn(ps_proj[:, P * n:P * n + P], kT[p][:, P * n:P * n + P])
                ins.then_inc(s["ktok_ps"], 1)

            def project_own(t, p, n):
                pe.wait_ge(s["v_ready"], t + 1)
                pe.wait_ge(s["vown_ready"], 4 * (SUB * t + n))
                for b in range(4):
                    ins = nc.tensor.matmul(ps_tr[:, P * b:P * b + P], repeat4[:, b, :, :].rearrange("p r j -> p (r j)"),
                                           v_tok[p][:, n, :, 0:D], start=True, stop=True)
                ins.then_inc(s["vown_ps"], 1)

            def front(t, p, n):
                if n == 0:
                    project_q(t)
                elif n == 1:
                    project_k(t)
                elif n == 2:
                    k_transposed(t, p)
                project_own(t, p, n)

            def score(c, n, p, t, g):
                rows32 = slice(32 * g, 32 * g + 32)
                if n == 0 and g == 0:
                    pe.wait_ge(s["q_ready"], t + 1)
                    pe.wait_ge(s["kheads_v"], 2 * (t + 1))
                    pe.wait_ge(s["kheads_p"], 2 * (t + 1))
                if not (isinstance(c, int) and c == 0):
                    pe.wait_ge(s["masked"], 4 * (c - 1) + g + 1)
                for b in range(4):
                    at = CHUNK * n + 32 * b
                    ins = nc.tensor.matmul(ps_scores[g][:, SPAN_AT[b]:SPAN_AT[b] + SPAN[b]],
                                           k_heads[p][rows32, 4 * n + b, :, :].rearrange("p r j -> p (r j)"),
                                           qT[p][rows32, at:CHUNK * (n + 1)], start=True, stop=True)
                ins.then_inc(s["score_ps"], 1)

            def key_values(c, n, p, t):
                if n == 0:
                    pe.wait_ge(s["ktok_ready"], t + 1)
                    pe.wait_ge(s["v_ready"], t + 1)
                pe.wait_ge(s["kv_own_ready"], c)
                if not (isinstance(c, int) and c == 0):
                    pe.wait_ge(s["masked"], 4 * c)
                nc.tensor.matmul(ps_kv, k_tok[p][:, n, :], v_tok[p][:, n, :, :].rearrange("p h d -> p (h d)"),
                                 start=True, stop=True).then_inc(s["kv_ps"], 1)

            def from_state(c, n, p):
                pe.wait_ge(s["state_ready"], c)
                pe.wait_ge(s["numT_ready"], c)
                for half in range(2):
                    nc.tensor.matmul(ps_numT[0:64 + QV, CHUNK * half:CHUNK * (half + 1)],
                                     state[:, n % 2, 2 * half:2 * half + 2, :].rearrange("p g d -> p (g d)")[:, 0:64 + QV],
                                     qT[p][:, CHUNK * n:CHUNK * (n + 1)], start=(half == 0), stop=False)

            def attend(c, n, p, t, g):
                if n == 0 and g == 0:
                    pe.wait_ge(s["vown_ready"], 4 * SUB * (t + 1))
                pe.wait_ge(s["masked"], 4 * c + g + 1)
                rows = slice(64 * (g % 2), 64 * (g % 2) + QV)
                for b in range(4):
                    ins = nc.tensor.matmul(ps_numT[rows, CHUNK * (g // 2) + 32 * b:CHUNK * (g // 2 + 1)],
                                           v_own[p][:, n, QUADS * b + g, :, :].rearrange("p r d -> p (r d)"),
                                           scores[:, g, SPAN_AT[b]:SPAN_AT[b] + SPAN[b]],
                                           start=False, stop=(g >= 2 and b == 3))
                ins.then_inc(s["attn_num_ps"], 1)

            def sums_turned(c):
                pe.wait_ge(s["numT_ready"], c + 1)
                pe.wait_ge(s["yattn_ready"], c)
                for half in range(2):
                    ins = turn(ps_num[:, CHUNK * half:CHUNK * half + 64 + QV], numT[:, CHUNK * half:CHUNK * (half + 1)])
                ins.then_inc(s["num_turned"], 1)

            def attn_transposed(c):
                pe.wait_ge(s["attn_ready"], c + 1)
                turn(ps_attnT, attn[:].rearrange("p h d -> p (h d)")).then_inc(s["attnT_ps"], 1)

            def out_project(c):
                pe.wait_ge(s["attnT_ready"], c + 1)
                nc.tensor.matmul(ps_wo, attnT[:], wT[:, 3, :], start=True, stop=True).then_inc(s["wo_ps"], 1)

            def attn_tile(t, p, last=False):
                for n in range(SUB):
                    c = SUB * t + n
                    begun = not (isinstance(c, int) and c == 0)
                    nt, np_, nn = (t, p, n + 1) if n < SUB - 1 else (t + 1, 1 - p, 0)
                    more = not (last and n == SUB - 1)
                    if not last and n == 0:
                        x_transposed(t + 1, 1 - p)
                    if begun:
                        sums_turned(c - 1)
                    from_state(c, n, p)
                    attend(c, n, p, t, 0)
                    attend(c, n, p, t, 1)
                    if begun:
                        attn_transposed(c - 1)
                    attend(c, n, p, t, 2)
                    attend(c, n, p, t, 3)
                    if more:
                        score(c + 1, nn, np_, nt, 0)
                    if not last and n == 0:
                        project_v(t + 1)
                    if begun:
                        out_project(c - 1)
                    if more:
                        score(c + 1, nn, np_, nt, 1)
                    if not last:
                        front(t + 1, 1 - p, n)
                    if more:
                        score(c + 1, nn, np_, nt, 2)
                        key_values(c + 1, nn, np_, nt)
                        score(c + 1, nn, np_, nt, 3)

            x_transposed(0, 0)
            project_v(0)
            for n in range(SUB):
                front(0, 0, n)
            key_values(0, 0, 0, 0)
            for g in range(QUADS):
                score(0, 0, 0, 0, g)
            attn_tile(0, 0)
            attn_tile(1, 1)
            with pe.Fori(1, PAIRS - 1) as i:
                attn_tile(2 * i, 0)
                attn_tile(2 * i + 1, 1)
            attn_tile(NT - 2, 0)
            attn_tile(NT - 1, 1, last=True)
            sums_turned(NC - 1)
            attn_transposed(NC - 1)
            out_project(NC - 1)

            pe.wait_ge(s["yattn_ready"], NC)
            pe.wait_ge(s["o_bias_ready"], 1)

            def recur(t, p, slot):
                if slot == 0:
                    pe.wait_ge(s["xq_ready"], t + 1)
                    pe.wait_ge(s["to_ready"], t)
                    for n in range(SUB):
                        ins = turn(ps_a[:, P * n:P * n + P], xq[:, n, :])
                    ins.then_inc(s["xqT_ps"], 1)
                elif slot == 1:
                    pe.wait_ge(s["xqT_ready"], t + 1)
                    for n in range(SUB):
                        ins = nc.tensor.matmul(ps_a[:, P * n:P * n + P], xqT[:, P * n:P * n + P], w8T[:],
                                               start=True, stop=True)
                    ins.then_inc(s["q8_ps"], 1)
                elif slot == 5:
                    pe.wait_ge(nm_r[0], SUB * (t + 1))
                    pe.wait_ge(s["deq_done"], t + 1)
                    for n in range(SUB):
                        ins = turn(ps_a[:, P * n:P * n + P], x2[p][:, n, :])
                    ins.then_inc(s["x2T_ps"], 1)
                elif slot == 7:
                    pe.wait_ge(s["x2T_ready"], t + 1)
                    nc.tensor.matmul(ps_a[:], wT[:, 4, :], x2T[:], start=True, stop=True).then_inc(s["f_ps"], 1)
                elif slot == 8:
                    pe.wait_ge(s["tf_ready"], t + 1)
                    nc.tensor.matmul(ps_a[:], wT[:, 5, :], x2T[:], start=True, stop=True).then_inc(s["i_ps"], 1)
                elif slot == 9:
                    pe.wait_ge(s["ti_ready"], t + 1)
                    nc.tensor.matmul(ps_a[:], wT[:, 7, :], x2T[:], start=True, stop=True).then_inc(s["z_ps"], 1)
                elif slot == 10:
                    pe.wait_ge(s["tz_ready"], t + 1)
                    nc.tensor.matmul(ps_a[:], ones_row[:], o_bias4[:].rearrange("o s e -> o (s e)"),
                                     start=True, stop=False)
                    for n in range(SUB):
                        ins = nc.tensor.matmul(ps_a[:, P * n:P * n + P], x2T[:, P * n:P * n + P], wT[:, 6, :],
                                               start=False, stop=(n == SUB - 1))
                    ins.then_inc(s["o_ps"], 1)

            def emit(t, p, slot):
                if slot == 1:
                    pe.wait_ge(s["cell_ready"], t + 1)
                    if not (isinstance(t, int) and t == 0):
                        pe.wait_ge(s["ymoe_ready"], t - 1)
                        pe.wait_ge(s["wT_ready"], t)
                    for n in range(SUB):
                        ins = turn(ps_b[:, P * n:P * n + P], cell2[p][:, P * n:P * n + P])
                    ins.then_inc(s["cellT_ps"], 1)
                elif slot == 6:
                    pe.wait_ge(nm_r[2], SUB * (t + 1))
                    pe.wait_ge(nm_r[1], SUB * (t + 1))
                    for n in range(SUB):
                        ins = turn(ps_b[:, P * n:P * n + P], x3[p][:, n, :])
                    ins.then_inc(s["x3T_ps"], 1)
                elif slot == 8:
                    pe.wait_ge(s["x3hi_ready"], t + 1)
                    pe.wait_ge(s["x3lo_ready"], t + 1)
                    pe.wait_ge(s["router_ready"], 1)
                    for n in range(SUB):
                        o = ps_b[:, EXPERTS * n:EXPERTS * (n + 1)]
                        tok = slice(P * n, P * n + P)
                        nc.tensor.matmul(o, x3T_hi[p][:, tok], w_router_hi[:], start=True, stop=False)
                        nc.tensor.matmul(o, x3T_lo[p][:, tok], w_router_hi[:], start=False, stop=False)
                        ins = nc.tensor.matmul(o, x3T_hi[p][:, tok], w_router_lo[:], start=False, stop=True)
                    ins.then_inc(s["logit_ps"], 1)
                elif slot == 10:
                    pe.wait_ge(s["route_step"], ROUTE * (t + 1))
                    for n in range(SUB):
                        ins = turn(ps_b[0:16, P * n:P * n + P], w_parts[:, n, :, :].rearrange("p a e -> p (a e)"))
                    ins.then_inc(s["wT_ps"], 1)

            def product3(o, w_cols, m, hi, lo, first, last):
                k = hi.shape[0]
                nc.tensor.matmul(o, w_hi[0:k, w_cols:w_cols + m], hi, start=first, stop=False)
                nc.tensor.matmul(o, w_hi[0:k, w_cols:w_cols + m], lo, start=False, stop=False)
                return nc.tensor.matmul(o, w_lo[0:k, w_cols:w_cols + m], hi, start=False, stop=last)

            def up(t, p, j):
                n = NJ * t + j
                m = P if j < NJ - 1 else LASTK
                early = isinstance(n, int) and n < 2
                if j == 0:
                    pe.wait_ge(s["x3hi_ready"], t + 1)
                    pe.wait_ge(s["x3lo_ready"], t + 1)
                if not early:
                    pe.wait_ge(s["silu_ready"], n - 1)
                product3(ps_g[j % 2][0:m], P * j, m, x3T_hi[p][:], x3T_lo[p][:], True, True).then_inc(s["g_ps"], 1)
                if not early:
                    pe.wait_ge(s["hid_ready"], n - 1)
                product3(ps_u[j % 2][0:m], HALL + P * j, m, x3T_hi[p][:], x3T_lo[p][:], True, True)\
                    .then_inc(s["u_ps"], 1)

            def spread(t, p, j):
                if j < NJR:
                    if j == 0:
                        pe.wait_ge(s["wT_ready"], t + 1)
                    pe.wait_ge(s["hid_ready"], NJ * t + j)
                    nc.tensor.matmul(ps_w[:], sel16_r[:, P * j:P * j + P], w_partsT[p][:], start=True, stop=True)\
                      .then_inc(s["w_ps"], 1)

            def down(t, p, j):
                n = NJ * t + j
                b = (NJ * p + j) % 4
                m = P if j < NJ - 1 else LASTK
                if j == 0:
                    pe.wait_ge(s["yT_ready"], t)
                pe.wait_ge(s["hi_ready"], n + 1)
                pe.wait_ge(s["lo_ready"], n + 1)
                product3(ps_y[:], 2 * HALL + P * j, P, hid_hi[b][0:m], hid_lo[b][0:m], j == 0, j == NJ - 1)\
                    .then_inc(s["down_ps"], 1)

            def finish(t):
                pe.wait_ge(s["yT_ready"], t + 1)
                pe.wait_ge(s["wT_ready"], min(t + 2, NT) if isinstance(t, int) else t + 2)
                for n in range(SUB):
                    ins = turn(ps_b[:, P * n:P * n + P], yT[:, P * n:P * n + P])
                ins.then_inc(s["y_ps"], 1)

            def moe_tile(t, p, last=False):
                for j in range(NJ):
                    nt, np_, nj = (t, p, j + AHEAD) if j + AHEAD < NJ else (t + 1, 1 - p, j + AHEAD - NJ)
                    more = j + AHEAD < NJ or not last
                    if more:
                        up(nt, np_, nj)
                    down(t, p, j)
                    if more:
                        spread(nt, np_, nj)
                    if j == 0 and not (isinstance(t, int) and t == 0):
                        finish(t - 1)
                    if not last:
                        recur(t + 2, p, j)
                        emit(t + 1, 1 - p, j)

            for slot in range(NJ):
                recur(0, 0, slot)
            for slot in range(NJ):
                recur(1, 1, slot)
                emit(0, 0, slot)
            pe.wait_ge(s["ff_split"], NT)
            pe.wait_ge(s["sel_r_ready"], 8)
            for j in range(AHEAD):
                up(0, 0, j)
                spread(0, 0, j)
            moe_tile(0, 0)
            moe_tile(1, 1)
            with pe.Fori(1, PAIRS - 1) as i:
                moe_tile(2 * i, 0)
                moe_tile(2 * i + 1, 1)
            moe_tile(NT - 2, 0)
            moe_tile(NT - 1, 1, last=True)
            finish(NT - 1)


_INS = ['L0_attn_x', 'L0_attn_Wq', 'L0_attn_Wk', 'L0_attn_Wv', 'L0_attn_Wo', 'L0_attn_bo', 'L0_ffn_weight_int8',
        'L0_ffn_weight_scale', 'L0_ffn_bias', 'L1_attn_W', 'L1_attn_b', 'L1_attn_ln_w', 'L1_attn_ln_b', 'L1_ffn_Wg',
        'L1_ffn_W1', 'L1_ffn_W2', 'L1_ffn_W3', 'L1_ffn_Ws1', 'L1_ffn_Ws2', 'L1_ffn_Ws3']
_OUTS = [((2, 2048, 128), 'float32')]


def kernel(**inputs):
    import numpy as _np
    import concourse.bacc as _bacc
    from concourse import mybir as _mybir
    from concourse.bass_utils import run_bass_kernel_spmd as _run

    nc = _bacc.Bacc("TRN2", target_bir_lowering=False, num_devices=1)
    arrays, args = {}, []
    for name in _INS:
        a = _np.ascontiguousarray(inputs[name])
        if a.dtype.kind in "iu":
            a = a.astype(_np.int64)
        arrays[f"in_{name}_dram"] = a
        args.append(nc.dram_tensor(f"in_{name}_dram", a.shape, _mybir.dt.from_np(a.dtype), kind="ExternalInput").ap())
    for i, (shape, dtype) in enumerate(_OUTS):
        dt = _mybir.dt.from_np(_np.dtype(dtype))
        args.append(nc.dram_tensor(f"out_{i}_dram", shape, dt, kind="ExternalOutput").ap())
    build_program(nc, *args)
    r = _run(nc, [arrays], core_ids=[0])
    got = tuple(r.results[0][f"out_{i}_dram"] for i in range(len(_OUTS)))
    return got[0]
```

```python
import concourse.bass as bass
from concourse import mybir
from contextlib import ExitStack

F32 = mybir.dt.float32
F32R = mybir.dt.float32r
BF16 = mybir.dt.bfloat16
I32 = mybir.dt.int32
ALU = mybir.AluOpType
ACT = mybir.ActivationFunctionType
AX = mybir.AxisListType

P = 128
CHUNK = 128
SUB = 4
TILE = SUB * CHUNK
LN_EPS = 1e-5
DEN_EPS = 1e-5
SCALE_EPS = 1e-5
MAGIC = 1.5 * 2.0 ** 23


def build_program(nc, x_in, Wq, Wk, Wv, Wo, bo, W8, w8_scale, ffn_bias, Wgates, gate_bias,
                  ln_w, ln_b, Wrouter, W1, W2, W3, Ws1, Ws2, Ws3, out):
    B, T_LEN, E = x_in.shape
    HEADS = 16
    D = E // HEADS
    QUADS = 4
    DV = D + 1
    NT = B * T_LEN // TILE
    NC = NT * SUB
    PAIRS = NT // 2
    TPB = T_LEN // TILE
    EXPERTS = Wrouter.shape[1]
    HID = W1.shape[2]
    HSH = Ws1.shape[1]
    ROUTED = EXPERTS * HID
    HALL = ROUTED + HSH
    NJ = -(-HALL // P)
    NJR = ROUTED // P
    LASTK = HALL - (NJ - 1) * P
    SHARED = NJ - NJR
    ROUTE = 21
    STEPS = 2 * NJ
    LAG = 14
    AHEAD = 3
    W_COLS = 2 * HALL + NJ * P
    WSLICE = W_COLS // NT
    QV = 4 * DV
    assert ROUTED % P == 0 and W_COLS % NT == 0 and E == P and TPB % 2 == 0

    x_tiles = x_in.rearrange("b (n s p) e -> (b n) p s e", p=P, s=SUB)
    out_tiles = out.rearrange("b (n s p) e -> (b n) p s e", p=P, s=SUB)

    with ExitStack() as ctx:
        def sb(name, shape, dt=F32):
            return ctx.enter_context(nc.sbuf_tensor(name, shape, dt))

        def bank(name, shape, dt=F32):
            return ctx.enter_context(nc.psum_tensor(name, shape, dt))

        def sem(name):
            return ctx.enter_context(nc.semaphore(name))

        ident = sb("ident", [P, P])
        causal = sb("causal", [P, CHUNK])
        head_of = sb("head_of", [P, QUADS, 4])
        head_of_2 = sb("head_of_2", [P, QUADS, 4])
        in_quad = sb("in_quad", [P, 4])
        keep = sb("keep", [P, PAIRS])
        carry = sb("carry", [P, 1])
        ones_row = sb("ones_row", [1, P])
        minus_half = sb("minus_half", [P, SUB])
        rev_index = sb("rev_index", [P, SUB, EXPERTS])
        sel16_r = sb("sel16_r", [16, ROUTED], F32R)
        wT = sb("wT", [P, 8, P])
        wT_hi = sb("wT_hi", [P, 8, P], F32R)
        wT_lo = sb("wT_lo", [P, 8, P], F32R)
        w8T = sb("w8T", [P, P], BF16)
        rows = sb("rows", [1, 6, P])
        rows_bc = sb("rows_bc", [P, 5, P])
        ones_r = sb("ones_r", [1, P], F32R)
        o_bias_hi = sb("o_bias_hi", [1, SUB, P], F32R)
        o_bias_lo = sb("o_bias_lo", [1, SUB, P], F32R)
        gate_b = sb("gate_b", [P, 3])
        gate_bh = sb("gate_bh", [P, 2])
        w_router = sb("w_router", [P, EXPERTS])
        w_router_hi = sb("w_router_hi", [P, EXPERTS], F32R)
        w_router_lo = sb("w_router_lo", [P, EXPERTS], F32R)
        w_hi = sb("w_hi", [P, W_COLS], F32R)
        w_lo = sb("w_lo", [P, W_COLS], F32R)
        amax = sb("amax", [P, NT])
        amax1 = sb("amax1", [P, 1])
        amax_all = sb("amax_all", [P, 1])
        x_scale = sb("x_scale", [P, 1])
        inv_scale = sb("inv_scale", [P, 1])
        deq_scale = sb("deq_scale", [P, P])
        x1_all = sb("x1_all", [P, NC + SUB, E])

        first = ctx.enter_context(ExitStack())

        def sb1(name, shape, dt=F32):
            return first.enter_context(nc.sbuf_tensor(name, shape, dt))

        sel16 = sb1("sel16", [16, ROUTED])
        w_nat = sb1("w_nat", [P, 9, P])
        w8_raw = sb1("w8_raw", [P, P, 2], I32)
        w_ff = sb1("w_ff", [P, W_COLS])
        x_cur = [sb1(f"x_cur{p}", [P, SUB, E]) for p in range(2)]
        x_bo = [sb1(f"x_bo{p}", [P, SUB, E]) for p in range(2)]
        xT = sb1("xT", [P, TILE])
        xT_hi = sb1("xT_hi", [P, TILE], F32R)
        xT_lo = sb1("xT_lo", [P, TILE], F32R)
        exp_qk = sb1("exp_qk", [P, TILE])
        qT = [sb1(f"qT{p}", [P, TILE]) for p in range(2)]
        kT = [sb1(f"kT{p}", [P, TILE]) for p in range(2)]
        k_heads = [sb1(f"k_heads{p}", [P, 4 * SUB, 4, 32]) for p in range(2)]
        k_tok = [sb1(f"k_tok{p}", [P, SUB, P]) for p in range(2)]
        v_tok = [sb1(f"v_tok{p}", [P, SUB, HEADS, DV]) for p in range(2)]
        v_own = [sb1(f"v_own{p}", [P, SUB, 4 * QUADS, 4, DV]) for p in range(2)]
        q_quad = [sb1(f"q_quad{n}", [P, QUADS, CHUNK]) for n in range(2)]
        scores = [sb1(f"scores{b}", [P, QUADS * (CHUNK - 32 * b)]) for b in range(4)]
        state = sb1("state", [P, 2, QUADS, 64])
        numT = sb1("numT", [64 + QV, 2 * CHUNK])
        kv_sum = sb1("kv_sum", [P, HEADS * DV])
        kv_own = sb1("kv_own", [P, HEADS * DV])
        den = sb1("den", [P, HEADS])
        rden = sb1("rden", [P, HEADS])
        attn = sb1("attn", [P, HEADS, D])
        attnT = sb1("attnT", [P, P])
        y_attn = [sb1(f"y_attn{p}", [P, SUB, E]) for p in range(2)]
        a_stats = sb1("a_stats", [P, SUB, 6])
        a_mv = sb1("a_mv", [P, SUB, 2])
        a_var = sb1("a_var", [P, SUB])
        a_rstd = sb1("a_rstd", [P, SUB])
        a_minus = sb1("a_minus", [P, SUB])
        a_shift = sb1("a_shift", [P, SUB])

        first.close()

        xq = sb("xq", [P, SUB, E])
        x1_b = sb("x1_b", [P, SUB, E])
        xqT = sb("xqT", [P, TILE], BF16)
        y_ffn = sb("y_ffn", [P, SUB, E])
        stats = [sb(f"stats{n}", [P, SUB, 6]) for n in range(4)]
        mv = [sb(f"mv{n}", [P, SUB, 2]) for n in range(4)]
        var_eps = [sb(f"var_eps{n}", [P, SUB]) for n in range(4)]
        rstd = [sb(f"rstd{n}", [P, SUB]) for n in range(4)]
        minus = [sb(f"minus{n}", [P, SUB]) for n in range(4)]
        shift = [sb(f"shift{n}", [P, SUB]) for n in range(4)]
        x2 = [sb(f"x2_{p}", [P, SUB, E]) for p in range(2)]
        x2T = sb("x2T", [P, TILE])
        x2T_hi = sb("x2T_hi", [P, TILE], F32R)
        x2T_lo = sb("x2T_lo", [P, TILE], F32R)
        tanh_f = sb("tanh_f", [P, TILE])
        tanh_i = sb("tanh_i", [P, TILE])
        tanh_z = sb("tanh_z", [P, TILE])
        tanh_o = [sb(f"tanh_o{p}", [P, SUB, E]) for p in range(2)]
        f_gate = sb("f_gate", [P, TILE])
        iz2 = sb("iz2", [P, TILE])
        cell2 = [sb(f"cell2_{p}", [P, TILE]) for p in range(2)]
        c_norm = sb("c_norm", [P, SUB, E])
        c_aff = sb("c_aff", [P, SUB, E])
        tanh_c = sb("tanh_c", [P, SUB, E])
        h2 = sb("h2", [P, SUB, E])
        y_lstm = sb("y_lstm", [P, SUB, E])

        x3 = [sb(f"x3_{p}", [P, SUB, E]) for p in range(2)]
        x3T_hi = [sb(f"x3T_hi{p}", [P, TILE], F32R) for p in range(2)]
        x3T_lo = [sb(f"x3T_lo{p}", [P, TILE], F32R) for p in range(2)]
        logits = sb("logits", [P, SUB, EXPERTS])
        logits2 = sb("logits2", [P, SUB, EXPERTS])
        top = [sb(f"top{n}", [P, SUB]) for n in range(2)]
        is_top = [sb(f"is_top{n}", [P, SUB, EXPERTS]) for n in range(2)]
        rank = [sb(f"rank{n}", [P, SUB, EXPERTS]) for n in range(2)]
        best = [sb(f"best{n}", [P, SUB]) for n in range(2)]
        pick = [sb(f"pick{n}", [P, SUB, EXPERTS]) for n in range(2)]
        gap = sb("gap", [P, SUB])
        tanh_gap = sb("tanh_gap", [P, SUB])
        pick_sum = sb("pick_sum", [P, SUB, EXPERTS])
        pick_dif = sb("pick_dif", [P, SUB, EXPERTS])
        dif_t = sb("dif_t", [P, SUB, EXPERTS])
        w2x = sb("w2x", [P, SUB, EXPERTS])
        w_tok = sb("w_tok", [P, SUB, EXPERTS])
        w_tok_r = sb("w_tok_r", [P, SUB, EXPERTS], F32R)
        w_parts = sb("w_parts", [P, SUB, 2, EXPERTS])
        w_partsT = [sb(f"w_partsT{p}", [16, TILE], F32R) for p in range(2)]
        silu_g = [sb(f"silu_g{n}", [P, TILE]) for n in range(2)]
        gu = [sb(f"gu{n}", [P, TILE]) for n in range(2)]
        hid = [sb(f"hid{n}", [P, TILE]) for n in range(2)]
        hid_hi = [sb(f"hid_hi{n}", [P, TILE], F32R) for n in range(4)]
        hid_lo = [sb(f"hid_lo{n}", [P, TILE], F32R) for n in range(4)]
        yT = sb("yT", [P, TILE])
        y_moe = sb("y_moe", [P, SUB, E])
        x4 = sb("x4", [P, SUB, E])

        pb = [bank(f"bank{n}", [P, 512]) for n in range(8)]
        ps_scores = pb[0:4]
        ps_proj = pb[5]
        ps_numT = pb[6][:, 0:2 * CHUNK]
        ps_kv = pb[4][:, 0:HEADS * DV]
        ps_num = pb[7][:, 0:4 * 64]
        ps_attnT = pb[7][:, 256:256 + P]
        ps_wo = pb[7][:, 384:384 + P]
        ps_g = (pb[0], pb[1], pb[4])
        ps_u = pb[2:4]
        ps_y = pb[5]
        ps_a = pb[6]
        ps_b = pb[7]
        ps_a2 = pb[0]
        first_block = 18

        s = {n: sem(n) for n in (
            "wl_square wl_gates wl_int8 wl_rows wl_cols wl_router wl_ff x_loaded out_stored z_set consts_ready "
            "one_set v_ones state_zero ff_pad_zero w_tr w_tr_copied w8_cast w8T_ready rows_bc_ps rows_bc_ready "
            "o_bias_ready gate_bh_ready quad_ready router_hi router_ready sel_r_ready ff_hi ff_split quad_zero "
            "qquad_ready wT_hi_ready wT_split xThi_ready xTlo_ready xT_ps xT_ready q_ps expq_ready expq_min "
            "q_ready k_ps expk_ready expk_min k_ready v_ps v_ready ktok_ps ktok_ready kheads_v kheads_p "
            "vown_ready vown_set num_turned numT_ready span_set xbo_ready score_ps masked kv_ps kv_own_ready "
            "state_ready state_kept attn_num_ps den_ready rden_ready attn_ready attnT_ps attnT_ready wo_ps "
            "yattn_ready astats_ready amv_ready avar_ready arstd_ready x1_ready amax_ready amax1_ready "
            "amax_all_ready scale_ready deq_ready xq_round xq_ready x1b_ready xqT_ps xqT_ready q8_ps deq_done "
            "yffn_ready x2T_ps x2T_ready x2hi_ready x2lo_ready o_bias_hi_ready f_ps tf_ready i_ps ti_ready z_ps "
            "tz_ready o_ps to_ready f_ready iz_ready cell_ready carry_ready cellT_ps cscaled caff_ready "
            "tc_ready h2_ready ylstm_ready x3T_ps x3hi_ready x3lo_ready logit_ps gap_ready tgap_ready wT_ps "
            "wT_ready g_ps u_ps w_ps silu_ready gu_ready hid_ready hi_ready lo_ready down_ps yT_ready y_ps "
            "ymoe_ready x4_ready route_step").split()}
        norms = ("ffn", "cell", "lstm", "moe")
        st_r = [sem(f"{n}_stats_ready") for n in norms]
        mv_r = [sem(f"{n}_meanvar_ready") for n in norms]
        ve_r = [sem(f"{n}_var_and_minus_ready") for n in norms]
        rs_r = [sem(f"{n}_rstd_and_shift_ready") for n in norms]
        nm_r = [sem(f"{n}_normed") for n in norms[:3]] + [s["x4_ready"]]

        block = ctx.enter_context(nc.Block())

        def block_of(j):
            return NJR + j if j < SHARED else j - SHARED

        def units(j):
            return LASTK if block_of(j) == NJ - 1 else P

        def settled(eng):
            eng.nop(nofuse=True)


        @block.sync
        def _(sp):
            def load_x(t, p, first=False):
                if not first:
                    sp.wait_ge(s["x_loaded"], 16 * t)
                    settled(sp)
                    sp.wait_ge(s["xT_ps"], t - 1)
                    settled(sp)
                    sp.wait_ge(s["xbo_ready"], t - 1)
                    settled(sp)
                sp.dma_start(x_cur[p][:], x_tiles[bass.ds(t, 1)].rearrange("o p s e -> (o p) s e")
                             if not isinstance(t, int) else x_tiles[t]).then_inc(s["x_loaded"], 16)

            load_x(0, 0, first=True)
            for n, w in enumerate((Wq, Wk, Wv, Wo)):
                sp.dma_start(w_nat[:, n, :], w).then_inc(s["wl_square"], 16)
            for n, r in enumerate((bo, ffn_bias, None, ln_w, ln_b, gate_bias[2 * P:3 * P])):
                src = w8_scale.rearrange("n o -> o n") if r is None else r.rearrange("(o n) -> o n", o=1)
                sp.dma_start(rows[:, n, :], src).then_inc(s["wl_rows"], 16)
            gb = gate_bias.rearrange("(g p o) -> g p o", p=P, o=1)
            for n, g in enumerate((0, 1, 3)):
                sp.dma_start(gate_b[:, n:n + 1], gb[g]).then_inc(s["wl_cols"], 16)
            sp.wait_ge(s["x_loaded"], 16)
            load_x(1, 1, first=True)
            sp.dma_start(w_nat[:, 4:8, :], Wgates.rearrange("(g p) d -> p g d", p=P)).then_inc(s["wl_gates"], 16)
            sp.dma_start(w8_raw[:].rearrange("p k w -> p (k w)"), W8.bitcast(I32)).then_inc(s["wl_int8"], 16)
            sp.dma_start(w_router[:], Wrouter).then_inc(s["wl_router"], 16)
            col = 0
            for routed, shared in ((W1, Ws1), (W2, Ws2)):
                sp.dma_start(w_ff[:, col:col + ROUTED].rearrange("c (e h) -> c e h", e=EXPERTS),
                              routed.rearrange("e c h -> c e h")).then_inc(s["wl_ff"], 16)
                sp.dma_start(w_ff[:, col + ROUTED:col + HALL], shared).then_inc(s["wl_ff"], 16)
                col += HALL
            sp.dma_start(w_ff[:, col:col + NJR * P].rearrange("p (j c) -> p j c", j=NJR),
                          W3.rearrange("e h c -> (e h) c").rearrange("(j p) c -> p j c", p=P)).then_inc(s["wl_ff"], 16)
            sp.dma_start(w_ff[:, col + NJR * P:col + (NJ - 1) * P].rearrange("p (j c) -> p j c", j=NJ - 1 - NJR),
                          Ws3[0:(NJ - 1 - NJR) * P, :].rearrange("(j p) c -> p j c", p=P)).then_inc(s["wl_ff"], 16)
            sp.wait_ge(s["ff_pad_zero"], 1)
            sp.dma_start(w_ff[0:LASTK, col + (NJ - 1) * P:col + NJ * P],
                          Ws3[(NJ - 1 - NJR) * P:HSH, :]).then_inc(s["wl_ff"], 16)
            with sp.Fori(1, PAIRS) as i:
                load_x(2 * i, 0)
                load_x(2 * i + 1, 1)

            def store(t):
                sp.wait_ge(s["x4_ready"], SUB * (t + 1))
                settled(sp)
                sp.dma_start(out_tiles[bass.ds(t, 1)].rearrange("o p s e -> (o p) s e"), x4[:])\
                  .then_inc(s["out_stored"], 16)

            with sp.Fori(0, NT) as t:
                store(t)
            sp.wait_ge(s["out_stored"], 16 * NT)

        @block.scalar
        def _(act):
            def weights_out(b):
                act.wait_ge(s["w_tr"], b + 1)
                nc.scalar.activation(wT[:, 4 * b:4 * b + 4, :], pb[(0, 6)[b]][:].rearrange("p (n c) -> p n c", n=4),
                                     ACT.Copy).then_inc(s["w_tr_copied"], 1)

            def rows_out():
                act.wait_ge(s["w_tr"], 3)
                act.wait_ge(s["rows_bc_ps"], 2)
                nc.scalar.activation(w8T[:], pb[7][:, 0:P], ACT.Copy).then_inc(s["w8T_ready"], 1)
                nc.scalar.activation(rows_bc[:, 0:4, :], pb[3][:].rearrange("p (n c) -> p n c", c=P), ACT.Copy)\
                  .then_inc(s["rows_bc_ready"], 1)
                nc.scalar.activation(rows_bc[:, 4:5, :], pb[7][:, P:2 * P].rearrange("p (n c) -> p n c", c=P), ACT.Copy)\
                  .then_inc(s["rows_bc_ready"], 1)

            def front(t, p, part):
                late = not (isinstance(t, int) and t == 0)
                if part == 0:
                    act.wait_ge(s["xT_ps"], t + 1)
                    act.wait_ge(s["v_ps"], t)
                    nc.scalar.activation(xT[:], ps_proj[:], ACT.Copy).then_inc(s["xT_ready"], 1)
                    act.wait_ge(s["k_ps"], t)
                    act.wait_ge(s["xTlo_ready"], t)
                    nc.scalar.activation(xT_hi[:], ps_proj[:], ACT.Copy).then_inc(s["xThi_ready"], 1)
                    act.wait_ge(s["v_ps"], t + 1)
                    if late:
                        act.wait_ge(s["kv_ps"], SUB * (t - 1))
                        act.wait_ge(s["vown_ready"], 16 * (t - 1))
                    act.wait_ge(s["v_ones"], 2)
                    nc.scalar.activation(v_tok[p][:].rearrange("p s h d -> p (s h) d")[:, :, 0:D],
                                         ps_proj[:].rearrange("p (n d) -> p n d", d=D), ACT.Copy)\
                      .then_inc(s["v_ready"], 1)
                elif part == 1:
                    act.wait_ge(s["q_ps"], t + 1)
                    act.wait_ge(s["k_ready"], t)
                    nc.scalar.activation(exp_qk[:], ps_proj[:], ACT.Exp).then_inc(s["expq_ready"], 1)
                elif part == 2:
                    act.wait_ge(s["k_ps"], t + 1)
                    act.wait_ge(s["q_ready"], t + 1)
                    nc.scalar.activation(exp_qk[:], ps_proj[:], ACT.Exp).then_inc(s["expk_ready"], 1)
                else:
                    act.wait_ge(s["ktok_ps"], t + 1)
                    if late:
                        act.wait_ge(s["kv_ps"], SUB * (t - 1))
                    nc.scalar.activation(k_tok[p][:].rearrange("p s d -> p (s d)"), ps_proj[:], ACT.Copy)\
                      .then_inc(s["ktok_ready"], 1)

            def own_values(t, p, b):
                if b == 0:
                    act.wait_ge(s["v_ready"], t + 1)
                    if not (isinstance(t, int) and t == 0):
                        act.wait_ge(s["attn_num_ps"], 4 * SUB * (t - 1))
                        settled(act)
                    else:
                        act.wait_ge(s["vown_set"], 10)
                for r in range(4):
                    nc.scalar.activation(v_own[p][32 * r:32 * r + 32, :, QUADS * b:QUADS * (b + 1), r, 0:D],
                                         v_tok[p][32 * b:32 * b + 32, :, r::4, 0:D],
                                         ACT.Copy).then_inc(s["vown_ready"], 1)

            def quads_apart(c, n, p, t):
                if n == 0:
                    act.wait_ge(s["q_ready"], t + 1)
                if isinstance(c, int) and c < 2:
                    act.wait_ge(s["quad_zero"], 2)
                else:
                    act.wait_ge(s["score_ps"], 4 * (c - 1))
                for g in range(QUADS):
                    rows32 = slice(32 * g, 32 * g + 32)
                    nc.scalar.activation(q_quad[n % 2][rows32, g, :], qT[p][rows32, CHUNK * n:CHUNK * (n + 1)],
                                         ACT.Copy).then_inc(s["qquad_ready"], 1)

            def chunk_turned(c):
                act.wait_ge(s["attnT_ps"], c + 1)
                act.wait_ge(s["wo_ps"], c)
                nc.scalar.activation(attnT[:], ps_attnT, ACT.Copy).then_inc(s["attnT_ready"], 1)

            def chunk_sums(c):
                act.wait_ge(s["attn_num_ps"], 4 * c + 4)
                act.wait_ge(s["num_turned"], c)
                nc.scalar.activation(numT[:], ps_numT[0:64 + QV], ACT.Copy).then_inc(s["numT_ready"], 1)

            def attn_norm(t, p):
                act.wait_ge(s["arstd_ready"], 2 * t + 2)
                act.wait_ge(s["astats_ready"], SUB * (t + 1))
                settled(act)
                for n in range(SUB):
                    nc.scalar.activation(x1_all[:, bass.ds(SUB * t + n, 1), :], y_attn[p][:, n:n + 1, :], ACT.Identity,
                                         bias=a_shift[:, n:n + 1], scale=a_rstd[:, n:n + 1]).then_inc(s["x1_ready"], 1)

            def attn_tile(t, p, last=False):
                for n in range(SUB):
                    c = SUB * t + n
                    begun = not (isinstance(c, int) and c == 0)
                    chunk_sums(c)
                    if begun:
                        chunk_turned(c - 1)
                    if not last:
                        front(t + 1, 1 - p, n)
                    if n < SUB - 2:
                        quads_apart(c + 2, n + 2, p, t)
                    elif not last:
                        quads_apart(c + 2, n + 2 - SUB, 1 - p, t + 1)
                    if not last:
                        for b in ((), (0, 1), (2,), (3,))[n]:
                            own_values(t + 1, 1 - p, b)
                    if n == 1 and not (isinstance(t, int) and t == 0):
                        attn_norm(t - 1, 1 - p)

            weights_out(0)
            for part in range(SUB):
                front(0, 0, part)
                if part == 1:
                    quads_apart(0, 0, 0, 0)
                    quads_apart(1, 1, 0, 0)
                if part == 2:
                    weights_out(1)
                    rows_out()
            for b in range(4):
                own_values(0, 0, b)
            attn_tile(0, 0)
            attn_tile(1, 1)
            with act.Fori(1, PAIRS - 1) as i:
                attn_tile(2 * i, 0)
                attn_tile(2 * i + 1, 1)
            attn_tile(NT - 2, 0)
            attn_tile(NT - 1, 1, last=True)
            chunk_turned(NC - 1)
            attn_norm(NT - 1, 1)

            def layer_norm(k, t, half, dst, src):
                act.wait_ge(rs_r[k], 2 * t + 2)
                for n in (2 * half, 2 * half + 1):
                    nc.scalar.activation(dst(n), src(n), ACT.Identity, bias=shift[k][:, n:n + 1],
                                         scale=rstd[k][:, n:n + 1]).then_inc(nm_r[k], 1)

            def recur(t, p, step, ps_a=ps_a):
                if step == 3:
                    act.wait_ge(s["xqT_ps"], t + 1)
                    act.wait_ge(s["q8_ps"], t)
                    nc.scalar.activation(xqT[:], ps_a[:], ACT.Copy, bias=-MAGIC).then_inc(s["xqT_ready"], 1)
                elif step in (11, 12):
                    if not (isinstance(t, int) and t < 2):
                        act.wait_ge(s["ylstm_ready"], t - 1)
                        act.wait_ge(s["x2T_ps"], t - 1)
                    layer_norm(0, t, step - 11, lambda n: x2[p][:, n, :], lambda n: y_ffn[:, n, :])
                elif step == 17:
                    act.wait_ge(s["x2T_ps"], t + 1)
                    act.wait_ge(s["z_ps"], t)
                    act.wait_ge(s["x2lo_ready"], t)
                    nc.scalar.activation(x2T_hi[:], ps_a[:], ACT.Copy).then_inc(s["x2hi_ready"], 1)
                    act.wait_ge(s["o_ps"], t)
                    nc.scalar.activation(x2T[:], ps_a[:], ACT.Copy).then_inc(s["x2T_ready"], 1)
                elif step == 19:
                    act.wait_ge(s["f_ps"], t + 1)
                    act.wait_ge(s["f_ready"], t)
                    nc.scalar.activation(tanh_f[:], ps_a[:], ACT.Tanh, bias=gate_bh[:, 0:1], scale=0.5)\
                      .then_inc(s["tf_ready"], 1)
                elif step == 21:
                    act.wait_ge(s["i_ps"], t + 1)
                    act.wait_ge(s["iz_ready"], t)
                    nc.scalar.activation(tanh_i[:], ps_a[:], ACT.Tanh, bias=gate_bh[:, 1:2], scale=0.5)\
                      .then_inc(s["ti_ready"], 1)
                elif step == 23:
                    act.wait_ge(s["z_ps"], t + 1)
                    nc.scalar.activation(tanh_z[:], ps_a[:], ACT.Tanh, bias=gate_b[:, 2:3])\
                      .then_inc(s["tz_ready"], 1)
                elif step == 26:
                    act.wait_ge(s["o_ps"], t + 1)
                    if not (isinstance(t, int) and t < 2):
                        act.wait_ge(s["h2_ready"], t - 1)
                    nc.scalar.activation(tanh_o[p][:].rearrange("p s e -> p (s e)"), ps_a[:], ACT.Tanh, scale=0.5)\
                      .then_inc(s["to_ready"], 1)

            def emit(t, p, step):
                if step in (6, 7):
                    act.wait_ge(s["caff_ready"], t)
                    layer_norm(1, t, step - 6, lambda n: c_norm[:, n, :], lambda n: ps_b[:, P * n:P * n + P])
                elif step == 9:
                    act.wait_ge(s["caff_ready"], t + 1)
                    act.wait_ge(s["h2_ready"], t)
                    nc.scalar.activation(tanh_c[:], c_aff[:], ACT.Tanh).then_inc(s["tc_ready"], 1)
                elif step in (15, 16):
                    if not (isinstance(t, int) and t < 2):
                        act.wait_ge(s["ymoe_ready"], t - 1)
                    layer_norm(2, t, step - 15, lambda n: x3[p][:, n, :], lambda n: y_lstm[:, n, :])
                elif step == 17:
                    act.wait_ge(s["x3T_ps"], t + 1)
                    if not (isinstance(t, int) and t < 2):
                        act.wait_ge(s["u_ps"], NJ * (t - 1))
                    nc.scalar.activation(x3T_hi[p][:], ps_b[:], ACT.Copy).then_inc(s["x3hi_ready"], 1)
                elif step == 23:
                    act.wait_ge(s["gap_ready"], t + 1)
                    act.wait_ge(s["route_step"], ROUTE * t)
                    nc.scalar.activation(tanh_gap[:], gap[:], ACT.Tanh, scale=0.5).then_inc(s["tgap_ready"], 1)
                elif step == 27:
                    act.wait_ge(s["wT_ps"], t + 1)
                    if not (isinstance(t, int) and t < 2):
                        act.wait_ge(s["w_ps"], NJR * (t - 1))
                    nc.scalar.activation(w_partsT[p][:], ps_b[0:16, :], ACT.Copy).then_inc(s["wT_ready"], 1)

            def block_silu(t, p, j):
                n = NJ * t + j
                m = units(j)
                act.wait_ge(s["g_ps"], n + 1)
                if not (isinstance(n, int) and n < 2):
                    act.wait_ge(s["hid_ready"], n - 1)
                nc.scalar.activation(silu_g[j % 2][0:m], ps_g[j % 3][0:m], ACT.Silu).then_inc(s["silu_ready"], 1)

            def block_high(t, p, j):
                n = NJ * t + j
                b = (NJ * p + j) % 4
                m = units(j)
                act.wait_ge(s["hid_ready"], n + 1)
                if not (isinstance(n, int) and n < 4):
                    act.wait_ge(s["down_ps"], n - 3)
                    act.wait_ge(s["lo_ready"], n - 3)
                nc.scalar.activation(hid_hi[b][0:m], hid[j % 2][0:m], ACT.Copy).then_inc(s["hi_ready"], 1)

            def finish(t):
                act.wait_ge(s["down_ps"], NJ * (t + 1))
                act.wait_ge(s["y_ps"], t)
                nc.scalar.activation(yT[:], ps_y[:], ACT.Copy).then_inc(s["yT_ready"], 1)

            def finish_norm(t, half):
                act.wait_ge(s["out_stored"], 16 * t)
                layer_norm(3, t, half, lambda n: x4[:, n, :], lambda n: y_moe[:, n, :])

            def moe_tile(t, p, last=False):
                begun = not (isinstance(t, int) and t == 0)
                for j in range(NJ):
                    if j == 0 and begun:
                        finish(t - 1)
                    if not last:
                        recur(t + 2, p, 2 * j)
                        emit(t + 1, 1 - p, 2 * j)
                    if j in (11, 12) and begun:
                        finish_norm(t - 1, j - 11)
                    ahead = j + AHEAD
                    if ahead < NJ:
                        block_silu(t, p, ahead)
                        block_high(t, p, ahead - 1)
                    elif not last:
                        block_silu(t + 1, 1 - p, ahead - NJ)
                        if ahead == NJ:
                            block_high(t, p, NJ - 1)
                        else:
                            block_high(t + 1, 1 - p, ahead - NJ - 1)
                    elif ahead == NJ:
                        block_high(t, p, NJ - 1)
                    if not last:
                        recur(t + 2, p, 2 * j + 1)
                        emit(t + 1, 1 - p, 2 * j + 1)

            act.wait_ge(s["gate_bh_ready"], 1)
            for step in range(2 * STEPS):
                if step < STEPS:
                    recur(0, 0, step)
                if step >= STEPS:
                    emit(0, 0, step - STEPS)
                if 0 <= step - LAG < STEPS:
                    recur(1, 1, step - LAG, ps_a=ps_a2)
                for j in range(AHEAD):
                    if step == STEPS + first_block + 2 * j:
                        block_silu(0, 0, j)
                        if j:
                            block_high(0, 0, j - 1)
            moe_tile(0, 0)
            moe_tile(1, 1)
            with act.Fori(1, PAIRS - 1) as i:
                moe_tile(2 * i, 0)
                moe_tile(2 * i + 1, 1)
            moe_tile(NT - 2, 0)
            moe_tile(NT - 1, 1, last=True)
            finish(NT - 1)
            finish_norm(NT - 1, 0)
            finish_norm(NT - 1, 1)

        @block.gpsimd
        def _(pool):
            nc.gpsimd.memset(ident[:], 0.0).then_inc(s["z_set"], 1)
            nc.gpsimd.memset(causal[:], 1.0).then_inc(s["z_set"], 1)
            nc.gpsimd.memset(head_of[:], 1.0).then_inc(s["z_set"], 1)
            pool.wait_ge(s["z_set"], 3)
            nc.gpsimd.affine_select(out=ident[:], in_=ident[:], compare_op=ALU.not_equal, fill=1.0, base=0,
                                    pattern=[[-1, P]], channel_multiplier=1).then_inc(s["one_set"], 1)
            nc.gpsimd.memset(x1_all[:, NC:NC + SUB, :], 0.0).then_inc(s["one_set"], 1)
            nc.gpsimd.affine_select(out=head_of_2[:], in_=head_of[:], compare_op=ALU.is_ge, fill=0.0, base=0,
                                    pattern=[[-4 * D, QUADS], [-D, 4]], channel_multiplier=1).then_inc(s["one_set"], 1)
            pool.wait_ge(s["one_set"], 3)
            nc.gpsimd.affine_select(out=head_of[:], in_=head_of_2[:], compare_op=ALU.is_ge, fill=0.0, base=D - 1,
                                    pattern=[[4 * D, QUADS], [D, 4]], channel_multiplier=-1).then_inc(s["one_set"], 1)
            nc.gpsimd.memset(ones_row[:], 1.0).then_inc(s["one_set"], 1)
            pool.wait_ge(s["one_set"], 5)
            nc.gpsimd.memset(minus_half[:], -0.5).then_inc(s["consts_ready"], 1)
            pool.wait_ge(s["consts_ready"], 1)
            nc.gpsimd.memset(w_ff[96:P, W_COLS - P:W_COLS], 0.0).then_inc(s["ff_pad_zero"], 1)
            pool.wait_ge(s["ff_pad_zero"], 1)
            for p in range(2):
                nc.gpsimd.memset(v_tok[p][:], 1.0).then_inc(s["v_ones"], 1)
            for r in range(4):
                part = causal[32 * r:32 * r + 32, :]
                nc.gpsimd.affine_select(out=part, in_=part, compare_op=ALU.is_ge, fill=0.0, base=0,
                                        pattern=[[1, CHUNK]], channel_multiplier=-1).then_inc(s["span_set"], 1)
                pool.wait_ge(s["span_set"], r + 1)
            def x_low(t):
                pool.wait_ge(s["xThi_ready"], t + 1)
                pool.wait_ge(s["k_ps"], t)
                settled(pool)
                nc.gpsimd.tensor_tensor(xT_lo[:], xT[:], xT_hi[:].bitcast(F32), ALU.subtract)\
                  .then_inc(s["xTlo_ready"], 1)

            x_low(0)
            for n in range(2):
                nc.gpsimd.memset(q_quad[n][:], 0.0).then_inc(s["quad_zero"], 1)
            for p in range(2):
                nc.gpsimd.memset(v_own[p][:], 0.0).then_inc(s["vown_set"], 1)
            pool.wait_ge(s["vown_set"], 2)
            for p in range(2):
                for r in range(4):
                    nc.gpsimd.memset(v_own[p][32 * r:32 * r + 32, :, :, r, D:DV], 1.0).then_inc(s["vown_set"], 1)
                    pool.wait_ge(s["vown_set"], 3 + 4 * p + r)
            nc.gpsimd.memset(state[:], 0.0).then_inc(s["state_zero"], 1)
            nc.gpsimd.memset(carry[:], 0.0).then_inc(s["state_zero"], 1)
            nc.gpsimd.memset(keep[:], 1.0).then_inc(s["state_zero"], 1)
            pool.wait_ge(s["state_zero"], 3)
            nc.gpsimd.memset(keep[:, TPB // 2 - 1:TPB // 2], 0.0).then_inc(s["state_zero"], 1)

            def keep_residual(t, p):
                pool.wait_ge(s["x_loaded"], 16 * (t + 1))
                if not (isinstance(t, int) and t == 0):
                    pool.wait_ge(s["yattn_ready"], SUB * (t - 1))
                settled(pool)
                nc.gpsimd.tensor_tensor(x_bo[p][:], x_cur[p][:],
                                        rows_bc[:, 0:1, :].to_broadcast([P, SUB, E]), ALU.add)\
                  .then_inc(s["xbo_ready"], 1)

            def split_heads(t, p):
                pool.wait_ge(s["k_ready"], t + 1)
                if not (isinstance(t, int) and t == 0):
                    pool.wait_ge(s["score_ps"], 4 * SUB * (t - 1))
                settled(pool)
                for r in (2, 3):
                    nc.gpsimd.tensor_scalar(k_heads[p][:, :, r, :], kT[p][:].rearrange("p (q j) -> p q j", j=32),
                                            in_quad[:, r:r + 1], 1.0, ALU.mult, ALU.mult)\
                      .then_inc(s["kheads_p"], 1)

            def attn_rstd(t):
                pool.wait_ge(s["amv_ready"], SUB * (t + 1))
                pool.wait_ge(s["x1_ready"], SUB * t)
                settled(pool)
                nc.gpsimd.tensor_scalar(a_var[:], a_mv[:, :, 1], LN_EPS, 1.0, ALU.add, ALU.mult)\
                  .then_inc(s["avar_ready"], 1)
                nc.gpsimd.tensor_scalar(a_minus[:], a_mv[:, :, 0], -1.0, 1.0, ALU.mult, ALU.mult)\
                  .then_inc(s["avar_ready"], 1)
                pool.wait_ge(s["avar_ready"], 2 * t + 2)
                settled(pool)
                nc.gpsimd.tensor_tensor(a_rstd[:], a_var[:], minus_half[:], ALU.pow).then_inc(s["arstd_ready"], 1)
                pool.wait_ge(s["arstd_ready"], 2 * t + 1)
                settled(pool)
                nc.gpsimd.tensor_tensor(a_shift[:], a_minus[:], a_rstd[:], ALU.mult).then_inc(s["arstd_ready"], 1)

            def split_weights(t):
                cols = bass.ds(t * WSLICE, WSLICE)
                nc.gpsimd.tensor_copy(w_hi[:, cols], w_ff[:, cols]).then_inc(s["ff_hi"], 1)
                pool.wait_ge(s["ff_hi"], t + 1)
                settled(pool)
                nc.gpsimd.tensor_tensor(w_lo[:, cols], w_ff[:, cols], w_hi[:, cols].bitcast(F32), ALU.subtract)\
                  .then_inc(s["ff_split"], 1)

            pool.wait_ge(s["quad_ready"], 1)
            split_heads(0, 0)
            pool.wait_ge(s["rows_bc_ready"], 2)
            keep_residual(0, 0)
            nc.gpsimd.iota(rev_index[:], pattern=[[0, SUB], [-1, EXPERTS]], base=EXPERTS, channel_multiplier=0,
                           allow_small_or_imprecise_dtypes=True).then_inc(s["consts_ready"], 1)
            pool.wait_ge(s["wl_router"], 16)
            nc.gpsimd.tensor_copy(w_router_hi[:], w_router[:]).then_inc(s["router_hi"], 1)
            pool.wait_ge(s["router_hi"], 1)
            nc.gpsimd.tensor_tensor(w_router_lo[:], w_router[:], w_router_hi[:].bitcast(F32), ALU.subtract)\
              .then_inc(s["router_ready"], 1)
            pool.wait_ge(s["wl_ff"], 16 * 7)

            def attn_tile(t, p, last=False):
                if not last:
                    x_low(t + 1)
                if not (isinstance(t, int) and t == 0):
                    attn_rstd(t - 1)
                if not last:
                    split_heads(t + 1, 1 - p)
                    keep_residual(t + 1, 1 - p)
                split_weights(t)

            def select_experts(n):
                e0 = EXPERTS * n
                nc.gpsimd.memset(sel16[:], 1.0).then_inc(s["sel_r_ready"], 1)
                pool.wait_ge(s["sel_r_ready"], 4 * n + 1)
                nc.gpsimd.affine_select(out=sel16[:], in_=sel16[:], compare_op=ALU.is_ge, fill=0.0, base=HID * e0,
                                        pattern=[[1, ROUTED]], channel_multiplier=-HID).then_inc(s["sel_r_ready"], 1)
                pool.wait_ge(s["sel_r_ready"], 4 * n + 2)
                nc.gpsimd.affine_select(out=sel16[:], in_=sel16[:], compare_op=ALU.is_ge, fill=0.0,
                                        base=HID - 1 - HID * e0,
                                        pattern=[[-1, ROUTED]], channel_multiplier=HID).then_inc(s["sel_r_ready"], 1)
                pool.wait_ge(s["sel_r_ready"], 4 * n + 3)
                if n == 0:
                    nc.gpsimd.tensor_copy(sel16_r[:], sel16[:]).then_inc(s["sel_r_ready"], 1)
                else:
                    nc.gpsimd.tensor_tensor(sel16_r[:], sel16_r[:].bitcast(F32), sel16[:], ALU.add)\
                      .then_inc(s["sel_r_ready"], 1)
                pool.wait_ge(s["sel_r_ready"], 4 * n + 4)

            attn_tile(0, 0)
            select_experts(0)
            attn_tile(1, 1)
            select_experts(1)
            with pool.Fori(1, PAIRS - 1) as i:
                attn_tile(2 * i, 0)
                attn_tile(2 * i + 1, 1)
            attn_tile(NT - 2, 0)
            attn_tile(NT - 1, 1, last=True)
            attn_rstd(NT - 1)

            pool.wait_ge(s["amax1_ready"], 1)
            nc.gpsimd.partition_all_reduce(amax_all[:], amax1[:], P, bass.bass_isa.ReduceOp.max)\
              .then_inc(s["amax_all_ready"], 1)

            def norm_std(k, t, eps):
                pool.wait_ge(mv_r[k], SUB * (t + 1))
                pool.wait_ge(nm_r[k], SUB * t)
                settled(pool)
                nc.gpsimd.tensor_scalar(var_eps[k][:], mv[k][:, :, 1], eps, 1.0, ALU.add, ALU.mult)\
                  .then_inc(ve_r[k], 1)
                nc.gpsimd.tensor_scalar(minus[k][:], mv[k][:, :, 0], -1.0, 1.0, ALU.mult, ALU.mult).then_inc(ve_r[k], 1)
                pool.wait_ge(ve_r[k], 2 * t + 2)
                settled(pool)
                nc.gpsimd.tensor_tensor(rstd[k][:], var_eps[k][:], minus_half[:], ALU.pow).then_inc(rs_r[k], 1)
                pool.wait_ge(rs_r[k], 2 * t + 1)
                settled(pool)
                nc.gpsimd.tensor_tensor(shift[k][:], minus[k][:], rstd[k][:], ALU.mult).then_inc(rs_r[k], 1)

            def recur(t, p, step):
                if step == 0:
                    pool.wait_ge(s["yffn_ready"], t)
                    settled(pool)
                    nc.gpsimd.tensor_tensor(x1_b[:], x1_all[:, bass.ds(SUB * t, SUB), :],
                                            rows_bc[:, 1:2, :].to_broadcast([P, SUB, E]), ALU.add)\
                      .then_inc(s["x1b_ready"], 1)
                elif step == 9:
                    norm_std(0, t, LN_EPS)
                elif step == 21:
                    pool.wait_ge(s["tf_ready"], t + 1)
                    pool.wait_ge(s["cell_ready"], t)
                    settled(pool)
                    nc.gpsimd.tensor_scalar(f_gate[:], tanh_f[:], 1.0, 0.5, ALU.add, ALU.mult)\
                      .then_inc(s["f_ready"], 1)

            def emit(t, p, step):
                if step == 3:
                    norm_std(1, t, 4 * LN_EPS)
                elif step == 13:
                    norm_std(2, t, LN_EPS)

            def block_low(t, p, j):
                n = NJ * t + j
                b = (NJ * p + j) % 4
                m = units(j)
                pool.wait_ge(s["hi_ready"], n + 1)
                if not (isinstance(n, int) and n < 4):
                    pool.wait_ge(s["down_ps"], n - 3)
                settled(pool)
                nc.gpsimd.tensor_tensor(hid_lo[b][0:m], hid[j % 2][0:m], hid_hi[b][0:m].bitcast(F32), ALU.subtract)\
                  .then_inc(s["lo_ready"], 1)

            def moe_tile(t, p, last=False):
                for j in range(NJ):
                    if not last:
                        recur(t + 2, p, 2 * j)
                        emit(t + 1, 1 - p, 2 * j)
                    ahead = j + AHEAD
                    if ahead <= NJ:
                        block_low(t, p, ahead - 1)
                    elif not last:
                        block_low(t + 1, 1 - p, ahead - NJ - 1)
                    if j == 8 and not (isinstance(t, int) and t == 0):
                        norm_std(3, t - 1, LN_EPS)
                    if not last:
                        recur(t + 2, p, 2 * j + 1)
                        emit(t + 1, 1 - p, 2 * j + 1)

            for step in range(2 * STEPS):
                if step < STEPS:
                    recur(0, 0, step)
                if step >= STEPS:
                    emit(0, 0, step - STEPS)
                if 0 <= step - LAG < STEPS:
                    recur(1, 1, step - LAG)
                for j in range(1, AHEAD):
                    if step == STEPS + first_block + 2 * j:
                        block_low(0, 0, j - 1)
            moe_tile(0, 0)
            moe_tile(1, 1)
            with pool.Fori(1, PAIRS - 1) as i:
                moe_tile(2 * i, 0)
                moe_tile(2 * i + 1, 1)
            moe_tile(NT - 2, 0)
            moe_tile(NT - 1, 1, last=True)
            norm_std(3, NT - 1, LN_EPS)

        @block.vector
        def _(dve):
            dve.wait_ge(s["consts_ready"], 1)
            nc.vector.tensor_reduce(in_quad[:], head_of[:].rearrange("p g r -> p r g"), AX.X, ALU.add)\
              .then_inc(s["quad_ready"], 1)
            def split_turned(b):
                dve.wait_ge(s["w_tr_copied"], b + 1)
                nc.vector.tensor_copy(wT_hi[:, 4 * b:4 * b + 4, :], wT[:, 4 * b:4 * b + 4, :]).then_inc(s["wT_hi_ready"], 1)
                dve.wait_ge(s["wT_hi_ready"], b + 1)
                nc.vector.tensor_tensor(wT_lo[:, 4 * b:4 * b + 4, :], wT[:, 4 * b:4 * b + 4, :],
                                        wT_hi[:, 4 * b:4 * b + 4, :].bitcast(F32), ALU.subtract).then_inc(s["wT_split"], 1)

            def parameters():
                dve.wait_ge(s["wl_rows"], 16 * 6)
                nc.vector.tensor_copy(o_bias_hi[:], rows[:, 5:6, :].to_broadcast([1, SUB, P]))\
                  .then_inc(s["o_bias_hi_ready"], 1)
                dve.wait_ge(s["o_bias_hi_ready"], 1)
                nc.vector.tensor_tensor(o_bias_lo[:], rows[:, 5:6, :].to_broadcast([1, SUB, P]), o_bias_hi[:].bitcast(F32),
                                        ALU.subtract).then_inc(s["o_bias_ready"], 1)
                nc.vector.tensor_copy(ones_r[:], ones_row[:]).then_inc(s["o_bias_ready"], 1)
                dve.wait_ge(s["wl_cols"], 16 * 3)
                nc.vector.tensor_scalar(gate_bh[:], gate_b[:, 0:2], 0.5, None, ALU.mult).then_inc(s["gate_bh_ready"], 1)
                dve.wait_ge(s["state_zero"], 4)
                dve.wait_ge(s["quad_ready"], 1)

            own_head = head_of[:].rearrange("p g r -> p (g r)").unsqueeze(2).to_broadcast([P, HEADS, DV])

            def front_q(t, p):
                dve.wait_ge(s["expq_ready"], t + 1)
                nc.vector.tensor_scalar(exp_qk[:], exp_qk[:], 1.0, None, ALU.min).then_inc(s["expq_min"], 1)
                dve.wait_ge(s["expq_min"], t + 1)
                if not (isinstance(t, int) and t == 0):
                    dve.wait_ge(s["attn_num_ps"], 4 * SUB * (t - 1))
                nc.vector.scalar_tensor_tensor(qT[p][:], ps_proj[:], 0.0, exp_qk[:], ALU.max, ALU.add)\
                  .then_inc(s["q_ready"], 1)

            def front_heads(t, p):
                dve.wait_ge(s["k_ready"], t + 1)
                for r in (0, 1):
                    nc.vector.tensor_scalar(k_heads[p][:, :, r, :], kT[p][:].rearrange("p (q j) -> p q j", j=32),
                                            in_quad[:, r:r + 1], None, ALU.mult)\
                      .then_inc(s["kheads_v"], 1)

            def front_k(t, p):
                dve.wait_ge(s["expk_ready"], t + 1)
                nc.vector.tensor_scalar(exp_qk[:], exp_qk[:], 1.0, None, ALU.min).then_inc(s["expk_min"], 1)
                dve.wait_ge(s["expk_min"], t + 1)
                if not (isinstance(t, int) and t == 0):
                    dve.wait_ge(s["score_ps"], 4 * SUB * (t - 1))
                    dve.wait_ge(s["kheads_p"], 2 * (t - 1))
                    dve.wait_ge(s["ktok_ps"], t - 1)
                nc.vector.scalar_tensor_tensor(kT[p][:], ps_proj[:], 0.0, exp_qk[:], ALU.max, ALU.add)\
                  .then_inc(s["k_ready"], 1)

            def mask(c, b):
                span = CHUNK - 32 * b
                by_quad = lambda a: a.rearrange("p (g i) -> p g i", g=QUADS)
                dve.wait_ge(s["score_ps"], 4 * c + b + 1)
                if not (isinstance(c, int) and c == 0):
                    dve.wait_ge(s["attn_num_ps"], 4 * (c - 1) + b + 1)
                nc.vector.tensor_tensor(by_quad(scores[b][:]), by_quad(ps_scores[b][:, 0:QUADS * span]),
                                        causal[:, 0:span].unsqueeze(1).to_broadcast([P, QUADS, span]), ALU.mult)\
                  .then_inc(s["masked"], 1)

            def state_of(par):
                return state[:, par, :, 0:QV]

            def quads(a):
                return a[:].rearrange("p (g d) -> p g d", g=QUADS)

            def update_state(c, par, ends_row=None):
                dve.wait_ge(s["kv_ps"], c + 1)
                dve.wait_ge(s["state_ready"], c)
                nc.vector.tensor_tensor(kv_own[:].rearrange("p (h d) -> p h d", h=HEADS),
                                        ps_kv.rearrange("p (h d) -> p h d", h=HEADS), own_head, ALU.mult)\
                  .then_inc(s["kv_own_ready"], 1)
                dve.wait_ge(s["kv_own_ready"], c + 1)
                if ends_row is None:
                    nc.vector.tensor_tensor(state_of(1 - par), state_of(par), quads(kv_own), ALU.add)\
                      .then_inc(s["state_ready"], 1)
                else:
                    nc.vector.tensor_tensor(quads(kv_sum), state_of(par), quads(kv_own), ALU.add)\
                      .then_inc(s["state_kept"], 1)
                    dve.wait_ge(s["state_kept"], ends_row + 1)
                    settled(dve)
                    nc.vector.tensor_scalar(state_of(1 - par), quads(kv_sum), keep[:, bass.ds(ends_row, 1)], None,
                                            ALU.mult).then_inc(s["state_ready"], 1)

            def normalise(c):
                num = ps_num.rearrange("p (g d) -> p g d", g=QUADS)[:, :, 0:QV].rearrange("p g (r d) -> p g r d", r=4)
                by_quad = lambda a: a[:].rearrange("p (g r) -> p g r", g=QUADS)
                dve.wait_ge(s["num_turned"], c + 1)
                dve.wait_ge(s["rden_ready"], c)
                nc.vector.tensor_scalar(by_quad(den), num[:, :, :, D], DEN_EPS, None, ALU.add)\
                  .then_inc(s["den_ready"], 1)
                dve.wait_ge(s["den_ready"], c + 1)
                dve.wait_ge(s["attn_ready"], c)
                nc.vector.reciprocal(rden[:], den[:]).then_inc(s["rden_ready"], 1)
                dve.wait_ge(s["rden_ready"], c + 1)
                dve.wait_ge(s["attnT_ps"], c)
                nc.vector.tensor_tensor(attn[:].rearrange("p (g r) d -> p g r d", g=QUADS), num[:, :, :, 0:D],
                                        by_quad(rden).unsqueeze(3).to_broadcast([P, QUADS, 4, D]), ALU.mult)\
                  .then_inc(s["attn_ready"], 1)

            def residual(t, p, n):
                c = SUB * t + n
                dve.wait_ge(s["wo_ps"], c + 1)
                dve.wait_ge(s["xbo_ready"], t + 1)
                if not (isinstance(t, int) and t == 0):
                    dve.wait_ge(s["x1_ready"], SUB * (t - 1))
                nc.vector.tensor_tensor(y_attn[p][:, n, :], ps_wo, x_bo[p][:, n, :], ALU.add)\
                  .then_inc(s["yattn_ready"], 1)
                dve.wait_ge(s["yattn_ready"], c + 1)
                dve.wait_ge(s["amv_ready"], SUB * t)
                nc.vector.bn_stats(a_stats[:, n, :], y_attn[p][:, n, :]).then_inc(s["astats_ready"], 1)

            def attn_spread(t):
                for n in range(SUB):
                    dve.wait_ge(s["astats_ready"], SUB * t + n + 1)
                    dve.wait_ge(s["avar_ready"], 2 * t)
                    settled(dve)
                    nc.vector.bn_aggr(a_mv[:, n, :], a_stats[:, n, :]).then_inc(s["amv_ready"], 1)

            def largest(t):
                dve.wait_ge(s["x1_ready"], SUB * (t + 1))
                settled(dve)
                nc.vector.tensor_reduce(amax[:, bass.ds(t, 1)], x1_all[:, bass.ds(SUB * t, SUB), :]
                                        .rearrange("p s e -> p (s e)"), AX.X, ALU.max,
                                        apply_absolute_value=True).then_inc(s["amax_ready"], 1)

            def attn_tile(t, p, i, last=False):
                for n in range(SUB):
                    c = SUB * t + n
                    begun = not (isinstance(c, int) and c == 0)
                    more = not (last and n == SUB - 1)
                    if begun:
                        normalise(c - 1)
                    update_state(c, n % 2, ends_row=i if (p == 1 and n == SUB - 1) else None)
                    if more:
                        mask(c + 1, 0)
                        mask(c + 1, 1)
                    if begun:
                        if n == 0:
                            residual(t - 1, 1 - p, SUB - 1)
                        else:
                            residual(t, p, n - 1)
                    if more:
                        mask(c + 1, 2)
                        mask(c + 1, 3)
                    if begun and n == 0:
                        attn_spread(t - 1)
                    if not last and n == 1:
                        front_q(t + 1, 1 - p)
                    if not last and n == 2:
                        front_k(t + 1, 1 - p)
                        front_heads(t + 1, 1 - p)
                    if n == 0 and not (isinstance(t, int) and t < 2):
                        largest(t - 2)

            split_turned(0)
            dve.wait_ge(s["wl_int8"], 16)
            nc.vector.tensor_copy(w_nat[:, 8, :], w8_raw[:, :, 0]).then_inc(s["w8_cast"], 1)
            front_q(0, 0)
            front_k(0, 0)
            front_heads(0, 0)
            parameters()
            split_turned(1)
            dve.wait_ge(s["span_set"], 4)
            for b in range(4):
                mask(0, b)
            attn_tile(0, 0, None)
            attn_tile(1, 1, 0)
            with dve.Fori(1, PAIRS - 1) as i:
                attn_tile(2 * i, 0, None)
                attn_tile(2 * i + 1, 1, i)
            attn_tile(NT - 2, 0, None)
            attn_tile(NT - 1, 1, PAIRS - 1, last=True)
            normalise(NC - 1)
            residual(NT - 1, 1, SUB - 1)
            attn_spread(NT - 1)
            largest(NT - 2)
            largest(NT - 1)

            dve.wait_ge(s["amax_ready"], NT)
            nc.vector.tensor_reduce(amax1[:], amax[:], AX.X, ALU.max).then_inc(s["amax1_ready"], 1)
            dve.wait_ge(s["amax_all_ready"], 1)
            nc.vector.tensor_scalar(x_scale[:], amax_all[:], 1.0 / 127.0, SCALE_EPS, ALU.mult, ALU.max)\
              .then_inc(s["scale_ready"], 1)
            dve.wait_ge(s["scale_ready"], 1)
            nc.vector.reciprocal(inv_scale[:], x_scale[:]).then_inc(s["scale_ready"], 1)
            nc.vector.tensor_scalar(deq_scale[:], rows_bc[:, 2, :], x_scale[:], None, ALU.mult)\
              .then_inc(s["deq_ready"], 1)
            dve.wait_ge(s["scale_ready"], 2)
            dve.wait_ge(s["deq_ready"], 1)

            dve.wait_ge(s["consts_ready"], 2)

            def layer_stats(k, t, src):
                for n in range(SUB):
                    dve.wait_ge(mv_r[k], SUB * t)
                    nc.vector.bn_stats(stats[k][:, n, :], src(n)).then_inc(st_r[k], 1)
                for n in range(SUB):
                    dve.wait_ge(st_r[k], SUB * t + n + 1)
                    dve.wait_ge(ve_r[k], 2 * t)
                    settled(dve)
                    nc.vector.bn_aggr(mv[k][:, n, :], stats[k][:, n, :]).then_inc(mv_r[k], 1)

            def recur(t, p, k, step, ps_a=ps_a):
                if step == 0:
                    dve.wait_ge(s["xqT_ps"], t)
                    settled(dve)
                    nc.vector.tensor_scalar(xq[:], x1_all[:, bass.ds(SUB * t, SUB), :], inv_scale[:], MAGIC,
                                            ALU.mult, ALU.add).then_inc(s["xq_round"], 1)
                    dve.wait_ge(s["xq_round"], t + 1)
                    nc.vector.tensor_scalar(xq[:], xq[:], MAGIC - 128.0, MAGIC + 127.0, ALU.max, ALU.min)\
                      .then_inc(s["xq_ready"], 1)
                elif step == 5:
                    dve.wait_ge(s["q8_ps"], t + 1)
                    dve.wait_ge(nm_r[0], SUB * t)
                    nc.vector.tensor_tensor(y_ffn[:], ps_a[:].rearrange("p (s e) -> p s e", s=SUB),
                                            deq_scale[:].unsqueeze(1).to_broadcast([P, SUB, E]), ALU.mult)\
                      .then_inc(s["deq_done"], 1)
                    dve.wait_ge(s["deq_done"], t + 1)
                    dve.wait_ge(s["x1b_ready"], t + 1)
                    nc.vector.tensor_tensor(y_ffn[:], y_ffn[:], x1_b[:], ALU.add).then_inc(s["yffn_ready"], 1)
                    dve.wait_ge(s["yffn_ready"], t + 1)
                elif step == 8:
                    layer_stats(0, t, lambda n: y_ffn[:, n, :])
                elif step == 18:
                    dve.wait_ge(s["x2hi_ready"], t + 1)
                    dve.wait_ge(s["x2T_ready"], t + 1)
                    dve.wait_ge(s["z_ps"], t)
                    nc.vector.tensor_tensor(x2T_lo[:], x2T[:], x2T_hi[:].bitcast(F32), ALU.subtract)\
                      .then_inc(s["x2lo_ready"], 1)
                elif step == 25:
                    dve.wait_ge(s["ti_ready"], t + 1)
                    dve.wait_ge(s["tz_ready"], t + 1)
                    dve.wait_ge(s["cell_ready"], t)
                    nc.vector.scalar_tensor_tensor(iz2[:], tanh_i[:], 1.0, tanh_z[:], ALU.add, ALU.mult)\
                      .then_inc(s["iz_ready"], 1)
                    dve.wait_ge(s["iz_ready"], t + 1)
                    dve.wait_ge(s["f_ready"], t + 1)
                    dve.wait_ge(s["carry_ready"], t)
                    if not (isinstance(t, int) and t < 2):
                        dve.wait_ge(s["cellT_ps"], t - 1)
                    nc.vector.tensor_tensor_scan(cell2[p][:], f_gate[:], iz2[:], carry[:], ALU.mult, ALU.add)\
                      .then_inc(s["cell_ready"], 1)
                    dve.wait_ge(s["cell_ready"], t + 1)
                    if p == 1:
                        settled(dve)
                        nc.vector.tensor_scalar(carry[:], cell2[p][:, TILE - 1:TILE], keep[:, bass.ds(k, 1)], None,
                                                ALU.mult).then_inc(s["carry_ready"], 1)
                    else:
                        nc.vector.tensor_copy(carry[:], cell2[p][:, TILE - 1:TILE]).then_inc(s["carry_ready"], 1)

            def emit(t, p, step):
                if step == 1:
                    dve.wait_ge(s["cellT_ps"], t + 1)
                    layer_stats(1, t, lambda n: ps_b[:, P * n:P * n + P])
                elif step == 8:
                    dve.wait_ge(nm_r[1], SUB * (t + 1))
                    nc.vector.tensor_tensor(c_norm[:], c_norm[:], rows_bc[:, 3:4, :].to_broadcast([P, SUB, E]), ALU.mult)\
                      .then_inc(s["cscaled"], 1)
                    dve.wait_ge(s["cscaled"], t + 1)
                    dve.wait_ge(s["tc_ready"], t)
                    nc.vector.tensor_tensor(c_aff[:], c_norm[:], rows_bc[:, 4:5, :].to_broadcast([P, SUB, E]), ALU.add)\
                      .then_inc(s["caff_ready"], 1)
                elif step == 10:
                    dve.wait_ge(s["tc_ready"], t + 1)
                    dve.wait_ge(s["to_ready"], t + 1)
                    dve.wait_ge(s["ylstm_ready"], t)
                    nc.vector.scalar_tensor_tensor(h2[:], tanh_o[p][:], 1.0, tanh_c[:], ALU.add, ALU.mult)\
                      .then_inc(s["h2_ready"], 1)
                    dve.wait_ge(s["h2_ready"], t + 1)
                    dve.wait_ge(nm_r[2], SUB * t)
                    nc.vector.scalar_tensor_tensor(y_lstm[:], h2[:], 0.5, x2[p][:], ALU.mult, ALU.add)\
                      .then_inc(s["ylstm_ready"], 1)
                elif step == 11:
                    dve.wait_ge(s["ylstm_ready"], t + 1)
                    layer_stats(2, t, lambda n: y_lstm[:, n, :])
                elif step == 17:
                    dve.wait_ge(s["x3T_ps"], t + 1)
                    dve.wait_ge(s["x3hi_ready"], t + 1)
                    if not (isinstance(t, int) and t < 2):
                        dve.wait_ge(s["u_ps"], NJ * (t - 1))
                    nc.vector.tensor_tensor(x3T_lo[p][:], ps_b[:], x3T_hi[p][:].bitcast(F32), ALU.subtract)\
                      .then_inc(s["x3lo_ready"], 1)
                elif step == 19:
                    route(t, 0)
                elif step == 21:
                    route(t, 1)
                elif step == 23:
                    route(t, 2)

            def route(t, part):
                def after(n):
                    dve.wait_ge(s["route_step"], ROUTE * t + n)

                def step(ins):
                    ins.then_inc(s["route_step"], 1)

                each = lambda a: a[:].unsqueeze(2).to_broadcast([P, SUB, EXPERTS])
                if part == 0:
                    dve.wait_ge(s["logit_ps"], t + 1)
                    after(0)
                    step(nc.vector.tensor_copy(logits[:], ps_b[:, 0:SUB * EXPERTS]
                                               .rearrange("p (s e) -> p s e", s=SUB)))
                if part < 2:
                    k, left = part, (logits, logits2)[part]
                    after(7 * k + 1)
                    step(nc.vector.tensor_reduce(top[k][:], left[:], AX.X, ALU.max))
                    after(7 * k + 2)
                    step(nc.vector.tensor_tensor(is_top[k][:], left[:], each(top[k]), ALU.is_equal))
                    if k == 1:
                        dve.wait_ge(s["tgap_ready"], t)
                        nc.vector.tensor_tensor(gap[:], top[0][:], top[1][:], ALU.subtract).then_inc(s["gap_ready"], 1)
                    after(7 * k + 3)
                    step(nc.vector.tensor_tensor(rank[k][:], is_top[k][:], rev_index[:], ALU.mult))
                    after(7 * k + 4)
                    step(nc.vector.tensor_reduce(best[k][:], rank[k][:], AX.X, ALU.max))
                    after(7 * k + 5)
                    step(nc.vector.tensor_tensor(pick[k][:], rank[k][:], each(best[k]), ALU.is_equal))
                    if k == 0:
                        after(6)
                        step(nc.vector.scalar_tensor_tensor(logits2[:], pick[0][:], -3.0e38, logits[:],
                                                            ALU.mult, ALU.add))
                        step(nc.vector.tensor_copy(pick_sum[:], pick[0][:]))
                    else:
                        after(13)
                        step(nc.vector.tensor_tensor(pick_dif[:], pick_sum[:], pick[1][:], ALU.subtract))
                        after(14)
                        step(nc.vector.tensor_tensor(pick_sum[:], pick_sum[:], pick[1][:], ALU.add))
                    return
                dve.wait_ge(s["tgap_ready"], t + 1)
                after(15)
                step(nc.vector.tensor_tensor(dif_t[:], pick_dif[:], each(tanh_gap), ALU.mult))
                after(16)
                step(nc.vector.tensor_tensor(w2x[:], pick_sum[:], dif_t[:], ALU.add))
                after(17)
                step(nc.vector.tensor_scalar(w_tok[:], w2x[:], 0.5, None, ALU.mult))
                after(18)
                step(nc.vector.tensor_copy(w_tok_r[:], w_tok[:]))
                after(19)
                dve.wait_ge(s["wT_ps"], t)
                step(nc.vector.tensor_copy(w_parts[:, :, 0, :], w_tok_r[:].bitcast(F32)))
                step(nc.vector.tensor_tensor(w_parts[:, :, 1, :], w_tok[:], w_tok_r[:].bitcast(F32), ALU.subtract))

            def block_product(t, p, j):
                n = NJ * t + j
                m = units(j)
                early = isinstance(n, int) and n < 2
                dve.wait_ge(s["silu_ready"], n + 1)
                dve.wait_ge(s["u_ps"], n + 1)
                if not early:
                    dve.wait_ge(s["hi_ready"], n - 1)
                    dve.wait_ge(s["lo_ready"], n - 1)
                if j >= SHARED:
                    nc.vector.tensor_tensor(gu[j % 2][0:m], silu_g[j % 2][0:m], ps_u[j % 2][0:m], ALU.mult)\
                      .then_inc(s["gu_ready"], 1)
                    dve.wait_ge(s["gu_ready"], NJR * t + j - SHARED + 1)
                    dve.wait_ge(s["w_ps"], NJR * t + j - SHARED + 1)
                    nc.vector.tensor_tensor(hid[j % 2][0:m], gu[j % 2][0:m], ps_g[j % 3][0:m], ALU.mult)\
                      .then_inc(s["hid_ready"], 1)
                else:
                    nc.vector.tensor_tensor(hid[j % 2][0:m], silu_g[j % 2][0:m], ps_u[j % 2][0:m], ALU.mult)\
                      .then_inc(s["hid_ready"], 1)

            def finish(t, p):
                dve.wait_ge(s["y_ps"], t + 1)
                dve.wait_ge(nm_r[3], SUB * t)
                nc.vector.tensor_tensor(y_moe[:], ps_b[:].rearrange("p (s e) -> p s e", s=SUB), x3[p][:], ALU.add)\
                  .then_inc(s["ymoe_ready"], 1)
                dve.wait_ge(s["ymoe_ready"], t + 1)

            def finish_stats(t):
                layer_stats(3, t, lambda n: y_moe[:, n, :])

            def moe_tile(t, p, k, last=False):
                begun = not (isinstance(t, int) and t == 0)
                for j in range(NJ):
                    if not last:
                        recur(t + 2, p, k, 2 * j)
                        emit(t + 1, 1 - p, 2 * j)
                    if begun and j == 7:
                        finish(t - 1, 1 - p)
                    ahead = j + AHEAD
                    if ahead < NJ:
                        block_product(t, p, ahead)
                    elif not last:
                        block_product(t + 1, 1 - p, ahead - NJ)
                    if not last:
                        recur(t + 2, p, k, 2 * j + 1)
                    if begun and j == 7:
                        finish_stats(t - 1)
                    if not last:
                        emit(t + 1, 1 - p, 2 * j + 1)

            for step in range(2 * STEPS):
                if step < STEPS:
                    recur(0, 0, None, step)
                if step >= STEPS:
                    emit(0, 0, step - STEPS)
                if 0 <= step - LAG < STEPS:
                    recur(1, 1, 0, step - LAG, ps_a=ps_a2)
                for j in range(AHEAD):
                    if step == STEPS + first_block + 2 * j:
                        block_product(0, 0, j)
            moe_tile(0, 0, None)
            moe_tile(1, 1, 1)
            with dve.Fori(1, PAIRS - 1) as i:
                moe_tile(2 * i, 0, None)
                moe_tile(2 * i + 1, 1, i + 1)
            moe_tile(NT - 2, 0, None)
            moe_tile(NT - 1, 1, None, last=True)
            finish(NT - 1, 1)
            finish_stats(NT - 1)

        @block.tensor
        def _(pe):
            def turn(dst, src):
                return nc.tensor.transpose(dst, src, ident[0:src.shape[0], 0:src.shape[0]])

            def product3(o, w1, w0, x_hi, x_lo, first, last):
                nc.tensor.matmul(o, w1, x_hi, start=first, stop=False)
                nc.tensor.matmul(o, w1, x_lo, start=False, stop=False)
                return nc.tensor.matmul(o, w0, x_hi, start=False, stop=last)

            def weights_turned(b):
                pe.wait_ge(s[("wl_square", "wl_gates")[b]], (16 * 4, 16)[b])
                for n in range(4):
                    ins = turn(pb[(0, 6)[b]][:, P * n:P * n + P], w_nat[:, 4 * b + n, :])
                ins.then_inc(s["w_tr"], 1)

            def rows_spread():
                pe.wait_ge(s["w8_cast"], 1)
                turn(pb[7][:, 0:P], w_nat[:, 8, :]).then_inc(s["w_tr"], 1)
                pe.wait_ge(s["wl_rows"], 16 * 6)
                nc.tensor.matmul(pb[3][:], ones_row[:], rows[:, 0:4, :], start=True, stop=True)\
                  .then_inc(s["rows_bc_ps"], 1)
                nc.tensor.matmul(pb[7][:, P:2 * P], ones_row[:], rows[:, 4, :], start=True, stop=True)\
                  .then_inc(s["rows_bc_ps"], 1)

            def x_transposed(t, p):
                pe.wait_ge(s["x_loaded"], 16 * (t + 1))
                pe.wait_ge(s["ktok_ready"], t)
                for n in range(SUB):
                    ins = turn(ps_proj[:, P * n:P * n + P], x_cur[p][:, n, :])
                ins.then_inc(s["xT_ps"], 1)

            def project_q(t):
                pe.wait_ge(s["v_ready"], t + 1)
                pe.wait_ge(s["xTlo_ready"], t + 1)
                pe.wait_ge(s["wT_split"], 1)
                product3(ps_proj[:], wT_hi[:, 0, :], wT_lo[:, 0, :], xT_hi[:], xT_lo[:], True, True).then_inc(s["q_ps"], 1)

            def project_k(t):
                pe.wait_ge(s["q_ready"], t + 1)
                product3(ps_proj[:], wT_hi[:, 1, :], wT_lo[:, 1, :], xT_hi[:], xT_lo[:], True, True).then_inc(s["k_ps"], 1)

            def project_v(t):
                pe.wait_ge(s["xT_ready"], t + 1)
                pe.wait_ge(s["xThi_ready"], t + 1)
                for n in range(SUB):
                    ins = nc.tensor.matmul(ps_proj[:, P * n:P * n + P], xT[:, P * n:P * n + P], wT[:, 2, :],
                                           start=True, stop=True)
                ins.then_inc(s["v_ps"], 1)

            def k_transposed(t, p):
                pe.wait_ge(s["k_ready"], t + 1)
                for n in range(SUB):
                    ins = turn(ps_proj[:, P * n:P * n + P], kT[p][:, P * n:P * n + P])
                ins.then_inc(s["ktok_ps"], 1)

            def score(c, n, p, t, b):
                if n == 0 and b == 0:
                    pe.wait_ge(s["kheads_v"], 2 * (t + 1))
                    pe.wait_ge(s["kheads_p"], 2 * (t + 1))
                if b == 0:
                    pe.wait_ge(s["qquad_ready"], 4 * (c + 1))
                if not (isinstance(c, int) and c == 0):
                    pe.wait_ge(s["masked"], 4 * (c - 1) + b + 1)
                nc.tensor.matmul(ps_scores[b][:, 0:QUADS * (CHUNK - 32 * b)],
                                 k_heads[p][:, 4 * n + b, :, :].rearrange("p r j -> p (r j)"),
                                 q_quad[n % 2][:, :, 32 * b:CHUNK], start=True, stop=True).then_inc(s["score_ps"], 1)

            def key_values(c, n, p, t):
                if n == 0:
                    pe.wait_ge(s["ktok_ready"], t + 1)
                    pe.wait_ge(s["v_ready"], t + 1)
                pe.wait_ge(s["kv_own_ready"], c)
                nc.tensor.matmul(ps_kv, k_tok[p][:, n, :], v_tok[p][:, n, :, :].rearrange("p h d -> p (h d)"),
                                 start=True, stop=True).then_inc(s["kv_ps"], 1)

            def from_state(c, n, p):
                pe.wait_ge(s["state_ready"], c)
                pe.wait_ge(s["numT_ready"], c)
                for half in range(2):
                    nc.tensor.matmul(ps_numT[0:64 + QV, CHUNK * half:CHUNK * (half + 1)],
                                     state[:, n % 2, 2 * half:2 * half + 2, :].rearrange("p g d -> p (g d)")[:, 0:64 + QV],
                                     qT[p][:, CHUNK * n:CHUNK * (n + 1)], start=(half == 0), stop=False)

            def attend(c, n, p, t, b):
                if n == 0 and b == 0:
                    pe.wait_ge(s["vown_ready"], 16 * (t + 1))
                pe.wait_ge(s["masked"], 4 * c + b + 1)
                span = CHUNK - 32 * b
                for g in range(QUADS):
                    rows = slice(64 * (g % 2), 64 * (g % 2) + QV)
                    ins = nc.tensor.matmul(ps_numT[rows, CHUNK * (g // 2) + 32 * b:CHUNK * (g // 2 + 1)],
                                           v_own[p][:, n, QUADS * b + g, :, :].rearrange("p r d -> p (r d)"),
                                           scores[b][:, g * span:(g + 1) * span],
                                           start=False, stop=(b == 3 and g >= 2))
                ins.then_inc(s["attn_num_ps"], 1)

            def sums_turned(c):
                pe.wait_ge(s["numT_ready"], c + 1)
                pe.wait_ge(s["yattn_ready"], c)
                for half in range(2):
                    ins = turn(ps_num[:, CHUNK * half:CHUNK * half + 64 + QV], numT[:, CHUNK * half:CHUNK * (half + 1)])
                ins.then_inc(s["num_turned"], 1)

            def attn_transposed(c):
                pe.wait_ge(s["attn_ready"], c + 1)
                turn(ps_attnT, attn[:].rearrange("p h d -> p (h d)")).then_inc(s["attnT_ps"], 1)

            def out_project(c):
                pe.wait_ge(s["attnT_ready"], c + 1)
                nc.tensor.matmul(ps_wo, attnT[:], wT[:, 3, :], start=True, stop=True).then_inc(s["wo_ps"], 1)

            def attn_tile(t, p, last=False):
                for n in range(SUB):
                    c = SUB * t + n
                    begun = not (isinstance(c, int) and c == 0)
                    nt, np_, nn = (t, p, n + 1) if n < SUB - 1 else (t + 1, 1 - p, 0)
                    more = not (last and n == SUB - 1)
                    if not last and n == 0:
                        x_transposed(t + 1, 1 - p)
                    if begun:
                        sums_turned(c - 1)
                    from_state(c, n, p)
                    attend(c, n, p, t, 0)
                    attend(c, n, p, t, 1)
                    attend(c, n, p, t, 2)
                    attend(c, n, p, t, 3)
                    if more:
                        score(c + 1, nn, np_, nt, 0)
                    if begun:
                        attn_transposed(c - 1)
                    if more:
                        score(c + 1, nn, np_, nt, 1)
                    if not last and n == 3:
                        k_transposed(t + 1, 1 - p)
                    if not last and n == 1:
                        project_q(t + 1)
                    if not last and n == 2:
                        project_k(t + 1)
                    if begun:
                        out_project(c - 1)
                    if more:
                        score(c + 1, nn, np_, nt, 2)
                    if not last and n == 0:
                        project_v(t + 1)
                    if more:
                        key_values(c + 1, nn, np_, nt)
                    if more:
                        score(c + 1, nn, np_, nt, 3)

            pe.wait_ge(s["consts_ready"], 1)
            weights_turned(0)
            x_transposed(0, 0)
            pe.wait_ge(s["w_tr_copied"], 1)
            project_v(0)
            project_q(0)
            project_k(0)
            weights_turned(1)
            rows_spread()
            k_transposed(0, 0)
            pe.wait_ge(s["w_tr_copied"], 2)
            pe.wait_ge(s["w8T_ready"], 1)
            pe.wait_ge(s["rows_bc_ready"], 2)
            pe.wait_ge(s["state_zero"], 4)
            key_values(0, 0, 0, 0)
            for b in range(4):
                score(0, 0, 0, 0, b)
            attn_tile(0, 0)
            attn_tile(1, 1)
            with pe.Fori(1, PAIRS - 1) as i:
                attn_tile(2 * i, 0)
                attn_tile(2 * i + 1, 1)
            attn_tile(NT - 2, 0)
            attn_tile(NT - 1, 1, last=True)
            sums_turned(NC - 1)
            attn_transposed(NC - 1)
            out_project(NC - 1)

            pe.wait_ge(s["yattn_ready"], NC)
            pe.wait_ge(s["o_bias_ready"], 2)

            def recur(t, p, step, ps_a=ps_a):
                if step == 3:
                    pe.wait_ge(s["xq_ready"], t + 1)
                    if not (isinstance(t, int) and t < 2):
                        pe.wait_ge(s["to_ready"], t)
                    for n in range(SUB):
                        ins = turn(ps_a[:, P * n:P * n + P], xq[:, n, :])
                    ins.then_inc(s["xqT_ps"], 1)
                elif step == 5:
                    pe.wait_ge(s["xqT_ready"], t + 1)
                    for n in range(SUB):
                        ins = nc.tensor.matmul(ps_a[:, P * n:P * n + P], xqT[:, P * n:P * n + P], w8T[:],
                                               start=True, stop=True)
                    ins.then_inc(s["q8_ps"], 1)
                elif step == 13:
                    pe.wait_ge(nm_r[0], SUB * (t + 1))
                    pe.wait_ge(s["deq_done"], t + 1)
                    for n in range(SUB):
                        ins = turn(ps_a[:, P * n:P * n + P], x2[p][:, n, :])
                    ins.then_inc(s["x2T_ps"], 1)
                elif step in (20, 22, 24):
                    g, before, after = ((4, "x2T_ready", "f_ps"), (5, "tf_ready", "i_ps"),
                                        (7, "ti_ready", "z_ps"))[(step - 20) // 2]
                    pe.wait_ge(s["x2lo_ready"], t + 1)
                    pe.wait_ge(s[before], t + 1)
                    product3(ps_a[:], wT_hi[:, g, :], wT_lo[:, g, :], x2T_hi[:], x2T_lo[:], True, True)\
                        .then_inc(s[after], 1)
                elif step == 25:
                    pe.wait_ge(s["tz_ready"], t + 1)
                    nc.tensor.matmul(ps_a[:], ones_r[:], o_bias_hi[:].rearrange("o s e -> o (s e)"),
                                     start=True, stop=False)
                    nc.tensor.matmul(ps_a[:], ones_r[:], o_bias_lo[:].rearrange("o s e -> o (s e)"),
                                     start=False, stop=False)
                    for n in range(SUB):
                        ins = nc.tensor.matmul(ps_a[:, P * n:P * n + P], x2T[:, P * n:P * n + P], wT[:, 6, :],
                                               start=False, stop=(n == SUB - 1))
                    ins.then_inc(s["o_ps"], 1)

            def emit(t, p, step):
                if step == 1:
                    pe.wait_ge(s["cell_ready"], t + 1)
                    if not (isinstance(t, int) and t == 0):
                        pe.wait_ge(s["wT_ready"], t)
                    for n in range(SUB):
                        ins = turn(ps_b[:, P * n:P * n + P], cell2[p][:, P * n:P * n + P])
                    ins.then_inc(s["cellT_ps"], 1)
                elif step == 17:
                    pe.wait_ge(nm_r[2], SUB * (t + 1))
                    pe.wait_ge(nm_r[1], SUB * (t + 1))
                    if not (isinstance(t, int) and t < 2):
                        pe.wait_ge(s["ymoe_ready"], t - 1)
                    for n in range(SUB):
                        ins = turn(ps_b[:, P * n:P * n + P], x3[p][:, n, :])
                    ins.then_inc(s["x3T_ps"], 1)
                elif step == 19:
                    pe.wait_ge(s["x3hi_ready"], t + 1)
                    pe.wait_ge(s["x3lo_ready"], t + 1)
                    pe.wait_ge(s["router_ready"], 1)
                    for n in range(SUB):
                        o = ps_b[:, EXPERTS * n:EXPERTS * (n + 1)]
                        tok = slice(P * n, P * n + P)
                        nc.tensor.matmul(o, x3T_hi[p][:, tok], w_router_hi[:], start=True, stop=False)
                        nc.tensor.matmul(o, x3T_lo[p][:, tok], w_router_hi[:], start=False, stop=False)
                        ins = nc.tensor.matmul(o, x3T_hi[p][:, tok], w_router_lo[:], start=False, stop=True)
                    ins.then_inc(s["logit_ps"], 1)
                elif step == 26:
                    pe.wait_ge(s["route_step"], ROUTE * (t + 1))
                    for n in range(SUB):
                        ins = turn(ps_b[0:16, P * n:P * n + P], w_parts[:, n, :, :].rearrange("p a e -> p (a e)"))
                    ins.then_inc(s["wT_ps"], 1)

            def ff(at, m, k=P):
                return w_hi[0:k, at:at + m], w_lo[0:k, at:at + m]

            def up(t, p, j):
                n = NJ * t + j
                m = units(j)
                early = isinstance(n, int) and n < 2
                if j == 0:
                    pe.wait_ge(s["x3hi_ready"], t + 1)
                    pe.wait_ge(s["x3lo_ready"], t + 1)
                last_of_bank = n - 3 if j >= 3 else n - 2
                if not (isinstance(n, int) and n < 3):
                    pe.wait_ge(s["hid_ready"], last_of_bank + 1)
                product3(ps_g[j % 3][0:m], *ff(P * block_of(j), m), x3T_hi[p][:], x3T_lo[p][:], True, True)\
                    .then_inc(s["g_ps"], 1)
                if not early:
                    pe.wait_ge(s["hid_ready"], n - 1)
                product3(ps_u[j % 2][0:m], *ff(HALL + P * block_of(j), m), x3T_hi[p][:], x3T_lo[p][:], True, True)\
                    .then_inc(s["u_ps"], 1)

            def spread(t, p, j):
                if j >= SHARED:
                    if j == SHARED:
                        pe.wait_ge(s["wT_ready"], t + 1)
                    pe.wait_ge(s["silu_ready"], NJ * t + j + 1)
                    nc.tensor.matmul(ps_g[j % 3][:], sel16_r[:, P * block_of(j):P * block_of(j) + P], w_partsT[p][:],
                                     start=True, stop=True)\
                      .then_inc(s["w_ps"], 1)

            def down(t, p, j):
                n = NJ * t + j
                b = (NJ * p + j) % 4
                m = units(j)
                if j == 0:
                    pe.wait_ge(s["yT_ready"], t)
                pe.wait_ge(s["hi_ready"], n + 1)
                pe.wait_ge(s["lo_ready"], n + 1)
                product3(ps_y[:], *ff(2 * HALL + P * block_of(j), P, m), hid_hi[b][0:m], hid_lo[b][0:m],
                         j == 0, j == NJ - 1)\
                    .then_inc(s["down_ps"], 1)

            def finish(t):
                pe.wait_ge(s["yT_ready"], t + 1)
                pe.wait_ge(nm_r[1], SUB * (min(t + 3, NT) if isinstance(t, int) else t + 3))
                if isinstance(t, int) and t >= NT - 2:
                    pe.wait_ge(s["wT_ready"], NT)
                    pe.wait_ge(s["ymoe_ready"], t)
                for n in range(SUB):
                    ins = turn(ps_b[:, P * n:P * n + P], yT[:, P * n:P * n + P])
                ins.then_inc(s["y_ps"], 1)

            def moe_tile(t, p, last=False):
                for j in range(NJ):
                    if not last:
                        recur(t + 2, p, 2 * j)
                        emit(t + 1, 1 - p, 2 * j)
                    nt, np_, nj = (t, p, j + AHEAD) if j + AHEAD < NJ else (t + 1, 1 - p, j + AHEAD - NJ)
                    more = j + AHEAD < NJ or not last
                    if more:
                        up(nt, np_, nj)
                    down(t, p, j)
                    if more:
                        spread(nt, np_, nj)
                    if j == 4 and not (isinstance(t, int) and t == 0):
                        finish(t - 1)
                    if not last:
                        recur(t + 2, p, 2 * j + 1)
                        emit(t + 1, 1 - p, 2 * j + 1)

            pe.wait_ge(s["ff_split"], NT)
            pe.wait_ge(s["sel_r_ready"], 8)
            for step in range(2 * STEPS):
                if step < STEPS:
                    recur(0, 0, step)
                if step >= STEPS:
                    emit(0, 0, step - STEPS)
                if 0 <= step - LAG < STEPS:
                    recur(1, 1, step - LAG, ps_a=ps_a2)
                for j in range(AHEAD):
                    if step == STEPS + first_block + 2 * j:
                        if j == 0:
                            pe.wait_ge(s["to_ready"], 2)
                        up(0, 0, j)
                        spread(0, 0, j)
            moe_tile(0, 0)
            moe_tile(1, 1)
            with pe.Fori(1, PAIRS - 1) as i:
                moe_tile(2 * i, 0)
                moe_tile(2 * i + 1, 1)
            moe_tile(NT - 2, 0)
            moe_tile(NT - 1, 1, last=True)
            finish(NT - 1)


_INS = ['L0_attn_x', 'L0_attn_Wq', 'L0_attn_Wk', 'L0_attn_Wv', 'L0_attn_Wo', 'L0_attn_bo', 'L0_ffn_weight_int8',
        'L0_ffn_weight_scale', 'L0_ffn_bias', 'L1_attn_W', 'L1_attn_b', 'L1_attn_ln_w', 'L1_attn_ln_b', 'L1_ffn_Wg',
        'L1_ffn_W1', 'L1_ffn_W2', 'L1_ffn_W3', 'L1_ffn_Ws1', 'L1_ffn_Ws2', 'L1_ffn_Ws3']
_OUTS = [((2, 2048, 128), 'float32')]


def kernel(**inputs):
    import numpy as _np
    import concourse.bacc as _bacc
    from concourse import mybir as _mybir
    from concourse.bass_utils import run_bass_kernel_spmd as _run

    nc = _bacc.Bacc("TRN2", target_bir_lowering=False, num_devices=1)
    arrays, args = {}, []
    for name in _INS:
        a = _np.ascontiguousarray(inputs[name])
        if a.dtype.kind in "iu":
            a = a.astype(_np.int64)
        arrays[f"in_{name}_dram"] = a
        args.append(nc.dram_tensor(f"in_{name}_dram", a.shape, _mybir.dt.from_np(a.dtype), kind="ExternalInput").ap())
    for i, (shape, dtype) in enumerate(_OUTS):
        dt = _mybir.dt.from_np(_np.dtype(dtype))
        args.append(nc.dram_tensor(f"out_{i}_dram", shape, dt, kind="ExternalOutput").ap())
    build_program(nc, *args)
    r = _run(nc, [arrays], core_ids=[0])
    got = tuple(r.results[0][f"out_{i}_dram"] for i in range(len(_OUTS)))
    return got[0]
```
